# Optimizing a Trainium2 kernel written in Bass

```python
import numpy as np
import jax
import jax.numpy as jnp

def _softmax(x, axis=-1):
    return jax.nn.softmax(x, axis=axis)

def _gelu(x):
    return jax.nn.gelu(x, approximate=True)

def _silu(x):
    return jax.nn.silu(x)

def _sigmoid(x):
    return jax.nn.sigmoid(x)

def _layernorm(x, axis=-1, eps=1e-05):
    m = jnp.mean(x, axis=axis, keepdims=True)
    v = jnp.var(x, axis=axis, keepdims=True)
    return (x - m) / jnp.sqrt(v + eps)

def _scatter_add(tgt, idx, src, axis=0):
    return tgt.at[idx].add(src)

def _segment_sum(src, seg, n):
    return jax.ops.segment_sum(src, seg, n)
kernel_name = 'mk_seq_preln_d1_jaxref_r8_3629d3'

def setup_inputs(seed: int=0):
    np.random.seed(seed)
    _w = jnp.asarray

    def _L0_attn_setup():
        import jax, jax.numpy as jnp
        import numpy as np
        D_MODEL = 128
        D_STATE = 16
        D_CONV = 4
        EXPAND = 2
        D_INNER = D_MODEL * EXPAND

        def soft_clamp(x, lo, hi, sharp):
            c = (hi + lo) / 2.0
            r = (hi - lo) / 2.0
            return jnp.tanh((x - c) / (r + 1e-08) * sharp) / sharp * r + c
        key = jax.random.key(seed)
        ks = jax.random.split(key, 9)
        B, L = (2, 128)
        x = jax.random.normal(ks[0], (B, L, D_MODEL), jnp.float32)
        norm_w = jnp.ones((D_MODEL,), jnp.float32)
        W_in = jax.random.normal(ks[1], (2 * D_INNER, D_MODEL), jnp.float32) * 0.02
        conv_w = jax.random.normal(ks[2], (D_INNER, 1, D_CONV), jnp.float32) * 0.02
        conv_b = jnp.zeros((D_INNER,), jnp.float32)
        W_dt = jax.random.normal(ks[3], (D_INNER, D_INNER), jnp.float32) * 0.02
        b_dt = jnp.full((D_INNER,), -2.0, jnp.float32)
        W_B = jax.random.normal(ks[4], (D_STATE, D_INNER), jnp.float32) * 0.02
        W_C = jax.random.normal(ks[5], (D_STATE, D_INNER), jnp.float32) * 0.02
        A_log = jax.random.normal(ks[6], (D_INNER, D_STATE), jnp.float32) * 0.1
        D_param = jnp.full((D_INNER,), 0.1, jnp.float32)
        W_out = jax.random.normal(ks[7], (D_MODEL, D_INNER), jnp.float32) * 0.02
        residual_scale = jnp.asarray(0.3, jnp.float32)
        return dict(x=x, norm_w=norm_w, W_in=W_in, conv_w=conv_w, conv_b=conv_b, W_dt=W_dt, b_dt=b_dt, W_B=W_B, W_C=W_C, A_log=A_log, D_param=D_param, W_out=W_out, residual_scale=residual_scale)
    _L0_attn_in = _L0_attn_setup()

    def _L0_ffn_setup():
        import jax, jax.numpy as jnp
        import numpy as np
        key = jax.random.key(seed)
        k1, k2, k3, k4 = jax.random.split(key, 4)
        B, T, M = (4, 256, 128)
        E, F = (16, 512)
        x = jax.random.normal(k1, (B, T, M), dtype=jnp.float32) * 0.02
        Wg = jax.random.normal(k2, (M, E), dtype=jnp.float32) * 0.02
        w1 = jax.random.normal(k3, (E, M, F), dtype=jnp.float32) * 0.02
        w2 = jax.random.normal(k4, (E, F, M), dtype=jnp.float32) * 0.02
        return {'x': x, 'Wg': Wg, 'w1': w1, 'w2': w2}
    _L0_ffn_in = _L0_ffn_setup()
    _d = {'L0_attn_x': _L0_attn_in['x'], 'L0_attn_norm_w': _L0_attn_in['norm_w'], 'L0_attn_W_in': _L0_attn_in['W_in'], 'L0_attn_conv_w': _L0_attn_in['conv_w'], 'L0_attn_conv_b': _L0_attn_in['conv_b'], 'L0_attn_W_dt': _L0_attn_in['W_dt'], 'L0_attn_b_dt': _L0_attn_in['b_dt'], 'L0_attn_W_B': _L0_attn_in['W_B'], 'L0_attn_W_C': _L0_attn_in['W_C'], 'L0_attn_A_log': _L0_attn_in['A_log'], 'L0_attn_D_param': _L0_attn_in['D_param'], 'L0_attn_W_out': _L0_attn_in['W_out'], 'L0_attn_residual_scale': _L0_attn_in['residual_scale'], 'L0_ffn_Wg': _L0_ffn_in['Wg'], 'L0_ffn_w1': _L0_ffn_in['w1'], 'L0_ffn_w2': _L0_ffn_in['w2']}
    _x0 = _d['L0_attn_x']
    _d['L0_attn_x'] = jax.random.normal(jax.random.fold_in(jax.random.key(seed), 1), (8, 512, 128), dtype=_x0.dtype)
    del _x0
    return _d

def reference(L0_attn_x, L0_attn_norm_w, L0_attn_W_in, L0_attn_conv_w, L0_attn_conv_b, L0_attn_W_dt, L0_attn_b_dt, L0_attn_W_B, L0_attn_W_C, L0_attn_A_log, L0_attn_D_param, L0_attn_W_out, L0_attn_residual_scale, L0_ffn_Wg, L0_ffn_w1, L0_ffn_w2):

    def _L0_attn_ref(x, norm_w, W_in, conv_w, conv_b, W_dt, b_dt, W_B, W_C, A_log, D_param, W_out, residual_scale):
        import jax, jax.numpy as jnp
        import numpy as np
        D_MODEL = 128
        D_STATE = 16
        D_CONV = 4
        EXPAND = 2
        D_INNER = D_MODEL * EXPAND

        def soft_clamp(x, lo, hi, sharp):
            c = (hi + lo) / 2.0
            r = (hi - lo) / 2.0
            return jnp.tanh((x - c) / (r + 1e-08) * sharp) / sharp * r + c
        B, L, _ = x.shape
        var = jnp.mean(x * x, axis=-1, keepdims=True)
        xn = x * jax.lax.rsqrt(var + 1e-06) * norm_w
        proj = xn @ W_in.T
        x_branch, gate = (proj[..., :D_INNER], proj[..., D_INNER:])
        xc = jax.lax.conv_general_dilated(jnp.swapaxes(x_branch, 1, 2), conv_w, (1,), [(D_CONV - 1, 0)], dimension_numbers=('NCH', 'OIH', 'NCH'), feature_group_count=D_INNER)
        xc = xc + conv_b[None, :, None]
        xc = jnp.swapaxes(xc, 1, 2)
        xc = xc * jax.nn.sigmoid(xc)
        dt = soft_clamp(jax.nn.softplus(xc @ W_dt.T + b_dt), 0.001, 0.1, 0.5)
        Bp = xc @ W_B.T
        Cp = xc @ W_C.T
        A = -jnp.exp(soft_clamp(A_log, -5.0, 5.0, 0.5))
        dt_A = soft_clamp(dt[..., None] * A[None, None], -8.0, 8.0, 0.5)
        dA = jnp.exp(dt_A)
        dB = dt[..., None] * Bp[:, :, None, :]
        h0 = jnp.zeros((B, D_INNER, D_STATE), jnp.float32)

        def step(h, inp):
            dA_t, dB_t, x_t, C_t, t = inp
            h = h * dA_t + dB_t * x_t[:, :, None]
            nrm = jnp.sqrt(jnp.sum(h * h, axis=(1, 2), keepdims=True))
            fac = jnp.minimum(20.0 / (nrm + 1e-08), 1.0)
            h = jnp.where(t % 10 == 0, h * fac, h)
            y = jnp.einsum('bdn,bn->bd', h, C_t) + D_param * x_t
            return (h, y)
        xs = (jnp.swapaxes(dA, 0, 1), jnp.swapaxes(dB, 0, 1), jnp.swapaxes(xc, 0, 1), jnp.swapaxes(Cp, 0, 1), jnp.arange(L))
        _, ys = jax.lax.scan(step, h0, xs)
        x_ssm = jnp.swapaxes(ys, 0, 1)
        x_out = x_ssm * (gate * jax.nn.sigmoid(gate)) @ W_out.T
        scale = jax.nn.sigmoid(residual_scale) * 0.5
        return x + scale * x_out

    def _L0_ffn_ref(x, Wg, w1, w2):
        import jax, jax.numpy as jnp
        import numpy as np
        d = x.shape[-1]
        xr = x.reshape(-1, d)
        S = xr.shape[0]
        E = Wg.shape[1]
        C = (S + E - 1) // E
        gate = jax.nn.softmax(xr @ Wg, axis=-1)
        idx = jnp.argmax(gate, axis=1)
        gates_s = jnp.take_along_axis(gate, idx[:, None], axis=1)[:, 0]
        onehot = jax.nn.one_hot(idx, E, dtype=jnp.int32)
        loc = jnp.sum((jnp.cumsum(onehot, axis=0) - 1) * onehot, axis=1)
        valid = loc < C
        loc_pad = jnp.minimum(loc, C)
        dispatched = jnp.zeros((E, C + 1, d), dtype=x.dtype).at[idx, loc_pad].set(xr)
        dispatched = dispatched[:, :C]
        h = jax.nn.relu(jnp.einsum('ecm,emf->ecf', dispatched, w1))
        expert_out = jnp.einsum('ecf,efm->ecm', h, w2)
        gathered = expert_out[idx, jnp.minimum(loc, C - 1)]
        combined = gathered * (gates_s * valid.astype(x.dtype))[:, None]
        return combined.reshape(x.shape)
    x = L0_attn_x
    x = x + _L0_attn_ref(_layernorm(x, axis=-1), L0_attn_norm_w, L0_attn_W_in, L0_attn_conv_w, L0_attn_conv_b, L0_attn_W_dt, L0_attn_b_dt, L0_attn_W_B, L0_attn_W_C, L0_attn_A_log, L0_attn_D_param, L0_attn_W_out, L0_attn_residual_scale)
    x = x + _L0_ffn_ref(_layernorm(x, axis=-1), L0_ffn_Wg, L0_ffn_w1, L0_ffn_w2)
    return x

_drawn_inputs = setup_inputs


def setup_inputs(seed=0):
    import zlib

    import numpy as np

    out = dict(_drawn_inputs(seed))
    spreads = {'L0_attn_norm_w': (1.0, 0.6),
     'L0_attn_conv_b': (0.0, 0.8),
     'L0_attn_b_dt': (-2.0, 0.6),
     'L0_attn_D_param': (0.10000000149011612, 0.6)}
    factors = {'L0_attn_W_in': 8.0,
     'L0_attn_conv_w': 8.0,
     'L0_attn_W_dt': 8.0,
     'L0_attn_W_B': 8.0,
     'L0_attn_W_C': 8.0,
     'L0_attn_A_log': 8.0,
     'L0_attn_W_out': 8.0,
     'L0_ffn_Wg': 8.0,
     'L0_ffn_w1': 8.0,
     'L0_ffn_w2': 8.0}
    for name, (base, spread) in spreads.items():
        noise = np.random.default_rng([zlib.crc32(name.encode()), seed]).standard_normal(out[name].shape)
        drawn = base * np.exp(spread * noise) if base else spread * noise
        out[name] = jnp.asarray(drawn.astype(out[name].dtype))
    for name, factor in factors.items():
        out[name] = (out[name] * factor).astype(out[name].dtype)
    return out
```

```python
from contextlib import ExitStack

import concourse.bass as bass
from concourse import mybir

ALU = mybir.AluOpType
ACT = mybir.ActivationFunctionType
AX_X = mybir.AxisListType.X
F32 = mybir.dt.float32
BF16 = mybir.dt.bfloat16
I32 = mybir.dt.int32

P = 128
SEG = 10
SLOT = SEG + 1
SPW = 6
WIN = SPW * SEG
COLS = WIN + 1
TAPS = 4
GRID = WIN + TAPS
RING = 3
CAP_MISS = 65536.0
MAX_NORM = 20.0


def at_least(eng, sem, n):
    if isinstance(n, int) and n <= 0:
        return
    eng.wait_ge(sem, n)


def mamba_moe(nc, x, norm_w, W_in, conv_w, conv_b, W_dt, b_dt, W_B, W_C, A_log, D_param, W_out,
              residual_scale, Wg, w1, w2, out):
    B, T, DM = x.shape
    DI, NST = A_log.shape
    E, _, F = w1.shape
    H = DI // P
    RH = NST * B
    ROWS = H * RH
    NSEG = (T + SEG - 1) // SEG
    NWIN = (NSEG + SPW - 1) // SPW
    TILES = B * GRID // P
    TOK = B * T
    NT = TOK // P
    CAP = (TOK + E - 1) // E
    FC = F // P
    CT = CAP // P
    assert DM == P and TILES * P == 512 and CAP == 256 and NWIN == 9 and B * SEG * H == 160
    BS = B * SEG
    NCH = [(0, 6), (6, 12), (12, 16)]

    with ExitStack() as ctx:
        def sb(name, shape, dt=F32):
            return ctx.enter_context(nc.sbuf_tensor(name, shape, dt))

        def sem(name):
            return ctx.enter_context(nc.semaphore(name))

        def dram(name, shape):
            return nc.dram_tensor(name, shape, F32, kind="Internal").ap()

        xpad = dram("xpad", (TOK + GRID, DM))
        b_d = dram("b_d", (NWIN, SPW, NST, BS))
        b0_d = dram("b0_d", (NST, B))
        xx_d = dram("xx_d", (NWIN, P, TILES * DM))
        x1_d = dram("x1_d", (TOK, DM))
        h2_d = dram("h2_d", (TOK, DM))
        lg_d = dram("lg_d", (TOK, E))
        disp_d = dram("disp_d", (TOK, DM))
        eo_d = dram("eo_d", (TOK, DM))

        ident = sb("ident", [P, P])
        norm_w8 = sb("norm_w8", [P, P])
        zeros = sb("zeros", [P, P])
        sel = sb("sel", [P, NST, P], BF16)
        wT = sb("wT", [P, 18, P])
        conv_c = sb("conv_c", [P, H, TAPS])
        cbh = sb("cbh", [P, H])
        bdt = sb("bdt", [P, H])
        dpar = sb("dpar", [P, H])
        asc = sb("asc", [P, H, NST])
        nw = sb("nw", [P, 1])
        rs = sb("rs", [P, 1])
        wg_s = sb("wg_s", [P, E])
        half_e = sb("half_e", [P, B])
        eps_rms = sb("eps_rms", [P, TILES])
        ones4 = sb("ones4", [P, TILES])
        guard8 = sb("guard8", [P, B])
        neghalf_e = sb("neghalf_e", [P, TILES])
        spb = sb("spb", [P, 1])
        pad = sb("pad", [P, 1])
        tri = sb("tri", [P, P])
        iota_i = sb("iota_i", [P, E], I32)
        iom = sb("iom", [P, E])
        tot = sb("tot", [P, E])
        totp = sb("totp", [P, E])

        z = sb("z", [P, H * NST * B * WIN])
        dA = sb("dA", [P, RING, ROWS * SLOT])
        h = sb("h", [P, RING, ROWS * SLOT])
        bb = sb("bb", [P, RING, NST * BS])
        sqb = sb("sqb", [P, ROWS])
        s8 = sb("s8", [P, B])
        nrm8 = sb("nrm8", [P, B])
        nrt8 = sb("nrt8", [P, B])
        fac8 = sb("fac8", [P, B])

        xt = sb("xt", [P, TILES, DM])
        xx = sb("xx", [P, TILES, DM])
        xxr = sb("xxr", [P, TILES, DM])
        xnT = sb("xnT", [P, B, GRID])
        bst = sb("bst", [P, TILES, 6])
        mv = sb("mv", [P, TILES, 2])
        ve = sb("ve", [P, TILES])
        lnp = sb("lnp", [P, 7, TILES])
        bst2 = sb("bst2", [P, TILES, 6])
        mv2 = sb("mv2", [P, TILES, 2])
        ve2 = sb("ve2", [P, TILES])
        rstd2 = sb("rstd2", [P, TILES])
        thx = sb("thx", [P, H, B * COLS])
        xc = sb("xc", [P, H, B * COLS])
        sgn = sb("sgn", [P, H, B * COLS])
        sgc = sb("sgc", [P, H, B * COLS])
        dtb = sb("dtb", [P, H, B * COLS])
        u = sb("u", [P, H, B * COLS])
        dxc = sb("dxc", [P, H, B * COLS])
        bcraw = sb("bcraw", [P, B * COLS])
        bsb = sb("bsb", [P, SPW, B, SEG])
        b0s = sb("b0s", [P, B])
        b0b = sb("b0b", [P, NST, B])
        cs = sb("cs", [P, B * COLS], BF16)
        yg = sb("yg", [P, H, B, GRID])
        h2b = sb("h2b", [P, TILES, DM])
        h2T = sb("h2T", [P, TILES, P])
        lgb = sb("lgb", [P, TILES, E])

        ps = ctx.enter_context(nc.psum_tensor("ps", [P, 8, 512], F32))
        YB, NB, P0, P1, P2 = 3, 4, 5, 6, 7
        B_XH, B_G, B_DT = (P0, P2), (P0, P2), (P1, P0)
        B_XT, B_BC, B_H2, B_OUT, B_LG = P2, P2, P0, P1, P1

        def cols(t, hf):
            return t[:, hf, :].rearrange("p (b c) -> p b c", b=B)

        def rows(t, r):
            return t[:, r, :].rearrange("p (r c) -> p r c", c=SLOT)

        def bank(k):
            return ps[:, k, :]

        def bankc(k):
            return ps[:, k, 0:B * COLS]

        zrow = z[:].rearrange("p (r b t) -> p r b t", r=H * NST, b=B)
        zall = z[:].rearrange("p (r t) -> p r t", t=WIN)

        nat = z[:, 0:18 * P].rearrange("p (k c) -> p k c", c=P)
        win_n = z[:, 18 * P:22 * P].rearrange("p (k c) -> p k c", c=P)

        ld_w = sem("ld_w"); ld_bc = sem("ld_bc"); ld_x = sem("ld_x"); ld_xx = sem("ld_xx")
        ld_bb = [sem(f"ld_bb{r}") for r in range(RING)]; ld_b0 = sem("ld_b0")
        st_pad = sem("st_pad"); st_b = sem("st_b"); st_b0 = sem("st_b0"); st_xx = sem("st_xx")
        st_x1 = sem("st_x1"); st_lg = sem("st_lg"); st_zero = sem("st_zero")
        const_pool = sem("const_pool"); const_dve = sem("const_dve"); asc_s = sem("asc_s")
        taps_ready = sem("taps_ready"); wtr_done = sem("wtr_done"); w_ready = sem("w_ready")
        rs_s = sem("rs_s"); fin_s = sem("fin_s"); iom_s = sem("iom_s")
        ln_stat = sem("ln_stat"); ln_small = sem("ln_small"); xn_ready = sem("xn_ready")
        xT_done = sem("xT_done"); xnT_ready = sem("xnT_ready")
        xh_done = sem("xh_done"); g_done = sem("g_done"); x_read = sem("x_read"); tg_done = sem("tg_done")
        xc_ready = sem("xc_ready"); sg_made = sem("sg_made")
        dt_done = sem("dt_done"); bc_done = sem("bc_done"); dt_read = sem("dt_read")
        ln_step = sem("ln_step"); sp_ready = sem("sp_ready"); dt_step = sem("dt_step")
        bc_read = sem("bc_read"); bsb_ready = sem("bsb_ready"); b0_ready = sem("b0_ready")
        cs_step = sem("cs_step"); u_done = sem("u_done")
        sg_ready = sem("sg_ready"); dxc_ready = sem("dxc_ready")
        tanh_done = sem("tanh_done")
        exp_done = sem("exp_done"); bm_done = sem("bm_done"); scan_done = sem("scan_done")
        sq_done = sem("sq_done"); nrm_done = sem("nrm_done"); red_done = sem("red_done")
        pow_done = sem("pow_done"); nrt_done = sem("nrt_done"); rec_done = sem("rec_done")
        h0_ready = sem("h0_ready"); cb_done = sem("cb_done"); cm_done = sem("cm_done")
        y_done = sem("y_done"); yg_done = sem("yg_done"); pre_done = sem("pre_done")
        op_done = sem("op_done"); x1_done = sem("x1_done"); st2_done = sem("st2_done")
        rstd2_done = sem("rstd2_done"); h2_ready = sem("h2_ready"); h2T_done = sem("h2T_done")
        h2T_ready = sem("h2T_ready"); lg_done = sem("lg_done"); lg_ready = sem("lg_ready")
        stat_step = sem("stat_step"); stat2_step = sem("stat2_step")

        N_WLOAD = 11
        LAST_SEGS = NSEG - SPW * (NWIN - 1)
        LS = NSEG - 1

        dAf = dA[:].rearrange("p r c -> p (r c)")
        hf_ = h[:].rearrange("p r c -> p (r c)")
        h2a = z[:, 0:NT * DM].rearrange("p (k m) -> p k m", m=DM)
        x1a = z[:, NT * DM:2 * NT * DM].rearrange("p (k m) -> p k m", m=DM)
        gat = z[:, 2 * NT * DM:3 * NT * DM].rearrange("p (k m) -> p k m", m=DM)

        def slab(k):
            return dAf[:, k * NT * E:(k + 1) * NT * E]

        lga, em, ex, eq, cand, ohe, cum, keep = (slab(k) for k in range(8))
        eos = dAf[:, 8 * NT * E:8 * NT * E + 2 * CT * DM].rearrange("p (q t m) -> p q t m", q=2, t=CT)
        small = dAf[:, 9 * NT * E + 2 * CT * DM - NT * E:][:, 0:14 * NT].rearrange("p (k c) -> p k c", c=NT)
        mx, im, slot0, loc, val, miss, si, lc, se, rse, gw = (small[:, k, :] for k in range(11))
        sidx = sb("sidx", [P, NT], I32)
        gidx = sb("gidx", [P, NT], I32)
        WR = 4
        w1s = hf_[:, 0:WR * F].rearrange("p (k f) -> p k f", k=WR)
        w2s = hf_[:, WR * F:2 * WR * F].rearrange("p (k c m) -> p k c m", k=WR, m=DM)
        xs = hf_[:, 2 * WR * F:2 * WR * F + WR * CAP].rearrange("p (k t m) -> p k t m", k=WR, m=DM)
        o0 = 2 * WR * F + WR * CAP
        xTs = hf_[:, o0:o0 + 2 * CAP].rearrange("p (k c) -> p k c", k=2)
        hTs = hf_[:, o0 + 2 * CAP:o0 + 2 * CAP + 2 * FC * CAP].rearrange("p (k c s) -> p k c s", k=2, s=CAP)

        ld_lg = sem("ld_lg"); ld_h2 = sem("ld_h2"); ld_x1 = sem("ld_x1")
        ld_we = [sem(f"ld_we{k}") for k in range(WR)]
        ld_xe = [sem(f"ld_xe{k}") for k in range(WR)]
        rt = sem("rt"); ex_done = sem("ex_done"); pre_mm = sem("pre_mm")
        idx_ready = sem("idx_ready"); scattered = sem("scattered")
        xeT_done = sem("xeT_done"); xeT_ready = sem("xeT_ready"); up_done = sem("up_done")
        relu_a = sem("relu_a"); relu_b = sem("relu_b"); down_done = sem("down_done")
        eo_ready = sem("eo_ready"); st_eo = [sem(f"st_eo{q}") for q in range(2)]
        gathered = [sem(f"gathered{k}") for k in range(4)]
        fin_done = sem("fin_done"); st_out = sem("st_out")
        GT = NT // 4

        def sp_tail(sp):
            sp.wait_ge(exp_done, NSEG)
            sp.wait_ge(scan_done, NSEG)
            sp.dma_start(lga, lg_d.rearrange("(p k) e -> p (k e)", p=P)).then_inc(ld_lg, 16)
            sp.dma_start(h2a, h2_d.rearrange("(p k) m -> p k m", p=P)).then_inc(ld_h2, 16)
            sp.wait_ge(y_done, NSEG)

            def weights(e, k):
                sp.dma_start(w1s[:, k, :], w1[bass.ds(e, 1)].rearrange("o m f -> (o m) f")).then_inc(ld_we[k], 16)
                sp.dma_start(w2s[:, k], w2[bass.ds(e, 1)].rearrange("o (c p) m -> (o p) c m", p=P)).then_inc(ld_we[k], 16)

            def tokens(e, k):
                sp.dma_start(xs[:, k], disp_d[bass.ds(e * CAP, CAP), :].rearrange("(t p) m -> p t m", p=P)).then_inc(ld_xe[k], 16)

            for k in range(WR):
                weights(k, k)
            sp.dma_start(x1a, x1_d.rearrange("(p k) m -> p k m", p=P)).then_inc(ld_x1, 16)
            sp.wait_ge(scattered, 16 * NT)
            for k in range(WR):
                tokens(k, k)

            def expert(e, k, more):
                if more:
                    sp.wait_ge(down_done, e + 1)
                    weights(e + WR, k)
                    tokens(e + WR, k)
                sp.wait_ge(eo_ready, e + 1)
                sp.dma_start(eo_d[bass.ds(e * CAP, CAP), :].rearrange("(t p) m -> p t m", p=P),
                             eos[:, k % 2]).then_inc(st_eo[k % 2], 16)

            with sp.Fori(0, E // WR - 1) as g:
                for k in range(WR):
                    expert(WR * g + k, k, True)
            for k in range(WR):
                expert(E - WR + k, k, False)
            outf = out.rearrange("b t d -> (b t) d").rearrange("(p k) m -> p k m", p=P)
            for g in range(4):
                sp.wait_ge(fin_done, g + 1)
                sp.dma_start(outf[:, g * GT:(g + 1) * GT, :], gat[:, g * GT:(g + 1) * GT, :]).then_inc(st_out, 16)
            sp.wait_ge(st_out, 64)

        def pool_tail(pool):
            pool.wait_ge(idx_ready, 2)
            pool.wait_ge(ld_h2, 16)
            pool.wait_ge(st_zero, 16)
            for k in range(NT):
                pool.indirect_dma_start(disp_d, bass.IndirectOffsetOnAxis(ap=sidx[:, k:k + 1], axis=0), h2a[:, k, :],
                                        None, bounds_check=TOK - 1, oob_is_err=False).then_inc(scattered, 16)
            for q in range(2):
                pool.wait_ge(st_eo[q], 8 * E)
            for k in range(NT):
                pool.indirect_dma_start(gat[:, k, :], None, eo_d, bass.IndirectOffsetOnAxis(ap=gidx[:, k:k + 1], axis=0),
                                        bounds_check=TOK - 1, oob_is_err=False).then_inc(gathered[k // GT], 16)

        def act_tail(act):
            act.wait_ge(rt, 2)
            act.activation(ex, em, ACT.Exp).then_inc(ex_done, 1)

            def turn_in(e, q):
                act.wait_ge(xeT_done, e + 1)
                at_least(act, up_done, 2 * (e - 1))
                act.copy(xTs[:, q, :], ps[:, q, 0:CAP]).then_inc(xeT_ready, 1)

            def relu(e, q):
                act.wait_ge(up_done, 2 * e + 1)
                at_least(act, down_done, e - 1)
                act.activation(hTs[:, q, 0:2].rearrange("p c s -> p (c s)"), ps[:, 2 + 2 * q, :],
                               ACT.Relu).then_inc(relu_a, 1)

            turn_in(0, 0)
            turn_in(1, 1)
            relu(0, 0)
            turn_in(2, 0)
            relu(1, 1)
            with act.Fori(1, E // 2 - 1) as g:
                turn_in(2 * g + 1, 1)
                relu(2 * g, 0)
                turn_in(2 * g + 2, 0)
                relu(2 * g + 1, 1)
            turn_in(E - 1, 1)
            relu(E - 2, 0)
            relu(E - 1, 1)

        def dve_tail(dve):
            v3 = lambda t: t.rearrange("p (k e) -> p k e", e=E)
            e3 = lambda t: t.rearrange("p (e k) -> p e k", k=NT)
            n = [0]

            def step(ins):
                n[0] += 1
                ins.then_inc(rt, 1)
                dve.wait_ge(rt, n[0])

            dve.wait_ge(ld_lg, 16)
            step(dve.tensor_reduce(mx, v3(lga), AX_X, ALU.max))
            step(dve.tensor_tensor(v3(em), v3(lga), mx.unsqueeze(2).to_broadcast([P, NT, E]), ALU.subtract))
            step(dve.tensor_scalar(eq, em, 0.0, None, ALU.is_equal))
            step(dve.tensor_tensor(v3(cand), v3(eq), iom[:].unsqueeze(1).to_broadcast([P, NT, E]), ALU.mult))
            step(dve.tensor_reduce(im, v3(cand), AX_X, ALU.min))
            step(dve.tensor_tensor(e3(ohe), iom[:].unsqueeze(2).to_broadcast([P, E, NT]),
                                   im.unsqueeze(1).to_broadcast([P, E, NT]), ALU.is_equal))
            step(dve.memset(keep, 1.0))
            step(dve.memset(e3(keep)[:, :, 0], 0.0))
            step(dve.tensor_tensor_scan(cum, keep, ohe, 0.0, ALU.mult, ALU.add))
            step(dve.tensor_copy(tot[:], e3(cum)[:, :, NT - 1]))
            dve.wait_ge(pre_mm, 1)
            step(dve.tensor_scalar(totp[:], ps[:, 0, 0:E], -1.0, None, ALU.add))
            step(dve.tensor_tensor(e3(cand), e3(cum), totp[:].unsqueeze(2).to_broadcast([P, E, NT]), ALU.add))
            step(dve.tensor_tensor(cum, cand, ohe, ALU.mult))
            step(dve.tensor_reduce(loc, cum.rearrange("p (e k) -> p k e", k=NT), AX_X, ALU.add))
            step(dve.tensor_scalar(slot0, im, float(CAP), float(E * CAP), ALU.mult, ALU.add))
            step(dve.tensor_scalar(val, loc, float(CAP), None, ALU.is_lt))
            step(dve.tensor_scalar(miss, val, -CAP_MISS, CAP_MISS, ALU.mult, ALU.add))
            step(dve.tensor_tensor(si, slot0, loc, ALU.add))
            step(dve.tensor_tensor(si, si, miss, ALU.add))
            step(dve.tensor_copy(sidx[:], si))
            dve.tensor_scalar(lc, loc, float(CAP - 1), None, ALU.min).then_inc(idx_ready, 1)
            dve.wait_ge(idx_ready, 1)
            dve.tensor_tensor(lc, lc, slot0, ALU.add).then_inc(fin_s, 1)
            dve.wait_ge(fin_s, 1)
            dve.tensor_copy(gidx[:], lc).then_inc(idx_ready, 1)
            dve.wait_ge(ex_done, 1)
            step(dve.tensor_reduce(se, v3(ex), AX_X, ALU.add))
            step(dve.reciprocal(rse, se))
            step(dve.tensor_tensor(gw, rse, val, ALU.mult))

            def relu(e, q):
                dve.wait_ge(up_done, 2 * e + 2)
                at_least(dve, down_done, e - 1)
                dve.tensor_scalar(hTs[:, q, 2:4].rearrange("p c s -> p (c s)"), ps[:, 3 + 2 * q, :], 0.0, None,
                                  ALU.max).then_inc(relu_b, 1)

            def take_out(e, q, before):
                dve.wait_ge(down_done, e + 1)
                at_least(dve, st_eo[q], 16 * before)
                dve.tensor_copy(eos[:, q].rearrange("p t m -> p (t m)"), ps[:, 6 + q, 0:CAP]).then_inc(eo_ready, 1)

            relu(0, 0)
            relu(1, 1)
            take_out(0, 0, 0)
            relu(2, 0)
            take_out(1, 1, 0)
            with dve.Fori(1, E // 2 - 1) as g:
                relu(2 * g + 1, 1)
                take_out(2 * g, 0, g)
                relu(2 * g + 2, 0)
                take_out(2 * g + 1, 1, g)
            relu(E - 1, 1)
            take_out(E - 2, 0, E // 2 - 1)
            take_out(E - 1, 1, E // 2 - 1)
            dve.wait_ge(ld_x1, 16)
            for g in range(4):
                dve.wait_ge(gathered[g], 16 * GT)
                for k in range(g * GT, (g + 1) * GT):
                    ins = dve.scalar_tensor_tensor(out=gat[:, k, :], in0=gat[:, k, :], scalar=gw[:, k:k + 1],
                                                   in1=x1a[:, k, :], op0=ALU.mult, op1=ALU.add)
                ins.then_inc(fin_done, 1)

        def pe_tail(pe):
            pe.wait_ge(rt, 10)
            pe.matmul(ps[:, 0, 0:E], tri[:], tot[:], start=True, stop=True).then_inc(pre_mm, 1)

            def turn(e, k):
                pe.wait_ge(ld_xe[k], 16 * (e // WR + 1) if isinstance(e, int) else e[1])
                ee = e if isinstance(e, int) else e[0]
                at_least(pe, xeT_ready, ee - 1)
                for t in range(CT):
                    ins = pe.transpose(ps[:, k % 2, t * P:(t + 1) * P], xs[:, k, t, :], ident[:])
                ins.then_inc(xeT_done, 1)

            def up(e, k):
                pe.wait_ge(ld_we[k], 32 * (e // WR + 1) if isinstance(e, int) else 2 * e[1])
                ee = e if isinstance(e, int) else e[0]
                pe.wait_ge(xeT_ready, ee + 1)
                q = k % 2
                for c in range(FC):
                    if c == 0:
                        at_least(pe, relu_a, ee - 1)
                    if c == 2:
                        at_least(pe, relu_b, ee - 1)
                    ins = pe.matmul(ps[:, 2 + 2 * q + c // 2, (c % 2) * CAP:(c % 2 + 1) * CAP],
                                    w1s[:, k, c * P:(c + 1) * P], xTs[:, q, :], start=True, stop=True)
                    if c % 2:
                        ins.then_inc(up_done, 1)

            def down(e, k):
                q = k % 2
                pe.wait_ge(relu_a, e + 1)
                pe.wait_ge(relu_b, e + 1)
                at_least(pe, eo_ready, e - 1)
                for t in range(CT):
                    for c in range(FC):
                        ins = pe.matmul(ps[:, 6 + q, t * P:(t + 1) * P], hTs[:, q, c, t * P:(t + 1) * P],
                                        w2s[:, k, c, :], start=(c == 0), stop=(c == FC - 1))
                ins.then_inc(down_done, 1)

            pe.wait_ge(rt, 11)
            turn(0, 0)
            turn(1, 1)
            up(0, 0)
            turn(2, 2)
            up(1, 1)
            down(0, 0)
            turn(3, 3)
            up(2, 2)
            down(1, 1)
            with pe.Fori(0, E // WR - 1) as g:
                for k in range(3, WR + 3):
                    turn((WR * g + k + 1, 16 * (g + 1 + (k + 1) // WR)), (k + 1) % WR)
                    up((WR * g + k, 16 * (g + 1 + k // WR)), k % WR)
                    down(WR * g + k - 1, (k - 1) % WR)
            up(E - 1, WR - 1)
            down(E - 2, WR - 2)
            down(E - 1, WR - 1)

        block = ctx.enter_context(nc.Block())

        @block.sync
        def _(sp):
            sp.dma_start(win_n, W_in.rearrange("(k p) c -> p k c", p=P)).then_inc(ld_w, 16)
            sp.dma_start(conv_c[:], conv_w.rearrange("(k p) o t -> p k (o t)", p=P)).then_inc(ld_w, 16)
            xq = x.rearrange("(i q) t m -> q t i m", q=2)

            def load_x_direct(t0, n, j0):
                for q in range(2):
                    sp.dma_start(xt[q * GRID + j0:q * GRID + j0 + n, :, :], xq[q, t0:t0 + n]).then_inc(ld_x, 16)

            sp.wait_ge(const_dve, 1)
            load_x_direct(0, GRID - 3, 3)
            sp.dma_start(z[:, 10 * P:14 * P].rearrange("p (j c) -> p j c", j=H),
                         W_dt.rearrange("(j p) c -> p j c", p=P)).then_inc(ld_w, 16)
            sp.dma_start(z[:, 16 * P:18 * P], W_out).then_inc(ld_w, 16)
            sp.dma_start(cbh[:], conv_b.rearrange("(k p) -> p k", p=P), allow_slow_non_contiguous=True).then_inc(ld_w, 16)
            sp.dma_start(bdt[:], b_dt.rearrange("(k p) -> p k", p=P), allow_slow_non_contiguous=True).then_inc(ld_w, 16)
            sp.dma_start(dpar[:], D_param.rearrange("(k p) -> p k", p=P), allow_slow_non_contiguous=True).then_inc(ld_w, 16)
            sp.dma_start(asc[:], A_log.rearrange("(k p) n -> p k n", p=P)).then_inc(ld_w, 16)
            sp.dma_start(nw[:], norm_w.rearrange("(p o) -> p o", o=1)).then_inc(ld_w, 16)
            sp.dma_start(rs[:], residual_scale.unsqueeze(0).to_broadcast([P, 1])).then_inc(ld_w, 16)
            sp.dma_start(wg_s[:], Wg).then_inc(ld_w, 16)
            sp.wait_ge(const_dve, 6)
            sp.dma_start(z[0:NST, 14 * P:16 * P], W_C).then_inc(ld_bc, 16)
            sp.dma_start(z[32:32 + NST, 14 * P:16 * P], W_B).then_inc(ld_bc, 16)
            sp.dma_start(z[64:64 + NST, 14 * P:16 * P], W_C).then_inc(ld_bc, 16)
            sp.dma_start(z[96:96 + NST, 14 * P:16 * P], W_C).then_inc(ld_bc, 16)
            sp.dma_start(xpad[0:TOK, :].rearrange("(r k) m -> r (k m)", r=P),
                         x.rearrange("b (r k) m -> (b r) (k m)", r=P // B)).then_inc(st_pad, 16)
            sp.dma_start(xpad[TOK:TOK + GRID, :], zeros[0:GRID, :]).then_inc(st_pad, 16)
            sp.dma_start(disp_d.rearrange("(p k) m -> p k m", p=P),
                         zeros[:].unsqueeze(1).to_broadcast([P, NT, P])).then_inc(st_zero, 16)

            def store_xx(v):
                sp.wait_ge(xn_ready, v + 1)
                sp.dma_start(xx_d[bass.ds(v, 1)].rearrange("o p c -> p (o c)"),
                             xx[:].rearrange("p i m -> p (i m)")).then_inc(st_xx, 16)

            def store_b(v):
                sp.wait_ge(bsb_ready, v + 1)
                sp.dma_start(b_d[bass.ds(v, 1)].rearrange("o s n c -> (o n) s c"),
                             bsb[32:32 + NST].rearrange("p s b t -> p s (b t)")).then_inc(st_b, 16)
                sp.wait_ge(st_b, 16 * (v + 1))

            def spread_b(w, s, first=False):
                S = SPW * w + s
                at_least(sp, bm_done, 2 * (S - RING + 1))
                sp.dma_start(bb[:, s % RING, :],
                             b_d[bass.ds(w, 1), s].rearrange("o n c -> o (n c)")
                             .to_broadcast([P, NST * BS])).then_inc(ld_bb[s % RING], 16)

            def load_x(v):
                sp.wait_ge(xT_done, v)
                for q in range(2):
                    src = xpad[bass.ds(WIN * v - 3 + q * T, (TILES - 1) * 2 * T + GRID), :]
                    src = bass.AP(tensor=src.tensor, offset=src.offset,
                                  ap=[[DM, GRID], [2 * T * DM, TILES], [1, DM]])
                    sp.dma_start(xt[q * GRID:(q + 1) * GRID, :, :], src).then_inc(ld_x, 16)

            def load_xx(o):
                at_least(sp, st_x1, 64 * o)
                if isinstance(o, int):
                    sp.wait_ge(st_xx, 16 * (o + 1))
                sp.dma_start(xxr[:].rearrange("p i m -> p (i m)"),
                             xx_d[bass.ds(o, 1)].rearrange("o p c -> p (o c)")).then_inc(ld_xx, 16)

            def store_out(o, n):
                sp.wait_ge(h2_ready, o + 1)
                for buf, dst in ((xxr, x1_d), (h2b, h2_d)):
                    for q in range(2):
                        d = dst[bass.ds(WIN * o + q * T, (TILES - 1) * 2 * T + n), :]
                        d = bass.AP(tensor=d.tensor, offset=d.offset,
                                    ap=[[DM, n], [2 * T * DM, TILES], [1, DM]])
                        sp.dma_start(d, buf[q * GRID + 3:q * GRID + 3 + n, :, :]).then_inc(st_x1, 16)

            def store_lg(o, n):
                sp.wait_ge(lg_ready, o + 1)
                for q in range(2):
                    d = lg_d[bass.ds(WIN * o + q * T, (TILES - 1) * 2 * T + n), :]
                    d = bass.AP(tensor=d.tensor, offset=d.offset,
                                ap=[[E, n], [2 * T * E, TILES], [1, E]])
                    sp.dma_start(d, lgb[q * GRID + 3:q * GRID + 3 + n, :, :]).then_inc(st_lg, 16)

            store_xx(0)
            sp.wait_ge(xT_done, 1)
            load_x_direct(WIN - 3, GRID, 0)
            sp.wait_ge(b0_ready, 1)
            sp.dma_start(b0_d, b0s[32:32 + NST, :]).then_inc(st_b0, 16)
            sp.wait_ge(st_b0, 16)
            sp.dma_start(b0b[:].rearrange("p n b -> p (n b)"),
                         b0_d.rearrange("(o n) b -> o (n b)", o=1).to_broadcast([P, NST * B])).then_inc(ld_b0, 16)
            store_b(0)
            for s in range(RING):
                spread_b(0, s)
            store_xx(1)
            sp.wait_ge(st_pad, 32)
            load_x(2)

            def iteration(w, prep, ln, out_, nseg):
                for s in range(nseg):
                    if s == 0 and out_:
                        load_xx(w - 1)
                    if s == 1 and out_ == 2:
                        store_lg(w - 2, WIN)
                    if s == 3 and prep:
                        store_b(w + 1)
                    if s + RING < nseg:
                        spread_b(w, s + RING)
                    elif prep:
                        spread_b(w + 1, s + RING - SPW)
                    if s == 5 and ln:
                        store_xx(w + 2)
                    if s == nseg - 1 and out_:
                        store_out(w - 1, WIN)
                    if s == 5 and ln == 2:
                        load_x(w + 3)

            iteration(0, True, 2, 0, SPW)
            iteration(1, True, 2, 1, SPW)
            with sp.Fori(2, NWIN - 3) as w:
                iteration(w, True, 2, 2, SPW)
            iteration(NWIN - 3, True, 1, 2, SPW)
            iteration(NWIN - 2, True, 0, 2, SPW)
            iteration(NWIN - 1, False, 0, 2, LAST_SEGS)
            load_xx(NWIN - 1)
            store_lg(NWIN - 2, WIN)
            store_out(NWIN - 1, T - WIN * (NWIN - 1))
            store_lg(NWIN - 1, T - WIN * (NWIN - 1))
            sp.wait_ge(st_x1, 64 * NWIN)
            sp.wait_ge(st_lg, 32 * NWIN)
            sp.wait_ge(st_zero, 16)
            sp_tail(sp)

        @block.gpsimd
        def _(pool):
            pool.memset(ident[:], 0.0).then_inc(const_pool, 1)
            pool.memset(sel[:], 0.0).then_inc(const_pool, 1)
            pool.wait_ge(const_pool, 2)
            pool.affine_select(out=ident[:], in_=ident[:], compare_op=ALU.not_equal, fill=1.0, base=0,
                               pattern=[[-1, P]], channel_multiplier=1).then_inc(const_pool, 1)
            for k, off in enumerate((0, 64, 96)):
                pool.affine_select(out=sel[:], in_=sel[:], compare_op=ALU.not_equal, fill=1.0, base=-off,
                                   pattern=[[-1, NST], [0, P]], channel_multiplier=1).then_inc(const_pool, 1)
                pool.wait_ge(const_pool, 4 + k)
            pool.memset(tri[:], 1.0).then_inc(const_pool, 1)
            pool.wait_ge(const_pool, 7)
            pool.affine_select(out=tri[:], in_=tri[:], compare_op=ALU.is_gt, fill=0.0, base=0,
                               pattern=[[1, P]], channel_multiplier=-1).then_inc(const_pool, 1)
            pool.iota(iota_i[:], [[1, E]], base=-E, channel_multiplier=0).then_inc(const_pool, 1)

            LNK = 8

            def ln_pool(v):
                pool.wait_ge(ln_stat, v + 1)
                n = [0]

                def step(ins):
                    n[0] += 1
                    ins.then_inc(ln_small, 1)
                    pool.wait_ge(ln_small, LNK * v + n[0])

                rstd, q, q2, q3, r2, r12, a1 = (lnp[:, k, :] for k in range(7))
                step(pool.tensor_tensor(rstd, ve[:], neghalf_e[:], ALU.pow))
                step(pool.tensor_tensor(q, rstd, rstd, ALU.mult))
                step(pool.tensor_tensor(q2, q, mv[:, :, 1], ALU.mult))
                step(pool.tensor_tensor(q3, q2, eps_rms[:], ALU.add))
                step(pool.tensor_tensor(r2, q3, neghalf_e[:], ALU.pow))
                step(pool.tensor_tensor(r12, rstd, r2, ALU.mult))
                step(pool.tensor_tensor(a1, rstd, ones4[:], ALU.add))
                step(pool.tensor_tensor(q, mv[:, :, 0], rstd, ALU.mult))

            def make_u(v):
                pool.wait_ge(dt_step, 2 * (v + 1))
                pool.wait_ge(xc_ready, v + 1)
                at_least(pool, bm_done, 2 * SPW * v)
                pool.tensor_tensor(u[:], dtb[:], xc[:], ALU.mult).then_inc(u_done, 1)

            def products(w, s, hf):
                S = SPW * w + s
                pool.wait_ge(u_done, w + 1)
                pool.wait_ge(ld_bb[s % RING], 16 * (SPW // RING * w + s // RING + 1))
                at_least(pool, y_done, S - RING + 1)
                us = cols(u, hf)[:, :, SEG * s + 1:SEG * s + 1 + SEG]
                hr = rows(h, s % RING)
                for k in range(4):
                    n0, nn = k * NST // 4, NST // 4
                    o = hr[:, hf * RH + n0 * B:hf * RH + (n0 + nn) * B, 1:SLOT]
                    ins = pool.tensor_tensor(
                        o.rearrange("p (n b) t -> p n b t", b=B),
                        us.unsqueeze(1).to_broadcast([P, nn, B, SEG]),
                        bb[:, s % RING, n0 * BS:(n0 + nn) * BS].rearrange("p (n b t) -> p n b t", b=B, t=SEG),
                        ALU.mult)
                ins.then_inc(bm_done, 1)

            def root(k):
                pool.wait_ge(red_done, k + 1)
                pool.tensor_tensor(nrm8[:], s8[:], half_e[:], ALU.pow).then_inc(pow_done, 1)
                pool.wait_ge(pow_done, k + 1)
                pool.tensor_tensor(nrt8[:], nrm8[:], guard8[:], ALU.add).then_inc(nrt_done, 1)

            def out_pool(o):
                pool.wait_ge(st2_done, o + 1)
                pool.tensor_tensor(rstd2[:], ve2[:], neghalf_e[:], ALU.pow).then_inc(rstd2_done, 1)

            pool.wait_ge(const_dve, 7)
            ln_pool(0)
            ln_pool(1)
            make_u(0)
            pool.wait_ge(u_done, 1)
            pool.wait_ge(ld_b0, 16)
            for hf in range(H):
                pool.tensor_tensor(sqb[:, hf * RH:(hf + 1) * RH].rearrange("p (n b) -> p n b", b=B),
                                   cols(u, hf)[:, :, 0].unsqueeze(1).to_broadcast([P, NST, B]),
                                   b0b[:], ALU.mult).then_inc(pre_done, 1)
            root(0)
            products(0, 0, 0)
            products(0, 0, 1)
            products(0, 1, 0)

            def iteration(w, prep, ln, out_, nseg):
                for s in range(nseg):
                    S = SPW * w + s
                    if s + 1 < nseg:
                        products(w, s + 1, 1)
                    elif prep:
                        products(w + 1, 0, 1)
                    if s == 2 and out_:
                        out_pool(w - 1)
                    if s == 3 and ln:
                        ln_pool(w + 2)
                    if prep or s + 1 < nseg:
                        root(S + 1)
                    if s == 4 and prep:
                        make_u(w + 1)
                    if s + 2 < nseg:
                        products(w, s + 2, 0)
                    elif prep:
                        products(w + 1, s + 2 - SPW, 0)

            iteration(0, True, 1, 0, SPW)
            with pool.Fori(1, NWIN - 2) as w:
                iteration(w, True, 1, 1, SPW)
            iteration(NWIN - 2, True, 0, 1, SPW)
            iteration(NWIN - 1, False, 0, 1, LAST_SEGS)
            out_pool(NWIN - 1)
            pool_tail(pool)

        @block.scalar
        def _(act):
            act.wait_ge(ld_w, 16 * N_WLOAD)
            act.activation(asc[:], asc[:], ACT.Tanh, scale=0.1).then_inc(asc_s, 1)
            act.wait_ge(asc_s, 1)
            act.activation(asc[:], asc[:], ACT.Exp, scale=10.0).then_inc(asc_s, 1)
            act.wait_ge(asc_s, 2)
            act.mul(asc[:], asc[:], -1.0 / 16.0).then_inc(asc_s, 1)
            act.activation(rs[:], rs[:], ACT.Tanh, scale=0.5).then_inc(rs_s, 1)
            act.mul(cbh[:], cbh[:], 0.5).then_inc(asc_s, 1)
            act.wait_ge(asc_s, 4)

            def evac_xT(v):
                act.wait_ge(xT_done, v + 1)
                at_least(act, g_done, 2 * v)
                act.copy(xnT[:].rearrange("p b t -> p (b t)"), bank(B_XT)).then_inc(xnT_ready, 1)

            def decay(w, s):
                S = SPW * w + s
                act.wait_ge(tanh_done, w + 1)
                at_least(act, scan_done, S - RING + 1)
                act.activation(rows(dA, s % RING)[:, :, 1:SLOT], zall[:, :, SEG * s:SEG * (s + 1)],
                               ACT.Exp, scale=16.0).then_inc(exp_done, 1)

            def take_over(w):
                act.wait_ge(sg_made, 2 * (w + 1))
                at_least(act, yg_done, SPW * w)
                act.copy(sgc[:], sgn[:]).then_inc(sg_ready, 1)
                act.wait_ge(xc_ready, w + 1)
                at_least(act, y_done, SPW * w)
                for hf in range(H):
                    act.activation(dxc[:, hf, :], xc[:, hf, :], ACT.Copy, scale=dpar[:, hf:hf + 1]).then_inc(dxc_ready, 1)

            def silu(v):
                for hf in range(H):
                    act.wait_ge(xh_done, 2 * v + hf + 1)
                    if hf == 0:
                        at_least(act, sp_ready, v)
                        at_least(act, u_done, v)
                        at_least(act, bc_done, v)
                        at_least(act, dxc_ready, 2 * v)
                    act.activation(thx[:, hf, :], bankc(B_XH[hf]), ACT.Tanh, bias=cbh[:, hf:hf + 1])
                    act.activation(xc[:, hf, :], bankc(B_XH[hf]), ACT.Identity, bias=cbh[:, hf:hf + 1]).then_inc(x_read, 1)
                at_least(act, sg_ready, v)
                for hf in range(H):
                    act.wait_ge(g_done, 2 * v + hf + 1)
                    act.activation(sgn[:, hf, :], bankc(B_G[hf]), ACT.Tanh).then_inc(tg_done, 1)

            def softplus(v):
                at_least(act, u_done, v)
                for hf in range(H):
                    act.wait_ge(dt_done, 2 * v + hf + 1)
                    act.activation(dtb[:, hf, :], bankc(B_DT[hf]), ACT.Abs, bias=bdt[:, hf:hf + 1])
                    if hf == 0:
                        act.wait_ge(xc_ready, v + 1)
                    act.activation(thx[:, hf, :], bankc(B_DT[hf]), ACT.Relu, bias=bdt[:, hf:hf + 1]).then_inc(dt_read, 1)
                act.wait_ge(bc_done, v + 1)
                at_least(act, cs_step, 5 * v)
                act.copy(bcraw[:], bankc(B_BC)).then_inc(bc_read, 1)
                at_least(act, st_b, 16 * v)
                act.copy(bsb[32:32 + NST].rearrange("p s b t -> p b s t"),
                         ps[32:32 + NST, B_BC, 0:B * COLS].rearrange("p (b c) -> p b c", b=B)[:, :, 1:COLS]
                         .rearrange("p b (s t) -> p b s t", t=SEG)).then_inc(bsb_ready, 1)
                if isinstance(v, int) and v == 0:
                    act.copy(b0s[32:32 + NST, :],
                             ps[32:32 + NST, B_BC, 0:B * COLS].rearrange("p (b c) -> p b c", b=B)[:, :, 0]).then_inc(b0_ready, 1)
                act.wait_ge(dt_read, 2 * (v + 1))
                act.activation(dtb[:], dtb[:], ACT.Exp, scale=-1.0).then_inc(ln_step, 1)
                act.wait_ge(ln_step, 2 * v + 1)
                act.activation(dtb[:], dtb[:], ACT.Ln, bias=1.0).then_inc(ln_step, 1)

            def clamp_dt(v):
                act.wait_ge(sp_ready, v + 1)
                act.activation(dtb[:], dtb[:], ACT.Tanh, scale=0.5 / 0.0495, bias=spb[:, 0:1]).then_inc(dt_step, 1)
                act.wait_ge(dt_step, 2 * v + 1)
                act.activation(dtb[:], dtb[:], ACT.Copy, scale=0.0495 / 0.5, bias=0.0505).then_inc(dt_step, 1)
                act.wait_ge(dt_step, 2 * (v + 1))

            def decay_tanh(v):
                at_least(act, exp_done, SPW * v)
                for hf in range(H):
                    for n in range(NST):
                        ins = act.activation(zrow[:, hf * NST + n], cols(dtb, hf)[:, :, 1:COLS], ACT.Tanh,
                                             scale=asc[:, hf, n:n + 1])
                ins.then_inc(tanh_done, 1)

            evac_xT(0)
            silu(0)
            softplus(0)
            clamp_dt(0)
            act.wait_ge(wtr_done, 5)
            decay_tanh(0)

            def iteration(w, prep, nseg):
                if prep:
                    evac_xT(w + 1)
                for s in range(3):
                    decay(w, s)
                take_over(w)
                if prep:
                    silu(w + 1)
                decay(w, 3)
                if prep:
                    decay(w, 4)
                    softplus(w + 1)
                    decay(w, 5)
                    clamp_dt(w + 1)
                    decay_tanh(w + 1)

            iteration(0, True, SPW)
            with act.Fori(1, NWIN - 1) as w:
                iteration(w, True, SPW)
            iteration(NWIN - 1, False, LAST_SEGS)
            act_tail(act)

        @block.vector
        def _(dve):
            dve.memset(xt[:], 0.0).then_inc(const_dve, 1)
            dve.memset(norm_w8[:], 1.0 / MAX_NORM ** 2).then_inc(const_dve, 1)
            dve.memset(zeros[:], 0.0).then_inc(const_dve, 1)
            dve.memset(half_e[:], 0.5).then_inc(const_dve, 1)
            dve.memset(neghalf_e[:], -0.5).then_inc(const_dve, 1)
            dve.memset(eps_rms[:], 1e-6)
            dve.memset(ones4[:], 1.0)
            dve.memset(guard8[:], 1e-8 / MAX_NORM)
            dve.memset(spb[:], -0.0505 * 0.5 / 0.0495)
            dve.memset(z[:, 14 * P:16 * P], 0.0).then_inc(const_dve, 1)
            dve.memset(yg[:], 0.0)
            for r in range(RING):
                ins = dve.memset(rows(dA, r)[:, :, 0], 0.0)
            ins.then_inc(const_dve, 1)

            def ln_stats(v, src, b6, m2, e1, ready, count, step, done):
                dve.wait_ge(ready, count)
                for i in range(TILES):
                    ins = dve.bn_stats(b6[:, i, :], src[:, i, :])
                ins.then_inc(step, 1)
                dve.wait_ge(step, 2 * v + 1)
                dve.memset(pad[:], 0.0)
                for i in range(TILES):
                    ins = dve.bn_aggr(m2[:, i, :], b6[:, i, :])
                ins.then_inc(step, 1)
                dve.wait_ge(step, 2 * (v + 1))
                dve.tensor_scalar(e1[:], m2[:, :, 1], 1e-5, None, ALU.add).then_inc(done, 1)

            def ln_in(v):
                ln_stats(v, xt, bst, mv, ve, ld_x, 32 * (v + 1), stat_step, ln_stat)

            def ln_apply(v):
                dve.wait_ge(ln_small, 8 * (v + 1))
                at_least(dve, st_xx, 16 * v)
                for i in range(TILES):
                    dve.tensor_scalar(xx[:, i, :], xt[:, i, :], lnp[:, 6, i:i + 1], lnp[:, 1, i:i + 1],
                                      ALU.mult, ALU.subtract)
                for i in range(TILES):
                    ins = dve.tensor_scalar(xt[:, i, :], xt[:, i, :], mv[:, i, 0:1], lnp[:, 5, i:i + 1],
                                            ALU.subtract, ALU.mult)
                ins.then_inc(xn_ready, 1)

            def make_xc(v):
                for hf in range(H):
                    dve.wait_ge(x_read, 2 * v + hf + 1)
                    ins = dve.scalar_tensor_tensor(out=xc[:, hf, :], in0=thx[:, hf, :], scalar=1.0,
                                                   in1=xc[:, hf, :], op0=ALU.add, op1=ALU.mult)
                ins.then_inc(xc_ready, 1)
                for hf in range(H):
                    dve.wait_ge(tg_done, 2 * v + hf + 1)
                    dve.scalar_tensor_tensor(out=sgn[:, hf, :], in0=sgn[:, hf, :], scalar=1.0,
                                             in1=bankc(B_G[hf]), op0=ALU.add,
                                             op1=ALU.mult).then_inc(sg_made, 1)

            def add_softplus(v):
                dve.wait_ge(ln_step, 2 * (v + 1))
                dve.tensor_tensor(dtb[:], dtb[:], thx[:], ALU.add).then_inc(sp_ready, 1)

            def split_c(v):
                dve.wait_ge(bc_read, v + 1)
                at_least(dve, cb_done, 3 * SPW * v)
                n = [0]

                def step(ins):
                    n[0] += 1
                    ins.then_inc(cs_step, 1)
                    dve.wait_ge(cs_step, 5 * v + n[0])

                step(dve.tensor_copy(cs[:], bcraw[:]))
                step(dve.tensor_tensor(bcraw[64:P], bcraw[64:P], cs[64:P], ALU.subtract))
                step(dve.tensor_copy(cs[64:P], bcraw[64:P]))
                step(dve.tensor_tensor(bcraw[96:P], bcraw[96:P], cs[96:P], ALU.subtract))
                step(dve.tensor_copy(cs[96:P], bcraw[96:P]))

            def sum_norm(k):
                dve.wait_ge(nrm_done, k + 1)
                dve.tensor_reduce(s8[:], ps[:, NB, 0:ROWS].rearrange("p (r b) -> p b r", b=B),
                                  AX_X, ALU.add).then_inc(red_done, 1)

            def restart(k, last, S_next, s_next):
                dve.wait_ge(nrt_done, k + 1)
                dve.reciprocal(fac8[:], nrt8[:]).then_inc(rec_done, 1)
                dve.wait_ge(rec_done, k + 1)
                at_least(dve, y_done, S_next - RING + 1)
                dve.scalar_tensor_tensor(
                    out=rows(h, s_next % RING)[:, :, 0].rearrange("p (r b) -> p r b", b=B),
                    in0=fac8[:].unsqueeze(1).to_broadcast([P, H * NST, B]), scalar=1.0,
                    in1=last.rearrange("p (r b) -> p r b", b=B), op0=ALU.min, op1=ALU.mult).then_inc(h0_ready, 1)

            def gate_y(w, s):
                S = SPW * w + s
                dve.wait_ge(y_done, S + 1)
                dve.wait_ge(sg_ready, w + 1)
                if s == 0:
                    at_least(dve, op_done, w)
                dve.tensor_tensor(
                    yg[:].rearrange("p h b t -> p (h b) t")[:, :, 3 + SEG * s:3 + SEG * (s + 1)],
                    ps[:, YB, 0:H * BS].rearrange("p (r t) -> p r t", t=SEG),
                    sgc[:].rearrange("p h (b c) -> p (h b) c", c=COLS)[:, :, SEG * s:SEG * (s + 1)],
                    ALU.mult).then_inc(yg_done, 1)

            def segment(w, s, last, extra):
                S = SPW * w + s
                dve.wait_ge(exp_done, S + 1)
                dve.wait_ge(bm_done, 2 * (S + 1))
                dve.wait_ge(h0_ready, S + 1)
                hs = h[:, s % RING, :]
                dve.tensor_tensor_scan(hs, dA[:, s % RING, :], hs, 0.0, ALU.mult, ALU.add).then_inc(scan_done, 1)
                dve.wait_ge(scan_done, S + 1)
                hr = rows(h, s % RING)
                hl = hr[:, :, SEG]
                if not last:
                    dve.tensor_tensor(sqb[:], hl, hl, ALU.mult).then_inc(sq_done, 1)
                if s > 0:
                    gate_y(w, s - 1)
                elif not (isinstance(w, int) and w == 0):
                    gate_y(w - 1, SPW - 1)
                h4 = hr.rearrange("p (f r) t -> p f r t", f=H)
                for j, (n0, n1) in enumerate(NCH):
                    dve.wait_ge(cb_done, 3 * S + j + 1)
                    m = h4[:, :, n0 * B:n1 * B, 0:SEG]
                    dve.tensor_tensor(m, m, ps[:, j, 0:(n1 - n0) * BS].rearrange("p (r t) -> p r t", t=SEG)
                                      .unsqueeze(1).to_broadcast([P, H, (n1 - n0) * B, SEG]),
                                      ALU.mult).then_inc(cm_done, 1)
                    if j == 0 and not last:
                        sum_norm(S + 1)
                extra()
                if not last:
                    restart(S + 1, hl, S + 1, s + 1)

            def add_out(o):
                dve.wait_ge(op_done, o + 1)
                dve.wait_ge(ld_xx, 16 * (o + 1))
                dve.scalar_tensor_tensor(out=xxr[:].rearrange("p i m -> p (i m)"), in0=bank(B_OUT), scalar=rs[:, 0:1],
                                         in1=xxr[:].rearrange("p i m -> p (i m)"), op0=ALU.mult,
                                         op1=ALU.add).then_inc(x1_done, 1)

            def out_stats(o):
                ln_stats(o, xxr, bst2, mv2, ve2, x1_done, o + 1, stat2_step, st2_done)

            def make_h2(o):
                dve.wait_ge(rstd2_done, o + 1)
                at_least(dve, st_x1, 64 * o)
                at_least(dve, h2T_done, o)
                for i in range(TILES):
                    ins = dve.tensor_scalar(h2b[:, i, :], xxr[:, i, :], mv2[:, i, 0:1], rstd2[:, i:i + 1],
                                            ALU.subtract, ALU.mult)
                ins.then_inc(h2_ready, 1)

            def evac_h2T(o):
                dve.wait_ge(h2T_done, o + 1)
                at_least(dve, lg_done, o)
                dve.tensor_copy(h2T[:].rearrange("p i m -> p (i m)"), bank(B_H2)).then_inc(h2T_ready, 1)

            def evac_lg(o):
                dve.wait_ge(lg_done, o + 1)
                at_least(dve, st_lg, 32 * o)
                dve.tensor_copy(lgb[:].rearrange("p i e -> p (i e)"), ps[:, B_LG, 0:TILES * E]).then_inc(lg_ready, 1)

            dve.wait_ge(const_pool, 9)
            dve.tensor_copy(iom[:], iota_i[:]).then_inc(iom_s, 1)
            dve.wait_ge(ld_w, 16 * N_WLOAD)
            for hf in range(H):
                for k in range(TAPS):
                    dve.tensor_scalar(nat[:, hf * TAPS + k, :], win_n[:, hf, :], conv_c[:, hf, k:k + 1], 0.5,
                                      ALU.mult, ALU.mult)
            dve.tensor_scalar(nat[:, 8:10, :], win_n[:, 2:4, :], 0.5, None, ALU.mult).then_inc(taps_ready, 1)
            ln_in(0)
            dve.wait_ge(wtr_done, 5)
            dve.tensor_scalar(wT[:, 0:8, :].rearrange("p (k c) m -> p k (c m)", k=2), ps[:, 0:2, :], nw[:, 0:1], None, ALU.mult)
            dve.tensor_scalar(wT[:, 8:10, :], ps[:, 2, 0:2 * P].rearrange("p (k c) -> p k c", c=P), nw[:, 0:1], None, ALU.mult)
            dve.tensor_copy(wT[:, 10:12, :], ps[:, 2, 2 * P:4 * P].rearrange("p (k c) -> p k c", c=P))
            dve.tensor_copy(wT[:, 12:16, :].rearrange("p k c -> p (k c)"), ps[:, 3, :])
            dve.tensor_copy(wT[:, 16:18, :].rearrange("p k c -> p (k c)"), ps[:, 4, 0:2 * P]).then_inc(w_ready, 1)
            dve.wait_ge(rs_s, 1)
            dve.tensor_scalar(rs[:], rs[:], 0.25, 0.25, ALU.mult, ALU.add).then_inc(rs_s, 1)
            ln_apply(0)
            ln_in(1)
            make_xc(0)
            add_softplus(0)
            split_c(0)
            ln_apply(1)
            dve.wait_ge(pre_done, 2)
            dve.tensor_copy(rows(h, 2)[:, :, 1], sqb[:]).then_inc(pre_done, 1)
            dve.wait_ge(pre_done, 3)
            h_first = rows(h, 2)[:, :, 1]
            dve.tensor_tensor(sqb[:], h_first, h_first, ALU.mult).then_inc(sq_done, 1)
            sum_norm(0)
            restart(0, h_first, 0, 0)

            def iteration(w, prep, ln, out_, nseg):
                def extra(s):
                    if s == 0:
                        if out_ == 2:
                            evac_lg(w - 2)
                    if s == 1:
                        if out_:
                            add_out(w - 1)
                        if prep:
                            make_xc(w + 1)
                        if out_:
                            out_stats(w - 1)
                    if s == 2:
                        if prep:
                            add_softplus(w + 1)
                        if ln:
                            ln_in(w + 2)
                    if s == 3 and out_:
                        make_h2(w - 1)
                    if s == 4:
                        if prep:
                            split_c(w + 1)
                        if ln:
                            ln_apply(w + 2)
                    if s == 5 and out_:
                        evac_h2T(w - 1)

                for s in range(nseg):
                    segment(w, s, (not prep) and s == nseg - 1, lambda s=s: extra(s))

            iteration(0, True, 1, 0, SPW)
            iteration(1, True, 1, 1, SPW)
            iteration(2, True, 1, 2, SPW)
            with dve.Fori(3, NWIN - 2) as w:
                iteration(w, True, 1, 2, SPW)
            iteration(NWIN - 2, True, 0, 2, SPW)
            iteration(NWIN - 1, False, 0, 2, LAST_SEGS)
            gate_y(NWIN - 1, LAST_SEGS - 1)
            evac_h2T(NWIN - 2)
            evac_lg(NWIN - 2)
            add_out(NWIN - 1)
            out_stats(NWIN - 1)
            make_h2(NWIN - 1)
            evac_h2T(NWIN - 1)
            evac_lg(NWIN - 1)
            dve_tail(dve)

        @block.tensor
        def _(pe):
            pe.wait_ge(const_pool, 3)
            pe.wait_ge(taps_ready, 1)
            pe.wait_ge(ld_w, 16 * N_WLOAD)
            pe.wait_ge(ld_bc, 64)
            for g in range(5):
                for k in range(4 * g, min(4 * g + 4, 18)):
                    ins = pe.transpose(ps[:, g, (k % 4) * P:(k % 4 + 1) * P], nat[:, k, :], ident[:])
                ins.then_inc(wtr_done, 1)

            def turn_x(v):
                pe.wait_ge(xn_ready, v + 1)
                at_least(pe, bc_read, v)
                at_least(pe, bsb_ready, v)
                if isinstance(v, int) and v == 1:
                    pe.wait_ge(b0_ready, 1)
                for i in range(TILES):
                    ins = pe.transpose(ps[:, B_XT, i * P:(i + 1) * P], xt[:, i, :], ident[:])
                ins.then_inc(xT_done, 1)

            def project(v):
                pe.wait_ge(xnT_ready, v + 1)
                at_least(pe, h2T_ready, v - 2)
                at_least(pe, dt_read, 2 * v)
                for hf in range(H):
                    for k in range(TAPS):
                        ins = pe.matmul(bankc(B_XH[hf]), wT[:, hf * TAPS + k, :], xnT[:, :, k:k + COLS],
                                        start=(k == 0), stop=(k == TAPS - 1))
                    ins.then_inc(xh_done, 1)
                for hf in range(H):
                    pe.wait_ge(x_read, 2 * v + hf + 1)
                    pe.matmul(bankc(B_G[hf]), wT[:, 8 + hf, :], xnT[:, :, 3:GRID],
                              start=True, stop=True).then_inc(g_done, 1)

            def project_dt(v):
                pe.wait_ge(xc_ready, v + 1)
                at_least(pe, x1_done, v - 1)
                for jh in range(H):
                    if jh == 1:
                        pe.wait_ge(sg_made, 2 * v + 1)
                    for ih in range(H):
                        ins = pe.matmul(bankc(B_DT[jh]), wT[:, 10 + jh * H + ih, :], xc[:, ih, :],
                                        start=(ih == 0), stop=(ih == H - 1))
                    ins.then_inc(dt_done, 1)
                pe.wait_ge(sg_made, 2 * v + 2)
                for ih in range(H):
                    ins = pe.matmul(bankc(B_BC), wT[:, 14 + ih, :], xc[:, ih, :], start=(ih == 0), stop=(ih == H - 1))
                ins.then_inc(bc_done, 1)

            def project_out(o):
                pe.wait_ge(yg_done, NSEG if last_window(o) else SPW * (o + 1))
                at_least(pe, lg_ready, o)
                if not last_window(o):
                    pe.wait_ge(dt_read, 2 * (o + 1) + 1)
                for i in range(TILES):
                    for hf in range(H):
                        ins = pe.matmul(ps[:, B_OUT, i * P:(i + 1) * P],
                                        yg[:, hf].rearrange("p b t -> p (b t)")[:, i * P:(i + 1) * P],
                                        wT[:, 16 + hf, :], start=(hf == 0), stop=(hf == H - 1))
                ins.then_inc(op_done, 1)

            def last_window(o):
                return isinstance(o, int) and o == NWIN - 1

            def turn_h2(o, v):
                pe.wait_ge(h2_ready, o + 1)
                if v is not None:
                    pe.wait_ge(dt_read, 2 * v + 2)
                for i in range(TILES):
                    ins = pe.transpose(ps[:, B_H2, i * P:(i + 1) * P], h2b[:, i, :], ident[:])
                ins.then_inc(h2T_done, 1)

            def route(o, v):
                pe.wait_ge(h2T_ready, o + 1)
                if v is not None:
                    pe.wait_ge(dt_read, 2 * v + 1)
                pe.wait_ge(x1_done, o + 1)
                for i in range(TILES):
                    ins = pe.matmul(ps[:, B_LG, i * E:(i + 1) * E], h2T[:, i, :], wg_s[:], start=True, stop=True)
                ins.then_inc(lg_done, 1)

            def norm_mm(k):
                pe.wait_ge(sq_done, k + 1)
                at_least(pe, red_done, k)
                pe.matmul(ps[:, NB, 0:ROWS], norm_w8[:], sqb[:], start=True, stop=True).then_inc(nrm_done, 1)

            def spread_c(w, s, j):
                S = SPW * w + s
                at_least(pe, cm_done, 3 * (S - 1) + j + 1)
                pe.wait_ge(cs_step, 5 * (w + 1))
                n0, n1 = NCH[j]
                for n in range(n0, n1):
                    ins = pe.matmul(ps[:, j, (n - n0) * BS:(n - n0 + 1) * BS], sel[:, n, :],
                                    cs[:].rearrange("p (b c) -> p b c", b=B)[:, :, SEG * s:SEG * (s + 1)],
                                    start=True, stop=True)
                ins.then_inc(cb_done, 1)

            def sum_states(w, s, j):
                S = SPW * w + s
                pe.wait_ge(cm_done, 3 * S + j + 1)
                if j == 0:
                    at_least(pe, yg_done, S)
                hr = rows(h, s % RING).rearrange("p (f r) t -> p f r t", f=H)
                n0, n1 = NCH[j]
                for n in range(n0, n1):
                    pe.matmul(ps[:, YB, 0:H * BS], ident[:], hr[:, :, n * B:(n + 1) * B, 0:SEG],
                              start=(n == 0), stop=False)

            def add_dx(w, s):
                pe.wait_ge(dxc_ready, 2 * (w + 1))
                pe.matmul(ps[:, YB, 0:H * BS], ident[:],
                          dxc[:].rearrange("p h (b c) -> p (h b) c", c=COLS)[:, :, SEG * s:SEG * (s + 1)],
                          start=False, stop=True).then_inc(y_done, 1)

            pe.wait_ge(w_ready, 1)
            pe.wait_ge(const_dve, 7)
            turn_x(0)
            pe.wait_ge(asc_s, 4)
            project(0)
            project_dt(0)
            pe.wait_ge(const_pool, 6)
            for j in range(3):
                spread_c(0, 0, j)
            turn_x(1)
            norm_mm(0)

            def iteration(w, prep, ln, out_, nseg):
                v = w + 1 if prep else None
                for s in range(nseg):
                    S = SPW * w + s
                    last = (not prep) and s == nseg - 1
                    if not last:
                        norm_mm(S + 1)
                    for j in range(3):
                        if s + 1 < nseg:
                            spread_c(w, s + 1, j)
                        elif prep:
                            spread_c(w + 1, 0, j)
                        sum_states(w, s, j)
                    add_dx(w, s)
                    if out_ and s == 0:
                        project_out(w - 1)
                    if prep:
                        if s == 0:
                            project(w + 1)
                        if s == 1:
                            project_dt(w + 1)
                    if out_:
                        if s == (4 if prep else 3):
                            turn_h2(w - 1, v)
                        if s == 5:
                            route(w - 1, v)
                    if ln and s == 5:
                        turn_x(w + 2)

            iteration(0, True, 1, 0, SPW)
            iteration(1, True, 1, 1, SPW)
            with pe.Fori(2, NWIN - 2) as w:
                iteration(w, True, 1, 1, SPW)
            iteration(NWIN - 2, True, 0, 1, SPW)
            iteration(NWIN - 1, False, 0, 1, LAST_SEGS)
            route(NWIN - 2, None)
            project_out(NWIN - 1)
            turn_h2(NWIN - 1, None)
            route(NWIN - 1, None)
            pe_tail(pe)


_INS = ['L0_attn_x', 'L0_attn_norm_w', 'L0_attn_W_in', 'L0_attn_conv_w', 'L0_attn_conv_b', 'L0_attn_W_dt',
        'L0_attn_b_dt', 'L0_attn_W_B', 'L0_attn_W_C', 'L0_attn_A_log', 'L0_attn_D_param', 'L0_attn_W_out',
        'L0_attn_residual_scale', 'L0_ffn_Wg', 'L0_ffn_w1', 'L0_ffn_w2']


def kernel(**inputs):
    import numpy as _np
    import concourse.bacc as _bacc
    from concourse import mybir as _mybir
    from concourse.bass_utils import run_bass_kernel_spmd as _run

    nc = _bacc.Bacc("TRN2", target_bir_lowering=False, num_devices=1)
    arrays, args = {}, []
    for name in _INS:
        a = _np.ascontiguousarray(inputs[name])
        if a.ndim == 0:
            a = a.reshape(1)
        arrays[f"in_{name}_dram"] = a
        args.append(nc.dram_tensor(f"in_{name}_dram", a.shape, _mybir.dt.from_np(a.dtype), kind="ExternalInput").ap())
    shape = inputs['L0_attn_x'].shape
    args.append(nc.dram_tensor("out_0_dram", shape, _mybir.dt.float32, kind="ExternalOutput").ap())
    mamba_moe(nc, *args)
    r = _run(nc, [arrays], core_ids=[0])
    return r.results[0]["out_0_dram"]
```

```python
from contextlib import ExitStack

import concourse.bass as bass
from concourse import mybir

ALU = mybir.AluOpType
ACT = mybir.ActivationFunctionType
AX_X = mybir.AxisListType.X
F32 = mybir.dt.float32
BF16 = mybir.dt.bfloat16
I32 = mybir.dt.int32

P = 128
SEG = 10
SLOT = SEG + 1
SPW = 6
WIN = SPW * SEG
COLS = WIN + 1
TAPS = 4
GRID = WIN + TAPS
RING = 3
CAP_MISS = 65536.0
MAX_NORM = 20.0
E_MAX = 2.0 ** 57


def at_least(eng, sem, n):
    if isinstance(n, int) and n <= 0:
        return
    eng.wait_ge(sem, n)


def mamba_moe(nc, x, norm_w, W_in, conv_w, conv_b, W_dt, b_dt, W_B, W_C, A_log, D_param, W_out,
              residual_scale, Wg, w1, w2, out):
    B, T, DM = x.shape
    DI, NST = A_log.shape
    E, _, F = w1.shape
    H = DI // P
    RH = NST * B
    ROWS = H * RH
    NSEG = (T + SEG - 1) // SEG
    NWIN = (NSEG + SPW - 1) // SPW
    TILES = B * GRID // P
    TOK = B * T
    NT = TOK // P
    CAP = (TOK + E - 1) // E
    FC = F // P
    CT = CAP // P
    assert DM == P and TILES * P == 512 and CAP == 256 and NWIN == 9 and B * SEG * H == 160
    BS = B * SEG
    NCH = [(0, 6), (6, 12), (12, 16)]

    with ExitStack() as ctx:
        def sb(name, shape, dt=F32):
            return ctx.enter_context(nc.sbuf_tensor(name, shape, dt))

        def sem(name):
            return ctx.enter_context(nc.semaphore(name))

        def dram(name, shape):
            return nc.dram_tensor(name, shape, F32, kind="Internal").ap()

        xpad = dram("xpad", (TOK + GRID, DM))
        b_d = dram("b_d", (NWIN, SPW, NST, BS))
        b0_d = dram("b0_d", (NST, B))
        xx_d = dram("xx_d", (NWIN, P, TILES * DM))
        x1_d = dram("x1_d", (TOK, DM))
        h2_d = dram("h2_d", (TOK, DM))
        lg_d = dram("lg_d", (TOK, E))
        disp_d = dram("disp_d", (TOK, DM))
        eo_d = dram("eo_d", (TOK, DM))

        ident = sb("ident", [P, P])
        ones_r = sb("ones_r", [B, P])
        bound_w = sb("bound_w", [P, 1])
        padp = sb("padp", [B, H])
        zeros = sb("zeros", [P, P])
        sel = sb("sel", [P, NST, P], BF16)
        wT = sb("wT", [P, 18, P])
        conv_c = sb("conv_c", [P, H, TAPS])
        cbh = sb("cbh", [P, H])
        bdt = sb("bdt", [P, H])
        dpar = sb("dpar", [P, H])
        asc = sb("asc", [P, H, NST])
        nw = sb("nw", [P, 1])
        rs = sb("rs", [P, 1])
        wg_s = sb("wg_s", [P, E])
        half_e = sb("half_e", [B, 1])
        eps_rms = sb("eps_rms", [P, TILES])
        ones4 = sb("ones4", [P, TILES])
        guard8 = sb("guard8", [B, 1])
        neghalf_e = sb("neghalf_e", [P, TILES])
        spb = sb("spb", [P, 1])
        pad = sb("pad", [P, 1])
        tri = sb("tri", [P, P])
        iota_i = sb("iota_i", [P, E], I32)
        iom = sb("iom", [P, E])

        z = sb("z", [P, H * NST * B * WIN])
        dA = sb("dA", [P, RING, ROWS * SLOT])
        h = sb("h", [P, RING, ROWS * SLOT])
        bb = sb("bb", [P, RING, NST * BS])
        sqb = sb("sqb", [P, ROWS])
        s_p = sb("s_p", [P, B])
        s8 = sb("s8", [B, 1])
        nrm8 = sb("nrm8", [B, 1])
        nrt8 = sb("nrt8", [B, 1])
        fac8 = sb("fac8", [B, 1])
        fac_d = sb("fac_d", [B, B])

        xt = sb("xt", [P, TILES, DM])
        xx = sb("xx", [P, TILES, DM])
        xxr = sb("xxr", [P, TILES, DM])
        xnT = sb("xnT", [P, B, GRID])
        bst = sb("bst", [P, TILES, 6])
        mv = sb("mv", [P, TILES, 2])
        ve = sb("ve", [P, TILES])
        lnp = sb("lnp", [P, 7, TILES])
        bst2 = sb("bst2", [P, TILES, 6])
        mv2 = sb("mv2", [P, TILES, 2])
        ve2 = sb("ve2", [P, TILES])
        rstd2 = sb("rstd2", [P, TILES])
        thx = sb("thx", [P, H, B * COLS])
        xc = sb("xc", [P, H, B * COLS])
        sgn = sb("sgn", [P, H, B * COLS])
        sgc = sb("sgc", [P, H, B * COLS])
        dtb = sb("dtb", [P, H, B * COLS])
        u = sb("u", [P, H, B * COLS])
        dxc = sb("dxc", [P, H, B * COLS])
        bcraw = sb("bcraw", [P, B * COLS])
        bsb = sb("bsb", [P, SPW, B, SEG])
        b0s = s_p
        b0b = sb("b0b", [P, NST, B])
        cs_next = sb("cs_next", [P, B * COLS], BF16)
        cs = sb("cs", [P, B * COLS], BF16)
        yg = sb("yg", [P, H, B, GRID])
        h2b = sb("h2b", [P, TILES, DM])
        h2T = sb("h2T", [P, TILES, P])
        lgb = sb("lgb", [P, TILES, E])

        ps = ctx.enter_context(nc.psum_tensor("ps", [P, 8, 512], F32))
        YB, NB, P0, P1, P2 = 3, 4, 5, 6, 7
        B_XH = B_G = B_DT = (P0, P2)
        B_XT = B_BC = B_H2 = B_OUT = B_LG = P1

        def cols(t, hf):
            return t[:, hf, :].rearrange("p (b c) -> p b c", b=B)

        def rows(t, r):
            return t[:, r, :].rearrange("p (r c) -> p r c", c=SLOT)

        def bank(k):
            return ps[:, k, :]

        def bankc(k):
            return ps[:, k, 0:B * COLS]

        zrow = z[:].rearrange("p (r b t) -> p r b t", r=H * NST, b=B)
        zall = z[:].rearrange("p (r t) -> p r t", t=WIN)

        nat = z[:, 0:18 * P].rearrange("p (k c) -> p k c", c=P)
        win_n = z[:, 18 * P:22 * P].rearrange("p (k c) -> p k c", c=P)

        ld_w = sem("ld_w"); ld_bc = sem("ld_bc"); ld_x = sem("ld_x"); ld_xx = sem("ld_xx")
        ld_bb = [sem(f"ld_bb{r}") for r in range(RING)]; ld_b0 = sem("ld_b0")
        st_pad = sem("st_pad"); st_b = sem("st_b"); st_b0 = sem("st_b0"); st_xx = sem("st_xx")
        st_x1 = sem("st_x1"); st_lg = sem("st_lg"); st_zero = sem("st_zero")
        const_pool = sem("const_pool"); const_dve = sem("const_dve"); asc_s = sem("asc_s")
        taps_ready = sem("taps_ready"); wtr_done = sem("wtr_done"); w_ready = sem("w_ready")
        rs_s = sem("rs_s"); fin_s = sem("fin_s"); iom_s = sem("iom_s")
        ln_stat = sem("ln_stat"); ln_small = sem("ln_small"); xn_ready = sem("xn_ready")
        xT_done = sem("xT_done"); xnT_ready = sem("xnT_ready")
        xh_done = sem("xh_done"); g_done = sem("g_done"); x_read = sem("x_read"); tg_done = sem("tg_done")
        xc_ready = sem("xc_ready"); sg_made = sem("sg_made")
        dt_done = sem("dt_done"); bc_done = sem("bc_done"); dt_read = sem("dt_read"); e_capped = sem("e_capped")
        ln_step = sem("ln_step"); dt_step = sem("dt_step")
        bc_read = sem("bc_read"); bsb_ready = sem("bsb_ready"); b0_ready = sem("b0_ready")
        cs_step = sem("cs_step"); u_done = sem("u_done")
        sg_ready = sem("sg_ready"); dxc_ready = sem("dxc_ready")
        tanh_done = sem("tanh_done")
        exp_done = sem("exp_done"); bm_done = sem("bm_done"); scan_done = sem("scan_done")
        sq_done = sem("sq_done"); nrm_done = sem("nrm_done"); red_done = sem("red_done")
        s8_ready = sem("s8_ready"); fac_made = sem("fac_made"); fac_done = sem("fac_done")
        pow_done = sem("pow_done"); nrt_done = sem("nrt_done"); rec_done = sem("rec_done")
        h0_ready = sem("h0_ready"); cb_done = sem("cb_done"); cm_done = sem("cm_done")
        y_done = sem("y_done"); yg_done = sem("yg_done"); pre_done = sem("pre_done")
        op_done = sem("op_done"); x1_done = sem("x1_done"); st2_done = sem("st2_done")
        rstd2_done = sem("rstd2_done"); h2_ready = sem("h2_ready"); h2T_done = sem("h2T_done")
        h2T_ready = sem("h2T_ready"); lg_done = sem("lg_done"); lg_ready = sem("lg_ready")
        stat_step = sem("stat_step"); stat2_step = sem("stat2_step")

        N_WLOAD = 11
        LAST_SEGS = NSEG - SPW * (NWIN - 1)
        LS = NSEG - 1

        dAf = dA[:].rearrange("p r c -> p (r c)")
        hf_ = h[:].rearrange("p r c -> p (r c)")
        h2a = z[:, 0:NT * DM].rearrange("p (k m) -> p k m", m=DM)
        x1a = z[:, NT * DM:2 * NT * DM].rearrange("p (k m) -> p k m", m=DM)
        gat = z[:, 2 * NT * DM:3 * NT * DM].rearrange("p (k m) -> p k m", m=DM)

        def slab(k):
            return dAf[:, k * NT * E:(k + 1) * NT * E]

        lga, em, ex, eq, cand, ohe, cum, keep = (slab(k) for k in range(8))
        eos = dAf[:, 8 * NT * E:8 * NT * E + 2 * CT * DM].rearrange("p (q t m) -> p q t m", q=2, t=CT)
        small = dAf[:, 9 * NT * E + 2 * CT * DM - NT * E:][:, 0:14 * NT].rearrange("p (k c) -> p k c", c=NT)
        mx, im, slot0, loc, val, miss, si, lc, se, rse, gw = (small[:, k, :] for k in range(11))
        tot = bst[:].rearrange("p i c -> p (i c)")[:, 0:E]
        totp = bst2[:].rearrange("p i c -> p (i c)")[:, 0:E]
        sidx = sb("sidx", [P, NT], I32)
        gidx = sb("gidx", [P, NT], I32)
        WR = 4
        w1s = hf_[:, 0:WR * F].rearrange("p (k f) -> p k f", k=WR)
        w2s = hf_[:, WR * F:2 * WR * F].rearrange("p (k c m) -> p k c m", k=WR, m=DM)
        xs = hf_[:, 2 * WR * F:2 * WR * F + WR * CAP].rearrange("p (k t m) -> p k t m", k=WR, m=DM)
        o0 = 2 * WR * F + WR * CAP
        xTs = hf_[:, o0:o0 + 2 * CAP].rearrange("p (k c) -> p k c", k=2)
        hTs = hf_[:, o0 + 2 * CAP:o0 + 2 * CAP + 2 * FC * CAP].rearrange("p (k c s) -> p k c s", k=2, s=CAP)

        ld_lg = sem("ld_lg"); ld_h2 = sem("ld_h2"); ld_x1 = sem("ld_x1")
        ld_we = [sem(f"ld_we{k}") for k in range(WR)]
        ld_xe = [sem(f"ld_xe{k}") for k in range(WR)]
        rt = sem("rt"); ex_done = sem("ex_done"); pre_mm = sem("pre_mm")
        idx_ready = sem("idx_ready"); scattered = sem("scattered")
        xeT_done = sem("xeT_done"); xeT_ready = sem("xeT_ready"); up_done = sem("up_done")
        relu_a = sem("relu_a"); relu_b = sem("relu_b"); down_done = sem("down_done")
        eo_ready = sem("eo_ready"); st_eo = [sem(f"st_eo{q}") for q in range(2)]
        gathered = [sem(f"gathered{k}") for k in range(4)]
        fin_done = sem("fin_done"); st_out = sem("st_out")
        GT = NT // 4

        def sp_tail(sp):
            sp.wait_ge(exp_done, NSEG)
            sp.wait_ge(scan_done, NSEG)
            sp.dma_start(lga, lg_d.rearrange("(p k) e -> p (k e)", p=P)).then_inc(ld_lg, 16)
            sp.dma_start(h2a, h2_d.rearrange("(p k) m -> p k m", p=P)).then_inc(ld_h2, 16)
            sp.wait_ge(y_done, NSEG)

            def weights(e, k):
                sp.dma_start(w1s[:, k, :], w1[bass.ds(e, 1)].rearrange("o m f -> (o m) f")).then_inc(ld_we[k], 16)
                sp.dma_start(w2s[:, k], w2[bass.ds(e, 1)].rearrange("o (c p) m -> (o p) c m", p=P)).then_inc(ld_we[k], 16)

            def tokens(e, k):
                sp.dma_start(xs[:, k], disp_d[bass.ds(e * CAP, CAP), :].rearrange("(t p) m -> p t m", p=P)).then_inc(ld_xe[k], 16)

            for k in range(WR):
                weights(k, k)
            sp.dma_start(x1a, x1_d.rearrange("(p k) m -> p k m", p=P)).then_inc(ld_x1, 16)
            sp.wait_ge(scattered, 16 * NT)
            for k in range(WR):
                tokens(k, k)

            def expert(e, k, more):
                if more:
                    sp.wait_ge(down_done, e + 1)
                    weights(e + WR, k)
                    tokens(e + WR, k)
                sp.wait_ge(eo_ready, e + 1)
                sp.dma_start(eo_d[bass.ds(e * CAP, CAP), :].rearrange("(t p) m -> p t m", p=P),
                             eos[:, k % 2]).then_inc(st_eo[k % 2], 16)

            with sp.Fori(0, E // WR - 1) as g:
                for k in range(WR):
                    expert(WR * g + k, k, True)
            for k in range(WR):
                expert(E - WR + k, k, False)
            outf = out.rearrange("b t d -> (b t) d").rearrange("(p k) m -> p k m", p=P)
            for g in range(4):
                sp.wait_ge(fin_done, g + 1)
                sp.dma_start(outf[:, g * GT:(g + 1) * GT, :], gat[:, g * GT:(g + 1) * GT, :]).then_inc(st_out, 16)
            sp.wait_ge(st_out, 64)

        def pool_tail(pool):
            pool.wait_ge(idx_ready, 2)
            pool.wait_ge(ld_h2, 16)
            pool.wait_ge(st_zero, 16)
            for k in range(NT):
                pool.indirect_dma_start(disp_d, bass.IndirectOffsetOnAxis(ap=sidx[:, k:k + 1], axis=0), h2a[:, k, :],
                                        None, bounds_check=TOK - 1, oob_is_err=False).then_inc(scattered, 16)
            for q in range(2):
                pool.wait_ge(st_eo[q], 8 * E)
            for k in range(NT):
                pool.indirect_dma_start(gat[:, k, :], None, eo_d, bass.IndirectOffsetOnAxis(ap=gidx[:, k:k + 1], axis=0),
                                        bounds_check=TOK - 1, oob_is_err=False).then_inc(gathered[k // GT], 16)

        def act_tail(act):
            act.wait_ge(rt, 2)
            act.activation(ex, em, ACT.Exp).then_inc(ex_done, 1)

            def turn_in(e, q):
                act.wait_ge(xeT_done, e + 1)
                at_least(act, up_done, 2 * (e - 1))
                act.copy(xTs[:, q, :], ps[:, q, 0:CAP]).then_inc(xeT_ready, 1)

            def relu(e, q):
                act.wait_ge(up_done, 2 * e + 1)
                at_least(act, down_done, e - 1)
                act.activation(hTs[:, q, 0:2].rearrange("p c s -> p (c s)"), ps[:, 2 + 2 * q, :],
                               ACT.Relu).then_inc(relu_a, 1)

            turn_in(0, 0)
            turn_in(1, 1)
            relu(0, 0)
            turn_in(2, 0)
            relu(1, 1)
            with act.Fori(1, E // 2 - 1) as g:
                turn_in(2 * g + 1, 1)
                relu(2 * g, 0)
                turn_in(2 * g + 2, 0)
                relu(2 * g + 1, 1)
            turn_in(E - 1, 1)
            relu(E - 2, 0)
            relu(E - 1, 1)

        def dve_tail(dve):
            v3 = lambda t: t.rearrange("p (k e) -> p k e", e=E)
            e3 = lambda t: t.rearrange("p (e k) -> p e k", k=NT)
            n = [0]

            def step(ins):
                n[0] += 1
                ins.then_inc(rt, 1)
                dve.wait_ge(rt, n[0])

            dve.wait_ge(ld_lg, 16)
            step(dve.tensor_reduce(mx, v3(lga), AX_X, ALU.max))
            step(dve.tensor_tensor(v3(em), v3(lga), mx.unsqueeze(2).to_broadcast([P, NT, E]), ALU.subtract))
            step(dve.tensor_scalar(eq, em, 0.0, None, ALU.is_equal))
            step(dve.tensor_tensor(v3(cand), v3(eq), iom[:].unsqueeze(1).to_broadcast([P, NT, E]), ALU.mult))
            step(dve.tensor_reduce(im, v3(cand), AX_X, ALU.min))
            step(dve.tensor_tensor(e3(ohe), iom[:].unsqueeze(2).to_broadcast([P, E, NT]),
                                   im.unsqueeze(1).to_broadcast([P, E, NT]), ALU.is_equal))
            step(dve.memset(keep, 1.0))
            step(dve.memset(e3(keep)[:, :, 0], 0.0))
            step(dve.tensor_tensor_scan(cum, keep, ohe, 0.0, ALU.mult, ALU.add))
            step(dve.tensor_copy(tot, e3(cum)[:, :, NT - 1]))
            dve.wait_ge(pre_mm, 1)
            step(dve.tensor_scalar(totp, ps[:, 0, 0:E], -1.0, None, ALU.add))
            step(dve.tensor_tensor(e3(cand), e3(cum), totp.unsqueeze(2).to_broadcast([P, E, NT]), ALU.add))
            step(dve.tensor_tensor(cum, cand, ohe, ALU.mult))
            step(dve.tensor_reduce(loc, cum.rearrange("p (e k) -> p k e", k=NT), AX_X, ALU.add))
            step(dve.tensor_scalar(slot0, im, float(CAP), float(E * CAP), ALU.mult, ALU.add))
            step(dve.tensor_scalar(val, loc, float(CAP), None, ALU.is_lt))
            step(dve.tensor_scalar(miss, val, -CAP_MISS, CAP_MISS, ALU.mult, ALU.add))
            step(dve.tensor_tensor(si, slot0, loc, ALU.add))
            step(dve.tensor_tensor(si, si, miss, ALU.add))
            step(dve.tensor_copy(sidx[:], si))
            dve.tensor_scalar(lc, loc, float(CAP - 1), None, ALU.min).then_inc(idx_ready, 1)
            dve.wait_ge(idx_ready, 1)
            dve.tensor_tensor(lc, lc, slot0, ALU.add).then_inc(fin_s, 1)
            dve.wait_ge(fin_s, 1)
            dve.tensor_copy(gidx[:], lc).then_inc(idx_ready, 1)
            dve.wait_ge(ex_done, 1)
            step(dve.tensor_reduce(se, v3(ex), AX_X, ALU.add))
            step(dve.reciprocal(rse, se))
            step(dve.tensor_tensor(gw, rse, val, ALU.mult))

            def relu(e, q):
                dve.wait_ge(up_done, 2 * e + 2)
                at_least(dve, down_done, e - 1)
                dve.tensor_scalar(hTs[:, q, 2:4].rearrange("p c s -> p (c s)"), ps[:, 3 + 2 * q, :], 0.0, None,
                                  ALU.max).then_inc(relu_b, 1)

            def take_out(e, q, before):
                dve.wait_ge(down_done, e + 1)
                at_least(dve, st_eo[q], 16 * before)
                dve.tensor_copy(eos[:, q].rearrange("p t m -> p (t m)"), ps[:, 6 + q, 0:CAP]).then_inc(eo_ready, 1)

            relu(0, 0)
            relu(1, 1)
            take_out(0, 0, 0)
            relu(2, 0)
            take_out(1, 1, 0)
            with dve.Fori(1, E // 2 - 1) as g:
                relu(2 * g + 1, 1)
                take_out(2 * g, 0, g)
                relu(2 * g + 2, 0)
                take_out(2 * g + 1, 1, g)
            relu(E - 1, 1)
            take_out(E - 2, 0, E // 2 - 1)
            take_out(E - 1, 1, E // 2 - 1)
            dve.wait_ge(ld_x1, 16)
            for g in range(4):
                dve.wait_ge(gathered[g], 16 * GT)
                for k in range(g * GT, (g + 1) * GT):
                    ins = dve.scalar_tensor_tensor(out=gat[:, k, :], in0=gat[:, k, :], scalar=gw[:, k:k + 1],
                                                   in1=x1a[:, k, :], op0=ALU.mult, op1=ALU.add)
                ins.then_inc(fin_done, 1)

        def pe_tail(pe):
            pe.wait_ge(rt, 10)
            pe.matmul(ps[:, 0, 0:E], tri[:], tot, start=True, stop=True).then_inc(pre_mm, 1)

            def turn(e, k):
                pe.wait_ge(ld_xe[k], 16 * (e // WR + 1) if isinstance(e, int) else e[1])
                ee = e if isinstance(e, int) else e[0]
                at_least(pe, xeT_ready, ee - 1)
                for t in range(CT):
                    ins = pe.transpose(ps[:, k % 2, t * P:(t + 1) * P], xs[:, k, t, :], ident[:])
                ins.then_inc(xeT_done, 1)

            def up(e, k):
                pe.wait_ge(ld_we[k], 32 * (e // WR + 1) if isinstance(e, int) else 2 * e[1])
                ee = e if isinstance(e, int) else e[0]
                pe.wait_ge(xeT_ready, ee + 1)
                q = k % 2
                for c in range(FC):
                    if c == 0:
                        at_least(pe, relu_a, ee - 1)
                    if c == 2:
                        at_least(pe, relu_b, ee - 1)
                    ins = pe.matmul(ps[:, 2 + 2 * q + c // 2, (c % 2) * CAP:(c % 2 + 1) * CAP],
                                    w1s[:, k, c * P:(c + 1) * P], xTs[:, q, :], start=True, stop=True)
                    if c % 2:
                        ins.then_inc(up_done, 1)

            def down(e, k):
                q = k % 2
                pe.wait_ge(relu_a, e + 1)
                pe.wait_ge(relu_b, e + 1)
                at_least(pe, eo_ready, e - 1)
                for t in range(CT):
                    for c in range(FC):
                        ins = pe.matmul(ps[:, 6 + q, t * P:(t + 1) * P], hTs[:, q, c, t * P:(t + 1) * P],
                                        w2s[:, k, c, :], start=(c == 0), stop=(c == FC - 1))
                ins.then_inc(down_done, 1)

            pe.wait_ge(rt, 11)
            turn(0, 0)
            turn(1, 1)
            up(0, 0)
            turn(2, 2)
            up(1, 1)
            down(0, 0)
            turn(3, 3)
            up(2, 2)
            down(1, 1)
            with pe.Fori(0, E // WR - 1) as g:
                for k in range(3, WR + 3):
                    turn((WR * g + k + 1, 16 * (g + 1 + (k + 1) // WR)), (k + 1) % WR)
                    up((WR * g + k, 16 * (g + 1 + k // WR)), k % WR)
                    down(WR * g + k - 1, (k - 1) % WR)
            up(E - 1, WR - 1)
            down(E - 2, WR - 2)
            down(E - 1, WR - 1)

        block = ctx.enter_context(nc.Block())

        @block.sync
        def _(sp):
            sp.dma_start(win_n, W_in.rearrange("(k p) c -> p k c", p=P)).then_inc(ld_w, 16)
            sp.dma_start(conv_c[:], conv_w.rearrange("(k p) o t -> p k (o t)", p=P)).then_inc(ld_w, 16)
            xq = x.rearrange("(i q) t m -> q t i m", q=2)

            def load_x_direct(t0, n, j0):
                for q in range(2):
                    sp.dma_start(xt[q * GRID + j0:q * GRID + j0 + n, :, :], xq[q, t0:t0 + n]).then_inc(ld_x, 16)

            sp.wait_ge(const_dve, 1)
            load_x_direct(0, GRID - 3, 3)
            sp.dma_start(z[:, 10 * P:14 * P].rearrange("p (j c) -> p j c", j=H),
                         W_dt.rearrange("(j p) c -> p j c", p=P)).then_inc(ld_w, 16)
            sp.dma_start(z[:, 16 * P:18 * P], W_out).then_inc(ld_w, 16)
            sp.dma_start(cbh[:], conv_b.rearrange("(k p) -> p k", p=P), allow_slow_non_contiguous=True).then_inc(ld_w, 16)
            sp.dma_start(bdt[:], b_dt.rearrange("(k p) -> p k", p=P), allow_slow_non_contiguous=True).then_inc(ld_w, 16)
            sp.dma_start(dpar[:], D_param.rearrange("(k p) -> p k", p=P), allow_slow_non_contiguous=True).then_inc(ld_w, 16)
            sp.dma_start(asc[:], A_log.rearrange("(k p) n -> p k n", p=P)).then_inc(ld_w, 16)
            sp.dma_start(nw[:], norm_w.rearrange("(p o) -> p o", o=1)).then_inc(ld_w, 16)
            sp.dma_start(rs[:], residual_scale.unsqueeze(0).to_broadcast([P, 1])).then_inc(ld_w, 16)
            sp.dma_start(wg_s[:], Wg).then_inc(ld_w, 16)
            sp.wait_ge(const_dve, 6)
            sp.dma_start(z[0:NST, 14 * P:16 * P], W_C).then_inc(ld_bc, 16)
            sp.dma_start(z[32:32 + NST, 14 * P:16 * P], W_B).then_inc(ld_bc, 16)
            sp.dma_start(z[64:64 + NST, 14 * P:16 * P], W_C).then_inc(ld_bc, 16)
            sp.dma_start(z[96:96 + NST, 14 * P:16 * P], W_C).then_inc(ld_bc, 16)
            sp.dma_start(xpad[0:TOK, :].rearrange("(r k) m -> r (k m)", r=P),
                         x.rearrange("b (r k) m -> (b r) (k m)", r=P // B)).then_inc(st_pad, 16)
            sp.dma_start(xpad[TOK:TOK + GRID, :], zeros[0:GRID, :]).then_inc(st_pad, 16)
            sp.dma_start(disp_d.rearrange("(p k) m -> p k m", p=P),
                         zeros[:].unsqueeze(1).to_broadcast([P, NT, P])).then_inc(st_zero, 16)

            def store_xx(v):
                sp.wait_ge(xn_ready, v + 1)
                sp.dma_start(xx_d[bass.ds(v, 1)].rearrange("o p c -> p (o c)"),
                             xx[:].rearrange("p i m -> p (i m)")).then_inc(st_xx, 16)

            def store_b(v):
                sp.wait_ge(bsb_ready, v + 1)
                sp.dma_start(b_d[bass.ds(v, 1)].rearrange("o s n c -> (o n) s c"),
                             bsb[32:32 + NST].rearrange("p s b t -> p s (b t)")).then_inc(st_b, 16)
                sp.wait_ge(st_b, 16 * (v + 1))

            def spread_b(w, s, first=False):
                S = SPW * w + s
                at_least(sp, bm_done, 2 * (S - RING + 1))
                sp.dma_start(bb[:, s % RING, :],
                             b_d[bass.ds(w, 1), s].rearrange("o n c -> o (n c)")
                             .to_broadcast([P, NST * BS])).then_inc(ld_bb[s % RING], 16)

            def load_x(v):
                sp.wait_ge(xT_done, v)
                for q in range(2):
                    src = xpad[bass.ds(WIN * v - 3 + q * T, (TILES - 1) * 2 * T + GRID), :]
                    src = bass.AP(tensor=src.tensor, offset=src.offset,
                                  ap=[[DM, GRID], [2 * T * DM, TILES], [1, DM]])
                    sp.dma_start(xt[q * GRID:(q + 1) * GRID, :, :], src).then_inc(ld_x, 16)

            def load_xx(o):
                at_least(sp, st_x1, 64 * o)
                if isinstance(o, int):
                    sp.wait_ge(st_xx, 16 * (o + 1))
                sp.dma_start(xxr[:].rearrange("p i m -> p (i m)"),
                             xx_d[bass.ds(o, 1)].rearrange("o p c -> p (o c)")).then_inc(ld_xx, 16)

            def store_out(o, n):
                sp.wait_ge(h2_ready, o + 1)
                for buf, dst in ((xxr, x1_d), (h2b, h2_d)):
                    for q in range(2):
                        d = dst[bass.ds(WIN * o + q * T, (TILES - 1) * 2 * T + n), :]
                        d = bass.AP(tensor=d.tensor, offset=d.offset,
                                    ap=[[DM, n], [2 * T * DM, TILES], [1, DM]])
                        sp.dma_start(d, buf[q * GRID + 3:q * GRID + 3 + n, :, :]).then_inc(st_x1, 16)

            def store_lg(o, n):
                sp.wait_ge(lg_ready, o + 1)
                for q in range(2):
                    d = lg_d[bass.ds(WIN * o + q * T, (TILES - 1) * 2 * T + n), :]
                    d = bass.AP(tensor=d.tensor, offset=d.offset,
                                ap=[[E, n], [2 * T * E, TILES], [1, E]])
                    sp.dma_start(d, lgb[q * GRID + 3:q * GRID + 3 + n, :, :]).then_inc(st_lg, 16)

            store_xx(0)
            sp.wait_ge(xT_done, 1)
            load_x_direct(WIN - 3, GRID, 0)
            sp.wait_ge(b0_ready, 1)
            sp.dma_start(b0_d, b0s[32:32 + NST, :]).then_inc(st_b0, 16)
            sp.wait_ge(st_b0, 16)
            sp.dma_start(b0b[:].rearrange("p n b -> p (n b)"),
                         b0_d.rearrange("(o n) b -> o (n b)", o=1).to_broadcast([P, NST * B])).then_inc(ld_b0, 16)
            store_b(0)
            for s in range(RING):
                spread_b(0, s)
            store_xx(1)
            sp.wait_ge(st_pad, 32)
            load_x(2)

            def iteration(w, prep, ln, out_, nseg):
                for s in range(nseg):
                    if s == 0 and out_:
                        load_xx(w - 1)
                    if s == 1 and out_ == 2:
                        store_lg(w - 2, WIN)
                    if s == 3 and prep:
                        store_b(w + 1)
                    if s == 4 and ln:
                        store_xx(w + 2)
                    if s == 4 and ln == 2:
                        load_x(w + 3)
                    if s + RING < nseg:
                        spread_b(w, s + RING)
                    elif prep:
                        spread_b(w + 1, s + RING - SPW)
                    if s == nseg - 1 and out_:
                        store_out(w - 1, WIN)

            iteration(0, True, 2, 0, SPW)
            iteration(1, True, 2, 1, SPW)
            with sp.Fori(2, NWIN - 3) as w:
                iteration(w, True, 2, 2, SPW)
            iteration(NWIN - 3, True, 1, 2, SPW)
            iteration(NWIN - 2, True, 0, 2, SPW)
            iteration(NWIN - 1, False, 0, 2, LAST_SEGS)
            load_xx(NWIN - 1)
            store_lg(NWIN - 2, WIN)
            store_out(NWIN - 1, T - WIN * (NWIN - 1))
            store_lg(NWIN - 1, T - WIN * (NWIN - 1))
            sp.wait_ge(st_x1, 64 * NWIN)
            sp.wait_ge(st_lg, 32 * NWIN)
            sp.wait_ge(st_zero, 16)
            sp_tail(sp)

        @block.gpsimd
        def _(pool):
            pool.memset(ident[:], 0.0).then_inc(const_pool, 1)
            pool.memset(sel[:], 0.0).then_inc(const_pool, 1)
            pool.wait_ge(const_pool, 2)
            pool.affine_select(out=ident[:], in_=ident[:], compare_op=ALU.not_equal, fill=1.0, base=0,
                               pattern=[[-1, P]], channel_multiplier=1).then_inc(const_pool, 1)
            for k, off in enumerate((0, 64, 96)):
                pool.affine_select(out=sel[:], in_=sel[:], compare_op=ALU.not_equal, fill=1.0, base=-off,
                                   pattern=[[-1, NST], [0, P]], channel_multiplier=1).then_inc(const_pool, 1)
                pool.wait_ge(const_pool, 4 + k)
            pool.memset(tri[:], 1.0).then_inc(const_pool, 1)
            pool.wait_ge(const_pool, 7)
            pool.affine_select(out=tri[:], in_=tri[:], compare_op=ALU.is_gt, fill=0.0, base=0,
                               pattern=[[1, P]], channel_multiplier=-1).then_inc(const_pool, 1)
            pool.iota(iota_i[:], [[1, E]], base=-E, channel_multiplier=0).then_inc(const_pool, 1)

            LNK = 8

            def ln_pool(v):
                pool.wait_ge(ln_stat, v + 1)
                n = [0]

                def step(ins):
                    n[0] += 1
                    ins.then_inc(ln_small, 1)
                    pool.wait_ge(ln_small, LNK * v + n[0])

                rstd, q, q2, q3, r2, r12, a1 = (lnp[:, k, :] for k in range(7))
                step(pool.tensor_tensor(rstd, ve[:], neghalf_e[:], ALU.pow))
                step(pool.tensor_tensor(q, rstd, rstd, ALU.mult))
                step(pool.tensor_tensor(q2, q, mv[:, :, 1], ALU.mult))
                step(pool.tensor_tensor(q3, q2, eps_rms[:], ALU.add))
                step(pool.tensor_tensor(r2, q3, neghalf_e[:], ALU.pow))
                step(pool.tensor_tensor(r12, rstd, r2, ALU.mult))
                step(pool.tensor_tensor(a1, rstd, ones4[:], ALU.add))
                step(pool.tensor_tensor(q, mv[:, :, 0], rstd, ALU.mult))

            def make_u(v):
                pool.wait_ge(dt_step, 2 * (v + 1))
                pool.wait_ge(xc_ready, v + 1)
                at_least(pool, bm_done, 2 * SPW * v)
                pool.tensor_tensor(u[:], dtb[:], xc[:], ALU.mult).then_inc(u_done, 1)

            def cap_e(v):
                for hf in range(H):
                    pool.wait_ge(dt_read, 2 * v + hf + 1)
                    pool.tensor_tensor(padp[:, hf:hf + 1], half_e[:], guard8[:], ALU.add)
                    pool.tensor_scalar(dtb[:, hf, :], dtb[:, hf, :], E_MAX, None, ALU.min).then_inc(e_capped, 1)

            def products(w, s, hf):
                S = SPW * w + s
                pool.wait_ge(u_done, w + 1)
                pool.wait_ge(ld_bb[s % RING], 16 * (SPW // RING * w + s // RING + 1))
                at_least(pool, y_done, S - RING + 1)
                us = cols(u, hf)[:, :, SEG * s + 1:SEG * s + 1 + SEG]
                hr = rows(h, s % RING)
                for k in range(4):
                    n0, nn = k * NST // 4, NST // 4
                    o = hr[:, hf * RH + n0 * B:hf * RH + (n0 + nn) * B, 1:SLOT]
                    ins = pool.tensor_tensor(
                        o.rearrange("p (n b) t -> p n b t", b=B),
                        us.unsqueeze(1).to_broadcast([P, nn, B, SEG]),
                        bb[:, s % RING, n0 * BS:(n0 + nn) * BS].rearrange("p (n b t) -> p n b t", b=B, t=SEG),
                        ALU.mult)
                ins.then_inc(bm_done, 1)

            def root(k):
                pool.wait_ge(s8_ready, k + 1)
                pool.tensor_tensor(nrm8[:], s8[:], half_e[:], ALU.pow).then_inc(pow_done, 1)
                pool.wait_ge(pow_done, k + 1)
                pool.tensor_tensor(nrt8[:], nrm8[:], guard8[:], ALU.add).then_inc(nrt_done, 1)

            def out_pool(o):
                pool.wait_ge(st2_done, o + 1)
                pool.tensor_tensor(rstd2[:], ve2[:], neghalf_e[:], ALU.pow).then_inc(rstd2_done, 1)

            pool.wait_ge(const_dve, 7)
            ln_pool(0)
            ln_pool(1)
            cap_e(0)
            make_u(0)
            pool.wait_ge(u_done, 1)
            pool.wait_ge(ld_b0, 16)
            for hf in range(H):
                pool.tensor_tensor(sqb[:, hf * RH:(hf + 1) * RH].rearrange("p (n b) -> p n b", b=B),
                                   cols(u, hf)[:, :, 0].unsqueeze(1).to_broadcast([P, NST, B]),
                                   b0b[:], ALU.mult).then_inc(pre_done, 1)
            root(0)
            products(0, 0, 0)
            products(0, 0, 1)
            products(0, 1, 0)

            def iteration(w, prep, ln, out_, nseg):
                for s in range(nseg):
                    S = SPW * w + s
                    if s + 1 < nseg:
                        products(w, s + 1, 1)
                    elif prep:
                        products(w + 1, 0, 1)
                    if prep or s + 1 < nseg:
                        root(S + 1)
                    if s == 1 and prep:
                        cap_e(w + 1)
                    if s == 2 and ln:
                        ln_pool(w + 2)
                    if s == 2 and out_:
                        out_pool(w - 1)
                    if s == 4 and prep:
                        make_u(w + 1)
                    if s + 2 < nseg:
                        products(w, s + 2, 0)
                    elif prep:
                        products(w + 1, s + 2 - SPW, 0)

            iteration(0, True, 1, 0, SPW)
            with pool.Fori(1, NWIN - 2) as w:
                iteration(w, True, 1, 1, SPW)
            iteration(NWIN - 2, True, 0, 1, SPW)
            iteration(NWIN - 1, False, 0, 1, LAST_SEGS)
            out_pool(NWIN - 1)
            pool_tail(pool)

        @block.scalar
        def _(act):
            act.wait_ge(ld_w, 16 * N_WLOAD)
            act.activation(asc[:], asc[:], ACT.Tanh, scale=0.1).then_inc(asc_s, 1)
            act.wait_ge(asc_s, 1)
            act.activation(asc[:], asc[:], ACT.Exp, scale=10.0).then_inc(asc_s, 1)
            act.wait_ge(asc_s, 2)
            act.mul(asc[:], asc[:], -1.0 / 16.0).then_inc(asc_s, 1)
            act.activation(rs[:], rs[:], ACT.Tanh, scale=0.5).then_inc(rs_s, 1)
            act.mul(cbh[:], cbh[:], 0.5).then_inc(asc_s, 1)
            act.wait_ge(asc_s, 4)

            def evac_xT(v):
                act.wait_ge(xT_done, v + 1)
                at_least(act, g_done, 2 * v)
                act.copy(xnT[:].rearrange("p b t -> p (b t)"), bank(B_XT)).then_inc(xnT_ready, 1)

            def decay(w, s):
                S = SPW * w + s
                act.wait_ge(tanh_done, w + 1)
                at_least(act, scan_done, S - RING + 1)
                act.activation(rows(dA, s % RING)[:, :, 1:SLOT], zall[:, :, SEG * s:SEG * (s + 1)],
                               ACT.Exp, scale=16.0).then_inc(exp_done, 1)

            def take_over(w):
                act.wait_ge(sg_made, 2 * (w + 1))
                at_least(act, yg_done, SPW * w)
                act.copy(sgc[:], sgn[:]).then_inc(sg_ready, 1)

            def scale_x(w):
                act.wait_ge(xc_ready, w + 1)
                at_least(act, y_done, SPW * w)
                for hf in range(H):
                    act.activation(dxc[:, hf, :], xc[:, hf, :], ACT.Copy, scale=dpar[:, hf:hf + 1]).then_inc(dxc_ready, 1)

            def silu_x(v):
                at_least(act, u_done, v)
                at_least(act, bc_done, v)
                at_least(act, dxc_ready, 2 * v)
                at_least(act, xc_ready, v)
                for hf in range(H):
                    act.wait_ge(xh_done, 2 * v + hf + 1)
                    act.activation(thx[:, hf, :], bankc(B_XH[hf]), ACT.Tanh, bias=cbh[:, hf:hf + 1])
                    act.activation(xc[:, hf, :], bankc(B_XH[hf]), ACT.Identity, bias=cbh[:, hf:hf + 1]).then_inc(x_read, 1)

            def tanh_gate(v, hf):
                act.wait_ge(g_done, 2 * v + hf + 1)
                if hf == 0:
                    at_least(act, sg_ready, v)
                act.activation(sgn[:, hf, :], bankc(B_G[hf]), ACT.Tanh).then_inc(tg_done, 1)

            def exp_dt(v, hf):
                if hf == 0:
                    at_least(act, u_done, v)
                act.wait_ge(dt_done, 2 * v + hf + 1)
                act.activation(dtb[:, hf, :], bankc(B_DT[hf]), ACT.Exp, bias=bdt[:, hf:hf + 1]).then_inc(dt_read, 1)

            def evac_bc(v):
                act.wait_ge(bc_done, v + 1)
                at_least(act, st_b, 16 * v)
                act.copy(bsb[32:32 + NST].rearrange("p s b t -> p b s t"),
                         ps[32:32 + NST, B_BC, 0:B * COLS].rearrange("p (b c) -> p b c", b=B)[:, :, 1:COLS]
                         .rearrange("p b (s t) -> p b s t", t=SEG)).then_inc(bsb_ready, 1)
                at_least(act, cs_step, 5 * v)
                act.copy(cs_next[:], bankc(B_BC)).then_inc(bc_read, 1)
                act.copy(bcraw[:], bankc(B_BC)).then_inc(bc_read, 1)
                if isinstance(v, int) and v == 0:
                    act.copy(b0s[32:32 + NST, :],
                             ps[32:32 + NST, B_BC, 0:B * COLS].rearrange("p (b c) -> p b c", b=B)[:, :, 0]).then_inc(b0_ready, 1)

            def clamp_dt(v):
                act.wait_ge(e_capped, 2 * (v + 1))
                act.activation(dtb[:], dtb[:], ACT.Ln, bias=1.0).then_inc(ln_step, 1)
                act.wait_ge(ln_step, v + 1)
                act.activation(dtb[:], dtb[:], ACT.Tanh, scale=0.5 / 0.0495, bias=spb[:, 0:1]).then_inc(dt_step, 1)
                act.wait_ge(dt_step, 2 * v + 1)
                act.activation(dtb[:], dtb[:], ACT.Copy, scale=0.0495 / 0.5, bias=0.0505).then_inc(dt_step, 1)
                act.wait_ge(dt_step, 2 * (v + 1))

            def evac_h2T(o):
                act.wait_ge(h2T_done, o + 1)
                at_least(act, lg_done, o)
                act.copy(h2T[:].rearrange("p i m -> p (i m)"), bank(B_H2)).then_inc(h2T_ready, 1)

            def decay_tanh(v, between):
                at_least(act, exp_done, SPW * v)
                for hf in range(H):
                    for n in range(NST):
                        if hf * NST + n in between:
                            between[hf * NST + n]()
                        ins = act.activation(zrow[:, hf * NST + n], cols(dtb, hf)[:, :, 1:COLS], ACT.Tanh,
                                             scale=asc[:, hf, n:n + 1])
                ins.then_inc(tanh_done, 1)

            evac_xT(0)
            silu_x(0)
            for hf in range(H):
                exp_dt(0, hf)
            evac_bc(0)
            clamp_dt(0)
            act.wait_ge(wtr_done, 5)
            decay_tanh(0, {2: lambda: tanh_gate(0, 0), 4: lambda: tanh_gate(0, 1), 8: lambda: evac_xT(1)})

            def iteration(w, prep, ln, out_, nseg):
                for s in range(3):
                    decay(w, s)
                scale_x(w)
                if prep:
                    silu_x(w + 1)
                take_over(w)
                decay(w, 3)
                if not prep:
                    evac_h2T(w - 1)
                    return
                for hf in range(H):
                    exp_dt(w + 1, hf)
                decay(w, 4)
                clamp_dt(w + 1)
                decay(w, 5)
                between = {BC_ROW: lambda: evac_bc(w + 1), G_ROWS[0]: lambda: tanh_gate(w + 1, 0),
                           G_ROWS[1]: lambda: tanh_gate(w + 1, 1)}
                if ln:
                    between[XT_ROW] = lambda: evac_xT(w + 2)
                if out_:
                    between[H2_ROW] = lambda: evac_h2T(w - 1)
                decay_tanh(w + 1, between)

            BC_ROW, G_ROWS, XT_ROW, H2_ROW = 0, (3, 6), 14, 24
            iteration(0, True, True, False, SPW)
            iteration(1, True, True, True, SPW)
            with act.Fori(2, NWIN - 2) as w:
                iteration(w, True, True, True, SPW)
            iteration(NWIN - 2, True, False, True, SPW)
            iteration(NWIN - 1, False, False, True, LAST_SEGS)
            evac_h2T(NWIN - 1)
            act_tail(act)

        @block.vector
        def _(dve):
            dve.memset(xt[:], 0.0).then_inc(const_dve, 1)
            dve.memset(bound_w[:], 1.0 / MAX_NORM ** 2).then_inc(const_dve, 1)
            dve.memset(ones_r[:], 1.0)
            dve.memset(zeros[:], 0.0).then_inc(const_dve, 1)
            dve.memset(half_e[:], 0.5).then_inc(const_dve, 1)
            dve.memset(neghalf_e[:], -0.5).then_inc(const_dve, 1)
            dve.memset(eps_rms[:], 1e-6)
            dve.memset(ones4[:], 1.0)
            dve.memset(guard8[:], 1e-8 / MAX_NORM)
            dve.memset(spb[:], -0.0505 * 0.5 / 0.0495)
            dve.memset(z[:, 14 * P:16 * P], 0.0).then_inc(const_dve, 1)
            dve.memset(yg[:], 0.0)
            for r in range(RING):
                ins = dve.memset(rows(dA, r)[:, :, 0], 0.0)
            ins.then_inc(const_dve, 1)

            def ln_stats(v, src, b6, m2, e1, ready, count, step, done):
                dve.wait_ge(ready, count)
                for i in range(TILES):
                    ins = dve.bn_stats(b6[:, i, :], src[:, i, :])
                ins.then_inc(step, 1)
                dve.wait_ge(step, 2 * v + 1)
                dve.memset(pad[:], 0.0)
                for i in range(TILES):
                    ins = dve.bn_aggr(m2[:, i, :], b6[:, i, :])
                ins.then_inc(step, 1)
                dve.wait_ge(step, 2 * (v + 1))
                dve.tensor_scalar(e1[:], m2[:, :, 1], 1e-5, None, ALU.add).then_inc(done, 1)

            def ln_in(v):
                ln_stats(v, xt, bst, mv, ve, ld_x, 32 * (v + 1), stat_step, ln_stat)

            def ln_apply(v):
                dve.wait_ge(ln_small, 8 * (v + 1))
                at_least(dve, st_xx, 16 * v)
                for i in range(TILES):
                    dve.tensor_scalar(xx[:, i, :], xt[:, i, :], lnp[:, 6, i:i + 1], lnp[:, 1, i:i + 1],
                                      ALU.mult, ALU.subtract)
                for i in range(TILES):
                    ins = dve.tensor_scalar(xt[:, i, :], xt[:, i, :], mv[:, i, 0:1], lnp[:, 5, i:i + 1],
                                            ALU.subtract, ALU.mult)
                ins.then_inc(xn_ready, 1)

            def make_xc(v):
                for hf in range(H):
                    dve.wait_ge(x_read, 2 * v + hf + 1)
                    ins = dve.scalar_tensor_tensor(out=xc[:, hf, :], in0=thx[:, hf, :], scalar=1.0,
                                                   in1=xc[:, hf, :], op0=ALU.add, op1=ALU.mult)
                ins.then_inc(xc_ready, 1)

            def make_gate(v, hf):
                dve.wait_ge(tg_done, 2 * v + hf + 1)
                dve.scalar_tensor_tensor(out=sgn[:, hf, :], in0=sgn[:, hf, :], scalar=1.0,
                                         in1=bankc(B_G[hf]), op0=ALU.add, op1=ALU.mult).then_inc(sg_made, 1)

            def split_c(v):
                dve.wait_ge(bc_read, 2 * (v + 1))
                n = [0]

                def step(ins):
                    n[0] += 1
                    ins.then_inc(cs_step, 1)
                    dve.wait_ge(cs_step, 5 * v + n[0])

                step(dve.tensor_tensor(bcraw[64:P], bcraw[64:P], cs_next[64:P], ALU.subtract))
                step(dve.tensor_copy(cs_next[64:P], bcraw[64:P]))
                step(dve.tensor_tensor(bcraw[96:P], bcraw[96:P], cs_next[96:P], ALU.subtract))
                step(dve.tensor_copy(cs_next[96:P], bcraw[96:P]))

            def take_c(v):
                at_least(dve, cb_done, 3 * SPW * v)
                dve.tensor_copy(cs[:], cs_next[:]).then_inc(cs_step, 1)

            def sum_squares(k):
                dve.wait_ge(sq_done, k + 1)
                dve.tensor_reduce(s_p[:], sqb[:].rearrange("p (r b) -> p b r", b=B), AX_X,
                                  ALU.add).then_inc(red_done, 1)

            def take_norm(k):
                dve.wait_ge(nrm_done, k + 1)
                dve.tensor_copy(s8[:], ps[0:B, NB, 0:1]).then_inc(s8_ready, 1)

            def factor(k):
                dve.wait_ge(nrt_done, k + 1)
                dve.reciprocal(fac8[:], nrt8[:]).then_inc(rec_done, 1)
                dve.wait_ge(rec_done, k + 1)
                dve.tensor_scalar(fac_d[:], ident[0:B, 0:B], fac8[:, 0:1], None, ALU.mult).then_inc(fac_made, 1)

            def restart(k, last, S_next, s_next):
                dve.wait_ge(fac_done, k + 1)
                at_least(dve, y_done, S_next - RING + 1)
                dve.scalar_tensor_tensor(
                    out=rows(h, s_next % RING)[:, :, 0].rearrange("p (r b) -> p r b", b=B),
                    in0=ps[:, NB, 0:B].unsqueeze(1).to_broadcast([P, H * NST, B]), scalar=1.0,
                    in1=last.rearrange("p (r b) -> p r b", b=B), op0=ALU.min, op1=ALU.mult).then_inc(h0_ready, 1)

            def gate_y(w, s):
                S = SPW * w + s
                dve.wait_ge(y_done, S + 1)
                dve.wait_ge(sg_ready, w + 1)
                if s == 0:
                    at_least(dve, op_done, w)
                dve.tensor_tensor(
                    yg[:].rearrange("p h b t -> p (h b) t")[:, :, 3 + SEG * s:3 + SEG * (s + 1)],
                    ps[:, YB, 0:H * BS].rearrange("p (r t) -> p r t", t=SEG),
                    sgc[:].rearrange("p h (b c) -> p (h b) c", c=COLS)[:, :, SEG * s:SEG * (s + 1)],
                    ALU.mult).then_inc(yg_done, 1)

            def segment(w, s, last, early, extra):
                S = SPW * w + s
                dve.wait_ge(exp_done, S + 1)
                dve.wait_ge(bm_done, 2 * (S + 1))
                dve.wait_ge(h0_ready, S + 1)
                hs = h[:, s % RING, :]
                dve.tensor_tensor_scan(hs, dA[:, s % RING, :], hs, 0.0, ALU.mult, ALU.add).then_inc(scan_done, 1)
                dve.wait_ge(scan_done, S + 1)
                hr = rows(h, s % RING)
                hl = hr[:, :, SEG]
                if not last:
                    dve.tensor_tensor(sqb[:], hl, hl, ALU.mult).then_inc(sq_done, 1)
                if s > 0:
                    gate_y(w, s - 1)
                elif not (isinstance(w, int) and w == 0):
                    gate_y(w - 1, SPW - 1)
                if not last:
                    sum_squares(S + 1)
                early()
                h4 = hr.rearrange("p (f r) t -> p f r t", f=H)
                for j, (n0, n1) in enumerate(NCH):
                    dve.wait_ge(cb_done, 3 * S + j + 1)
                    m = h4[:, :, n0 * B:n1 * B, 0:SEG]
                    dve.tensor_tensor(m, m, ps[:, j, 0:(n1 - n0) * BS].rearrange("p (r t) -> p r t", t=SEG)
                                      .unsqueeze(1).to_broadcast([P, H, (n1 - n0) * B, SEG]),
                                      ALU.mult).then_inc(cm_done, 1)
                    if j == 0 and not last:
                        take_norm(S + 1)
                    if j == 1 and not last:
                        factor(S + 1)
                extra()
                if not last:
                    restart(S + 1, hl, S + 1, s + 1)

            def add_out(o):
                dve.wait_ge(op_done, o + 1)
                dve.wait_ge(ld_xx, 16 * (o + 1))
                dve.scalar_tensor_tensor(out=xxr[:].rearrange("p i m -> p (i m)"), in0=bank(B_OUT), scalar=rs[:, 0:1],
                                         in1=xxr[:].rearrange("p i m -> p (i m)"), op0=ALU.mult,
                                         op1=ALU.add).then_inc(x1_done, 1)

            def out_stats(o):
                ln_stats(o, xxr, bst2, mv2, ve2, x1_done, o + 1, stat2_step, st2_done)

            def make_h2(o):
                dve.wait_ge(rstd2_done, o + 1)
                at_least(dve, st_x1, 64 * o)
                at_least(dve, h2T_done, o)
                for i in range(TILES):
                    ins = dve.tensor_scalar(h2b[:, i, :], xxr[:, i, :], mv2[:, i, 0:1], rstd2[:, i:i + 1],
                                            ALU.subtract, ALU.mult)
                ins.then_inc(h2_ready, 1)

            def evac_lg(o):
                dve.wait_ge(lg_done, o + 1)
                at_least(dve, st_lg, 32 * o)
                dve.tensor_copy(lgb[:].rearrange("p i e -> p (i e)"), ps[:, B_LG, 0:TILES * E]).then_inc(lg_ready, 1)

            dve.wait_ge(const_pool, 9)
            dve.tensor_copy(iom[:], iota_i[:]).then_inc(iom_s, 1)
            dve.wait_ge(ld_w, 16 * N_WLOAD)
            for hf in range(H):
                for k in range(TAPS):
                    dve.tensor_scalar(nat[:, hf * TAPS + k, :], win_n[:, hf, :], conv_c[:, hf, k:k + 1], 0.5,
                                      ALU.mult, ALU.mult)
            dve.tensor_scalar(nat[:, 8:10, :], win_n[:, 2:4, :], 0.5, None, ALU.mult).then_inc(taps_ready, 1)
            ln_in(0)
            dve.wait_ge(wtr_done, 5)
            dve.tensor_scalar(wT[:, 0:8, :].rearrange("p (k c) m -> p k (c m)", k=2), ps[:, 0:2, :], nw[:, 0:1], None, ALU.mult)
            dve.tensor_scalar(wT[:, 8:10, :], ps[:, 2, 0:2 * P].rearrange("p (k c) -> p k c", c=P), nw[:, 0:1], None, ALU.mult)
            dve.tensor_copy(wT[:, 10:12, :], ps[:, 2, 2 * P:4 * P].rearrange("p (k c) -> p k c", c=P))
            dve.tensor_copy(wT[:, 12:16, :].rearrange("p k c -> p (k c)"), ps[:, 3, :])
            dve.tensor_copy(wT[:, 16:18, :].rearrange("p k c -> p (k c)"), ps[:, 4, 0:2 * P]).then_inc(w_ready, 1)
            dve.wait_ge(rs_s, 1)
            dve.tensor_scalar(rs[:], rs[:], 0.25, 0.25, ALU.mult, ALU.add).then_inc(rs_s, 1)
            ln_apply(0)
            ln_in(1)
            make_xc(0)
            split_c(0)
            take_c(0)
            for hf in range(H):
                make_gate(0, hf)
            ln_apply(1)
            dve.wait_ge(pre_done, 2)
            dve.tensor_copy(rows(h, 2)[:, :, 1], sqb[:]).then_inc(pre_done, 1)
            dve.wait_ge(pre_done, 3)
            h_first = rows(h, 2)[:, :, 1]
            dve.tensor_tensor(sqb[:], h_first, h_first, ALU.mult).then_inc(sq_done, 1)
            sum_squares(0)
            take_norm(0)
            factor(0)
            restart(0, h_first, 0, 0)

            def iteration(w, prep, ln, out_, nseg):
                def early(s):
                    if s == 1 and ln:
                        ln_in(w + 2)
                    if s == 2 and out_:
                        out_stats(w - 1)
                    if s == 3 and ln:
                        ln_apply(w + 2)
                    if s == 4 and prep:
                        make_gate(w + 1, 1)
                    if s == 5:
                        take_c(w + 1)

                def late(s):
                    if s == 0:
                        if out_ == 2:
                            evac_lg(w - 2)
                        if prep:
                            make_xc(w + 1)
                    if s == 1 and out_:
                        add_out(w - 1)
                    if s == 3:
                        if prep:
                            make_gate(w + 1, 0)
                        if out_:
                            make_h2(w - 1)
                    if s == 4 and prep:
                        split_c(w + 1)

                for s in range(nseg):
                    segment(w, s, (not prep) and s == nseg - 1, lambda s=s: early(s), lambda s=s: late(s))

            iteration(0, True, 1, 0, SPW)
            iteration(1, True, 1, 1, SPW)
            iteration(2, True, 1, 2, SPW)
            with dve.Fori(3, NWIN - 2) as w:
                iteration(w, True, 1, 2, SPW)
            iteration(NWIN - 2, True, 0, 2, SPW)
            iteration(NWIN - 1, False, 0, 2, LAST_SEGS)
            gate_y(NWIN - 1, LAST_SEGS - 1)
            evac_lg(NWIN - 2)
            add_out(NWIN - 1)
            out_stats(NWIN - 1)
            make_h2(NWIN - 1)
            evac_lg(NWIN - 1)
            dve_tail(dve)

        @block.tensor
        def _(pe):
            pe.wait_ge(const_pool, 3)
            pe.wait_ge(taps_ready, 1)
            pe.wait_ge(ld_w, 16 * N_WLOAD)
            pe.wait_ge(ld_bc, 64)
            for g in range(5):
                for k in range(4 * g, min(4 * g + 4, 18)):
                    ins = pe.transpose(ps[:, g, (k % 4) * P:(k % 4 + 1) * P], nat[:, k, :], ident[:])
                ins.then_inc(wtr_done, 1)

            def turn_x(v):
                pe.wait_ge(xn_ready, v + 1)
                at_least(pe, bc_read, 2 * v)
                at_least(pe, bsb_ready, v)
                if isinstance(v, int) and v == 1:
                    pe.wait_ge(b0_ready, 1)
                for i in range(TILES):
                    ins = pe.transpose(ps[:, B_XT, i * P:(i + 1) * P], xt[:, i, :], ident[:])
                ins.then_inc(xT_done, 1)

            def project_x(v, hf, k0=0, k1=TAPS):
                if k0 == 0:
                    if hf == 0:
                        pe.wait_ge(xnT_ready, v + 1)
                    at_least(pe, sg_made, 2 * (v - 1) + hf + 1)
                for k in range(k0, k1):
                    ins = pe.matmul(bankc(B_XH[hf]), wT[:, hf * TAPS + k, :], xnT[:, :, k:k + COLS],
                                    start=(k == 0), stop=(k == TAPS - 1))
                if k1 == TAPS:
                    ins.then_inc(xh_done, 1)

            def project_gate(v, hf):
                pe.wait_ge(dt_read, 2 * v + hf + 1)
                pe.matmul(bankc(B_G[hf]), wT[:, 8 + hf, :], xnT[:, :, 3:GRID],
                          start=True, stop=True).then_inc(g_done, 1)

            def project_dt(v, hf):
                pe.wait_ge(xc_ready, v + 1)
                for ih in range(H):
                    ins = pe.matmul(bankc(B_DT[hf]), wT[:, 10 + hf * H + ih, :], xc[:, ih, :],
                                    start=(ih == 0), stop=(ih == H - 1))
                ins.then_inc(dt_done, 1)

            def project_bc(v):
                at_least(pe, x1_done, v - 1)
                for ih in range(H):
                    ins = pe.matmul(bankc(B_BC), wT[:, 14 + ih, :], xc[:, ih, :], start=(ih == 0), stop=(ih == H - 1))
                ins.then_inc(bc_done, 1)

            def project_out(o):
                pe.wait_ge(yg_done, NSEG if last_window(o) else SPW * (o + 1))
                at_least(pe, lg_ready, o)
                if isinstance(o, int) and o == 0:
                    pe.wait_ge(xnT_ready, 3)
                for i in range(TILES):
                    for hf in range(H):
                        ins = pe.matmul(ps[:, B_OUT, i * P:(i + 1) * P],
                                        yg[:, hf].rearrange("p b t -> p (b t)")[:, i * P:(i + 1) * P],
                                        wT[:, 16 + hf, :], start=(hf == 0), stop=(hf == H - 1))
                ins.then_inc(op_done, 1)

            def last_window(o):
                return isinstance(o, int) and o == NWIN - 1

            def turn_h2(o, used):
                pe.wait_ge(h2_ready, o + 1)
                if used is not None:
                    pe.wait_ge(*used)
                for i in range(TILES):
                    ins = pe.transpose(ps[:, B_H2, i * P:(i + 1) * P], h2b[:, i, :], ident[:])
                ins.then_inc(h2T_done, 1)

            def route(o):
                pe.wait_ge(h2T_ready, o + 1)
                for i in range(TILES):
                    ins = pe.matmul(ps[:, B_LG, i * E:(i + 1) * E], h2T[:, i, :], wg_s[:], start=True, stop=True)
                ins.then_inc(lg_done, 1)

            def norm_sum(k):
                pe.wait_ge(red_done, k + 1)
                at_least(pe, h0_ready, k)
                pe.matmul(ps[0:B, NB, 0:1], s_p[:], bound_w[:], start=True, stop=True).then_inc(nrm_done, 1)

            def norm_spread(k):
                pe.wait_ge(fac_made, k + 1)
                pe.matmul(ps[:, NB, 0:B], ones_r[:], fac_d[:], start=True, stop=True).then_inc(fac_done, 1)

            def spread_c(w, s, j):
                S = SPW * w + s
                at_least(pe, cm_done, 3 * (S - 1) + j + 1)
                pe.wait_ge(cs_step, 5 * (w + 1))
                n0, n1 = NCH[j]
                for n in range(n0, n1):
                    ins = pe.matmul(ps[:, j, (n - n0) * BS:(n - n0 + 1) * BS], sel[:, n, :],
                                    cs[:].rearrange("p (b c) -> p b c", b=B)[:, :, SEG * s:SEG * (s + 1)],
                                    start=True, stop=True)
                ins.then_inc(cb_done, 1)

            def sum_states(w, s, j):
                S = SPW * w + s
                pe.wait_ge(cm_done, 3 * S + j + 1)
                if j == 0:
                    at_least(pe, yg_done, S)
                hr = rows(h, s % RING).rearrange("p (f r) t -> p f r t", f=H)
                n0, n1 = NCH[j]
                for n in range(n0, n1):
                    pe.matmul(ps[:, YB, 0:H * BS], ident[:], hr[:, :, n * B:(n + 1) * B, 0:SEG],
                              start=(n == 0), stop=False)

            def add_dx(w, s):
                pe.wait_ge(dxc_ready, 2 * (w + 1))
                pe.matmul(ps[:, YB, 0:H * BS], ident[:],
                          dxc[:].rearrange("p h (b c) -> p (h b) c", c=COLS)[:, :, SEG * s:SEG * (s + 1)],
                          start=False, stop=True).then_inc(y_done, 1)

            pe.wait_ge(w_ready, 1)
            pe.wait_ge(const_dve, 7)
            turn_x(0)
            pe.wait_ge(asc_s, 4)
            for hf in range(H):
                project_x(0, hf)
            for hf in range(H):
                project_dt(0, hf)
            project_bc(0)
            for hf in range(H):
                project_gate(0, hf)
            pe.wait_ge(const_pool, 6)
            for j in range(3):
                spread_c(0, 0, j)
            turn_x(1)
            norm_sum(0)
            norm_spread(0)
            for hf in range(H):
                project_x(1, hf)

            def iteration(w, prep, ln, out_, nseg):
                def first(s):
                    if s == 1 and prep:
                        project_dt(w + 1, 1)
                    if s == 2 and prep:
                        project_gate(w + 1, 0)
                    if s == 3 and ln:
                        turn_x(w + 2)
                    if s == 4:
                        if ln:
                            project_x(w + 2, 0, 2, 3)
                        if out_:
                            turn_h2(w - 1, (xnT_ready, w + 3) if ln else (bc_read, 2 * (w + 2)))
                    if s == 5:
                        if ln:
                            project_x(w + 2, 1, 1, 2)
                        if out_:
                            route(w - 1)

                def last_(s):
                    if s == 0:
                        if out_:
                            project_out(w - 1)
                        if prep:
                            project_dt(w + 1, 0)
                    if s == 1 and prep:
                        project_bc(w + 1)
                    if s == 2 and prep:
                        project_gate(w + 1, 1)
                    if ln:
                        if s == 3:
                            project_x(w + 2, 0, 0, 2)
                        if s == 4:
                            project_x(w + 2, 0, 3, 4)
                            project_x(w + 2, 1, 0, 1)
                        if s == 5:
                            project_x(w + 2, 1, 2, 4)
                    if s == 3 and not prep:
                        turn_h2(w - 1, None)

                for s in range(nseg):
                    S = SPW * w + s
                    last = (not prep) and s == nseg - 1
                    if not last:
                        norm_sum(S + 1)
                    first(s)
                    for j in range(3):
                        if s + 1 < nseg:
                            spread_c(w, s + 1, j)
                        elif prep:
                            spread_c(w + 1, 0, j)
                        sum_states(w, s, j)
                        if j == 0 and not last:
                            norm_spread(S + 1)
                    add_dx(w, s)
                    last_(s)

            iteration(0, True, 1, 0, SPW)
            iteration(1, True, 1, 1, SPW)
            with pe.Fori(2, NWIN - 2) as w:
                iteration(w, True, 1, 1, SPW)
            iteration(NWIN - 2, True, 0, 1, SPW)
            iteration(NWIN - 1, False, 0, 1, LAST_SEGS)
            route(NWIN - 2)
            project_out(NWIN - 1)
            turn_h2(NWIN - 1, None)
            route(NWIN - 1)
            pe_tail(pe)


_INS = ['L0_attn_x', 'L0_attn_norm_w', 'L0_attn_W_in', 'L0_attn_conv_w', 'L0_attn_conv_b', 'L0_attn_W_dt',
        'L0_attn_b_dt', 'L0_attn_W_B', 'L0_attn_W_C', 'L0_attn_A_log', 'L0_attn_D_param', 'L0_attn_W_out',
        'L0_attn_residual_scale', 'L0_ffn_Wg', 'L0_ffn_w1', 'L0_ffn_w2']


def kernel(**inputs):
    import numpy as _np
    import concourse.bacc as _bacc
    from concourse import mybir as _mybir
    from concourse.bass_utils import run_bass_kernel_spmd as _run

    nc = _bacc.Bacc("TRN2", target_bir_lowering=False, num_devices=1)
    arrays, args = {}, []
    for name in _INS:
        a = _np.ascontiguousarray(inputs[name])
        if a.ndim == 0:
            a = a.reshape(1)
        arrays[f"in_{name}_dram"] = a
        args.append(nc.dram_tensor(f"in_{name}_dram", a.shape, _mybir.dt.from_np(a.dtype), kind="ExternalInput").ap())
    shape = inputs['L0_attn_x'].shape
    args.append(nc.dram_tensor("out_0_dram", shape, _mybir.dt.float32, kind="ExternalOutput").ap())
    mamba_moe(nc, *args)
    r = _run(nc, [arrays], core_ids=[0])
    return r.results[0]["out_0_dram"]
```

```python
from contextlib import ExitStack

import concourse.bass as bass
from concourse import mybir

ALU = mybir.AluOpType
ACT = mybir.ActivationFunctionType
AX_X = mybir.AxisListType.X
F32 = mybir.dt.float32
BF16 = mybir.dt.bfloat16
I32 = mybir.dt.int32

P = 128
SEG = 10
SLOT = SEG + 1
SPW = 6
WIN = SPW * SEG
COLS = WIN + 1
TAPS = 4
GRID = WIN + TAPS
RING = 3
LNK = 10
NO_TOKEN = 65536.0
MAX_NORM = 20.0
E_MAX = 2.0 ** 57


def at_least(eng, sem, n):
    if isinstance(n, int) and n <= 0:
        return
    eng.wait_ge(sem, n)


def mamba_moe(nc, x, norm_w, W_in, conv_w, conv_b, W_dt, b_dt, W_B, W_C, A_log, D_param, W_out,
              residual_scale, Wg, w1, w2, out):
    B, T, DM = x.shape
    DI, NST = A_log.shape
    E, _, F = w1.shape
    H = DI // P
    RH = NST * B
    ROWS = H * RH
    NSEG = (T + SEG - 1) // SEG
    NWIN = (NSEG + SPW - 1) // SPW
    TILES = B * GRID // P
    TOK = B * T
    NT = TOK // P
    CAP = (TOK + E - 1) // E
    FC = F // P
    CT = CAP // P
    assert DM == P and TILES * P == 512 and CAP == 256 and NWIN == 9 and B * SEG * H == 160
    BS = B * SEG
    NCH = [(0, 6), (6, 12), (12, 16)]

    with ExitStack() as ctx:
        def sb(name, shape, dt=F32):
            return ctx.enter_context(nc.sbuf_tensor(name, shape, dt))

        def sem(name):
            return ctx.enter_context(nc.semaphore(name))

        def dram(name, shape):
            return nc.dram_tensor(name, shape, F32, kind="Internal").ap()

        xpad = dram("xpad", (TOK + GRID, DM))
        b_d = dram("b_d", (NWIN, SPW, NST, BS))
        b0_d = dram("b0_d", (NST, B))
        xx_d = dram("xx_d", (NWIN, P, TILES * DM))
        rows_d = dram("rows_d", (TOK, 2 * DM))
        lg_d = dram("lg_d", (TOK, E))
        outr = out.rearrange("b t d -> (b t) d")

        ident = sb("ident", [P, P])
        ones_r = sb("ones_r", [B, P])
        bound_w = sb("bound_w", [P, 1])
        sel = sb("sel", [P, NST, P], BF16)
        wT = sb("wT", [P, 18, P])
        conv_c = sb("conv_c", [P, H, TAPS])
        cbh = sb("cbh", [P, H])
        bdt = sb("bdt", [P, H])
        dpar = sb("dpar", [P, H])
        asc = sb("asc", [P, H, NST])
        nw = sb("nw", [P, 1])
        rs = sb("rs", [P, 1])
        wg_s = sb("wg_s", [P, E])
        half_e = sb("half_e", [B, 1])
        eps_rms = sb("eps_rms", [P, TILES])
        ones4 = sb("ones4", [P, TILES])
        minus4 = sb("minus4", [P, TILES])
        nmean2 = sb("nmean2", [P, TILES])
        nbias2 = sb("nbias2", [P, TILES])
        guard8 = sb("guard8", [B, 1])
        neghalf_e = sb("neghalf_e", [P, TILES])
        spb = sb("spb", [P, 1])
        pad = sb("pad", [P, 1])
        tri = sb("tri", [P, P])
        iota_i = sb("iota_i", [P, P], I32)

        z = sb("z", [P, H * NST * B * WIN])
        dA = sb("dA", [P, RING, ROWS * SLOT])
        h = sb("h", [P, RING, ROWS * SLOT])
        bb = sb("bb", [P, RING, NST * BS])
        sqb = sb("sqb", [P, ROWS])
        s_p = sb("s_p", [P, B])
        s8 = sb("s8", [B, 1])
        nrm8 = sb("nrm8", [B, 1])
        nrt8 = sb("nrt8", [B, 1])
        fac8 = sb("fac8", [B, 1])
        fac_d = sb("fac_d", [B, B])

        xt = sb("xt", [P, TILES, DM])
        xx = sb("xx", [P, TILES, DM])
        xxr = sb("xxr", [P, TILES, DM])
        xnT = sb("xnT", [P, B, GRID])
        bst = sb("bst", [P, TILES, 6])
        mv = sb("mv", [P, TILES, 2])
        ve = sb("ve", [P, TILES])
        lnp = sb("lnp", [P, 9, TILES])
        bst2 = sb("bst2", [P, TILES, 6])
        mv2 = sb("mv2", [P, TILES, 2])
        ve2 = sb("ve2", [P, TILES])
        rstd2 = sb("rstd2", [P, TILES])
        thx = sb("thx", [P, H, B * COLS])
        xc = sb("xc", [P, H, B * COLS])
        sgn = sb("sgn", [P, H, B * COLS])
        sgc = sb("sgc", [P, H, B * COLS])
        dtb = sb("dtb", [P, H, B * COLS])
        u = sb("u", [P, H, B * COLS])
        dxc = sb("dxc", [P, H, B * COLS])
        bcraw = sb("bcraw", [P, B * COLS])
        bsb = sb("bsb", [P, SPW, B, SEG])
        b0s = s_p
        b0b = sb("b0b", [P, NST, B])
        cs_next = sb("cs_next", [P, B * COLS], BF16)
        cs = sb("cs", [P, B * COLS], BF16)
        yg = sb("yg", [P, H, B, GRID])
        h2b = sb("h2b", [P, TILES, DM])
        h2T = sb("h2T", [P, TILES, P])
        lgb = sb("lgb", [P, TILES, E])

        ps = ctx.enter_context(nc.psum_tensor("ps", [P, 8, 512], F32))
        YB, NB, P0, P1, P2 = 3, 4, 5, 6, 7
        B_XH = B_G = B_DT = (P0, P2)
        B_XT = B_BC = B_H2 = B_OUT = B_LG = P1

        def out_bank(o):
            return P0 if isinstance(o, int) and o == NWIN - 1 else B_OUT

        def cols(t, hf):
            return t[:, hf, :].rearrange("p (b c) -> p b c", b=B)

        def rows(t, r):
            return t[:, r, :].rearrange("p (r c) -> p r c", c=SLOT)

        def bank(k):
            return ps[:, k, :]

        def bankc(k):
            return ps[:, k, 0:B * COLS]

        zrow = z[:].rearrange("p (r b t) -> p r b t", r=H * NST, b=B)
        zall = z[:].rearrange("p (r t) -> p r t", t=WIN)

        nat = z[:, 0:18 * P].rearrange("p (k c) -> p k c", c=P)
        win_n = z[:, 18 * P:22 * P].rearrange("p (k c) -> p k c", c=P)

        ld_w = sem("ld_w"); ld_bc = sem("ld_bc"); ld_x = sem("ld_x"); ld_xx = sem("ld_xx")
        ld_bb = [sem(f"ld_bb{r}") for r in range(RING)]; ld_b0 = sem("ld_b0")
        st_pad = sem("st_pad"); st_b = sem("st_b"); st_b0 = sem("st_b0"); st_xx = sem("st_xx")
        st_x1 = sem("st_x1"); st_lg = sem("st_lg")
        const_pool = sem("const_pool"); const_dve = sem("const_dve"); asc_s = sem("asc_s")
        taps_ready = sem("taps_ready"); wtr_done = sem("wtr_done"); w_ready = sem("w_ready")
        rs_s = sem("rs_s"); 
        ln_stat = sem("ln_stat"); ln_small = sem("ln_small"); xx_made = sem("xx_made"); xn_ready = sem("xn_ready")
        xT_done = sem("xT_done"); xnT_ready = sem("xnT_ready")
        xh_done = sem("xh_done"); g_done = sem("g_done"); x_read = sem("x_read"); tg_done = sem("tg_done")
        xc_ready = sem("xc_ready"); sg_made = sem("sg_made")
        dt_done = sem("dt_done"); bc_done = sem("bc_done"); dt_read = sem("dt_read"); e_capped = sem("e_capped")
        ln_step = sem("ln_step"); dt_step = sem("dt_step")
        bc_read = sem("bc_read"); bsb_ready = sem("bsb_ready"); b0_ready = sem("b0_ready")
        cs_step = sem("cs_step"); u_done = sem("u_done")
        sg_ready = sem("sg_ready"); dxc_ready = sem("dxc_ready")
        tanh_done = sem("tanh_done")
        exp_done = sem("exp_done"); bm_done = sem("bm_done"); scan_done = sem("scan_done")
        sq_done = sem("sq_done"); nrm_done = sem("nrm_done"); red_done = sem("red_done")
        s8_ready = sem("s8_ready"); fac_made = sem("fac_made"); fac_done = sem("fac_done")
        pow_done = sem("pow_done"); nrt_done = sem("nrt_done"); rec_done = sem("rec_done")
        h0_ready = sem("h0_ready"); cb_done = sem("cb_done"); cm_done = sem("cm_done")
        y_done = sem("y_done"); yg_done = sem("yg_done"); pre_done = sem("pre_done")
        op_done = sem("op_done"); x1_done = sem("x1_done"); st2_done = sem("st2_done")
        rstd2_done = sem("rstd2_done"); h2_ready = sem("h2_ready"); h2T_done = sem("h2T_done")
        h2T_ready = sem("h2T_ready"); lg_done = sem("lg_done"); lg_ready = sem("lg_ready")
        stat_step = sem("stat_step"); stat2_step = sem("stat2_step")

        N_WLOAD = 11
        LAST_SEGS = NSEG - SPW * (NWIN - 1)
        LS = NSEG - 1

        dAf = dA[:].rearrange("p r c -> p (r c)")
        hf_ = h[:].rearrange("p r c -> p (r c)")
        NS = E * CT

        def take(area, start, *shape):
            n = 1
            for d in shape:
                n *= d
            flat = area[:, start:start + n]
            names = "abcd"[:len(shape)]
            pat = " ".join(names)
            sizes = {c: d for c, d in zip(names, shape)}
            return (flat if len(shape) == 1 else flat.rearrange(f"p ({pat}) -> p {pat}", **sizes)), start + n

        WR = 4
        o = 0
        w1s, o = take(z, o, WR, F)
        w2s, o = take(z, o, WR, FC, DM)
        ohlo, o = take(z, o, NT * P // 2)
        ohlo = ohlo.bitcast(BF16).rearrange("p (k c) -> p k c", c=P)
        ohhi, o = take(z, o, NT * NS // 2)
        ohhi = ohhi.bitcast(BF16).rearrange("p (k c) -> p k c", c=NS)
        idw, o = take(z, o, NT * NS)
        idw = idw.bitcast(BF16).rearrange("p (k f c) -> p k f c", f=2, c=NS)
        gtw, o = take(z, o, NT * NS * 3 // 2)
        gtw = gtw.bitcast(BF16).rearrange("p (k f c) -> p k f c", f=3, c=NS)
        xs, o = take(z, o, WR, CT, 2 * DM)
        fin, o = take(z, o, WR, CT, DM)
        xTs, o = take(z, o, 2, CAP)
        hTs, _ = take(hf_, 0, 2, FC, CAP)
        o = 0
        lga, o = take(dAf, o, NT * E)
        em, o = take(dAf, o, NT * E)
        ex, o = take(dAf, o, NT * E)
        eq, o = take(dAf, o, NT * E)
        cand, o = take(dAf, o, NT * E)
        ohe, o = take(dAf, o, NT * E)
        cum, o = take(dAf, o, NT * E)
        keep, o = take(dAf, o, NT * E)
        mx, o = take(dAf, o, NT)
        im, o = take(dAf, o, NT)
        loc, o = take(dAf, o, NT)
        upper, o = take(dAf, o, NT)
        tile_no, o = take(dAf, o, NT)
        lo, o = take(dAf, o, NT)
        se, o = take(dAf, o, NT)
        gw, o = take(dAf, o, NT)
        part1, o = take(dAf, o, NT)
        place, o = take(dAf, o, NT)
        held, o = take(dAf, o, NS)
        gparts, o = take(dAf, o, 3 * NT // 2)
        gparts = gparts.bitcast(BF16).rearrange("p (f k) -> p f k", f=3)
        iol, o = take(dAf, o, P)
        iot, o = take(dAf, o, NS)
        iom, o = take(dAf, o, E)
        empty, o = take(dAf, o, NS)
        gs, o = take(dAf, o, NS)
        tot = bst[:].rearrange("p i c -> p (i c)")[:, 0:E]
        totp = bst2[:].rearrange("p i c -> p (i c)")[:, 0:E]
        sidx = sb("sidx", [P, NS], I32)
        gidx = sb("gidx", [P, NS], I32)
        PRE, SLOTS, GATES = 0, 6, 7

        ld_lg = sem("ld_lg")
        ld_we = [sem(f"ld_we{k}") for k in range(WR)]
        gathered = [sem(f"gathered{k}") for k in range(WR)]
        scattered = [sem(f"scattered{k}") for k in range(WR)]
        rt = sem("rt"); em_ready = sem("em_ready"); ex_done = sem("ex_done")
        tot_ready = sem("tot_ready"); pre_mm = sem("pre_mm"); pre_read = sem("pre_read")
        hi_ready = sem("hi_ready"); lo_ready = sem("lo_ready"); places_in = sem("places_in")
        gtw_done = sem("gtw_done"); slots_done = sem("slots_done"); gates_done = sem("gates_done")
        gs_ready = sem("gs_ready"); idx_ready = sem("idx_ready")
        xeT_done = sem("xeT_done"); xeT_ready = sem("xeT_ready"); up_done = sem("up_done")
        relu_a = sem("relu_a"); relu_b = sem("relu_b"); down_done = sem("down_done")
        fin_made = sem("fin_made")
        LOCH = 4

        def sp_tail(sp):
            sp.wait_ge(scan_done, NSEG)
            sp.dma_start(lga, lg_d.rearrange("(p k) e -> p (k e)", p=P)).then_inc(ld_lg, 16)
            sp.wait_ge(exp_done, NSEG)

            def weights(e, k):
                sp.dma_start(w1s[:, k, :], w1[bass.ds(e, 1)].rearrange("o m f -> (o m) f")).then_inc(ld_we[k], 16)
                sp.dma_start(w2s[:, k], w2[bass.ds(e, 1)].rearrange("o (c p) m -> (o p) c m", p=P)).then_inc(ld_we[k], 16)

            for k in range(WR):
                weights(k, k)
            with sp.Fori(0, E // WR - 1) as g:
                for k in range(WR):
                    sp.wait_ge(down_done, WR * g + k + 1)
                    weights(WR * g + k + WR, k)
            for q in range(WR):
                sp.wait_ge(scattered[q], 16 * CT * (E // WR))

        def pool_tail(pool):
            def gather(e):
                for t in range(CT):
                    i = CT * e + t
                    pool.indirect_dma_start(xs[:, e % WR, t, :], None, rows_d,
                                            bass.IndirectOffsetOnAxis(ap=gidx[:, i:i + 1], axis=0),
                                            bounds_check=TOK - 1, oob_is_err=False).then_inc(gathered[e % WR], 16)

            def scatter(e):
                for t in range(CT):
                    i = CT * e + t
                    pool.indirect_dma_start(outr, bass.IndirectOffsetOnAxis(ap=sidx[:, i:i + 1], axis=0),
                                            fin[:, e % WR, t, :], None,
                                            bounds_check=TOK - 1, oob_is_err=False).then_inc(scattered[e % WR], 16)

            pool.wait_ge(hi_ready, 1)
            pool.tensor_tensor(idw[:, :, 1, :], ohhi, place.unsqueeze(2).to_broadcast([P, NT, NS]), ALU.mult).then_inc(places_in, 1)
            pool.wait_ge(st_x1, 96 * NWIN)
            pool.wait_ge(idx_ready, 1)
            for e in range(WR):
                gather(e)
            pool.wait_ge(idx_ready, 2)
            for e in range(E):
                pool.wait_ge(fin_made, e + 1)
                if e + WR < E:
                    gather(e + WR)
                scatter(e)

        def act_tail(act):
            act.wait_ge(em_ready, 1)
            act.activation(ex, em, ACT.Exp).then_inc(ex_done, 1)

            def turn_in(e, q):
                act.wait_ge(xeT_done, e + 1)
                at_least(act, up_done, 2 * (e - 1))
                act.copy(xTs[:, q, :], ps[:, q, 0:CAP]).then_inc(xeT_ready, 1)

            def relu(e, q):
                act.wait_ge(up_done, 2 * e + 1)
                at_least(act, down_done, e - 1)
                act.activation(hTs[:, q, 0:2].rearrange("p c s -> p (c s)"), ps[:, 2 + 2 * q, :],
                               ACT.Relu).then_inc(relu_a, 1)

            turn_in(0, 0)
            turn_in(1, 1)
            relu(0, 0)
            turn_in(2, 0)
            relu(1, 1)
            with act.Fori(1, E // 2 - 1) as g:
                turn_in(2 * g + 1, 1)
                relu(2 * g, 0)
                turn_in(2 * g + 2, 0)
                relu(2 * g + 1, 1)
            turn_in(E - 1, 1)
            relu(E - 2, 0)
            relu(E - 1, 1)

        def dve_tail(dve):
            v3 = lambda t: t.rearrange("p (k e) -> p k e", e=E)
            e3 = lambda t: t.rearrange("p (e k) -> p e k", k=NT)
            n = [0]

            def step(ins):
                n[0] += 1
                ins.then_inc(rt, 1)
                dve.wait_ge(rt, n[0])

            dve.tensor_copy(part1, sidx[:])
            dve.memset(keep, 1.0)
            step(dve.tensor_copy(iol, iota_i[:]))
            dve.tensor_scalar(iot, iol[:, 0:NS], float(-NS), None, ALU.add)
            dve.tensor_scalar(iom, iol[:, 0:E], float(-E), None, ALU.add)
            dve.tensor_copy(place, iol[:, 0:NT])
            step(dve.memset(e3(keep)[:, :, 0], 0.0))
            dve.wait_ge(ld_lg, 16)
            step(dve.tensor_reduce(mx, v3(lga), AX_X, ALU.max))
            step(dve.tensor_tensor(v3(eq), v3(lga), mx.unsqueeze(2).to_broadcast([P, NT, E]), ALU.is_equal))
            step(dve.tensor_tensor(v3(cand), v3(eq), iom.unsqueeze(1).to_broadcast([P, NT, E]), ALU.mult))
            step(dve.tensor_reduce(im, v3(cand), AX_X, ALU.min))
            step(dve.tensor_tensor(e3(ohe), iom.unsqueeze(2).to_broadcast([P, E, NT]),
                                   im.unsqueeze(1).to_broadcast([P, E, NT]), ALU.is_equal))
            step(dve.tensor_tensor_scan(cum, keep, ohe, 0.0, ALU.mult, ALU.add))
            dve.tensor_copy(tot, e3(cum)[:, :, NT - 1]).then_inc(tot_ready, 1)
            dve.tensor_tensor(v3(em), v3(lga), mx.unsqueeze(2).to_broadcast([P, NT, E]), ALU.subtract).then_inc(em_ready, 1)
            dve.wait_ge(pre_mm, 1)
            dve.tensor_scalar(totp, ps[:, PRE, 0:E], -1.0, None, ALU.add).then_inc(pre_read, 1)
            dve.wait_ge(pre_read, 1)
            step(dve.tensor_tensor(e3(cand), e3(cum), totp.unsqueeze(2).to_broadcast([P, E, NT]), ALU.add))
            step(dve.tensor_tensor(cum, cand, ohe, ALU.mult))
            step(dve.tensor_reduce(loc, cum.rearrange("p (e k) -> p k e", k=NT), AX_X, ALU.add))
            step(dve.tensor_scalar(upper, loc, float(P), None, ALU.is_ge))
            dve.scalar_tensor_tensor(out=tile_no, in0=im, scalar=float(CT), in1=upper, op0=ALU.mult, op1=ALU.add)
            step(dve.scalar_tensor_tensor(out=lo, in0=upper, scalar=float(-P), in1=loc, op0=ALU.mult, op1=ALU.add))
            dve.tensor_tensor(ohhi, iot.unsqueeze(1).to_broadcast([P, NT, NS]),
                              tile_no.unsqueeze(2).to_broadcast([P, NT, NS]), ALU.is_equal).then_inc(hi_ready, 1)
            dve.wait_ge(hi_ready, 1)
            dve.tensor_tensor(idw[:, :, 0, :], ohhi, part1.unsqueeze(2).to_broadcast([P, NT, NS]), ALU.mult).then_inc(hi_ready, 1)
            for c in range(LOCH):
                kk = slice(c * NT // LOCH, (c + 1) * NT // LOCH)
                dve.tensor_tensor(ohlo[:, kk, :], iol.unsqueeze(1).to_broadcast([P, NT // LOCH, P]),
                                  lo[:, kk].unsqueeze(2).to_broadcast([P, NT // LOCH, P]),
                                  ALU.is_equal).then_inc(lo_ready, 1)
            dve.wait_ge(slots_done, 1)
            step(dve.tensor_reduce(held, ps[:, SLOTS, 0:2 * NS].rearrange("p (f c) -> p c f", c=NS), AX_X, ALU.add))
            dve.tensor_scalar(gidx[:], held, float(-NT), 0.0, ALU.add, ALU.max).then_inc(idx_ready, 1)
            dve.wait_ge(ex_done, 1)
            step(dve.tensor_reduce(se, v3(ex), AX_X, ALU.add))
            step(dve.reciprocal(gw, se))
            for f in range(3):
                step(dve.tensor_copy(gparts[:, f, :], gw))
                if f < 2:
                    step(dve.tensor_tensor(gw, gw, gparts[:, f, :], ALU.subtract))
                dve.tensor_tensor(gtw[:, :, f, :], ohhi, gparts[:, f, :].unsqueeze(2).to_broadcast([P, NT, NS]),
                                  ALU.mult).then_inc(gtw_done, 1)
            step(dve.tensor_scalar(empty, held, 0.5, NO_TOKEN, ALU.is_lt, ALU.mult))
            dve.scalar_tensor_tensor(out=sidx[:], in0=held, scalar=float(-NT), in1=empty,
                                     op0=ALU.add, op1=ALU.add).then_inc(idx_ready, 1)
            def relu(e, q):
                dve.wait_ge(up_done, 2 * e + 2)
                at_least(dve, down_done, e - 1)
                dve.tensor_scalar(hTs[:, q, 2:4].rearrange("p c s -> p (c s)"), ps[:, 3 + 2 * q, :], 0.0, None,
                                  ALU.max).then_inc(relu_b, 1)

            def take_out(e, k, before):
                dve.wait_ge(down_done, e + 1)
                at_least(dve, scattered[k], 16 * CT * before)
                for t in range(CT):
                    ins = dve.scalar_tensor_tensor(out=fin[:, k, t, :], in0=ps[:, 6 + k % 2, t * P:(t + 1) * P],
                                                   scalar=gs[:, bass.ds(CT * e + t, 1)], in1=xs[:, k, t, DM:2 * DM],
                                                   op0=ALU.mult, op1=ALU.add)
                ins.then_inc(fin_made, 1)

            relu(0, 0)
            dve.wait_ge(gates_done, 1)
            dve.tensor_reduce(gs, ps[:, GATES, 0:3 * NS].rearrange("p (f c) -> p c f", c=NS), AX_X,
                              ALU.add).then_inc(gs_ready, 1)
            dve.wait_ge(gs_ready, 1)
            take_out(0, 0, 0)
            relu(1, 1)
            relu(2, 0)
            take_out(1, 1, 0)
            relu(3, 1)
            take_out(2, 2, 0)
            relu(4, 0)
            take_out(3, 3, 0)
            relu(5, 1)
            with dve.Fori(1, E // WR - 1) as g:
                for k in range(WR):
                    take_out(WR * g + k, k, g)
                    relu(WR * g + k + 2, k % 2)
            for e in range(E - WR, E):
                take_out(e, e % WR, E // WR - 1)
                if e + 2 < E:
                    relu(e + 2, e % 2)

        def pe_tail(pe):
            pe.wait_ge(tot_ready, 1)
            pe.matmul(ps[:, PRE, 0:E], tri[:], tot, start=True, stop=True).then_inc(pre_mm, 1)
            pe.wait_ge(hi_ready, 2)
            pe.wait_ge(places_in, 1)
            for k in range(NT):
                if k % (NT // LOCH) == 0:
                    pe.wait_ge(lo_ready, k // (NT // LOCH) + 1)
                ins = pe.matmul(ps[:, SLOTS, 0:2 * NS], ohlo[:, k, :], idw[:, k].rearrange("p f c -> p (f c)"),
                                start=(k == 0), stop=(k == NT - 1))
            ins.then_inc(slots_done, 1)

            def gates():
                pe.wait_ge(gtw_done, 3)
                for k in range(NT):
                    ins = pe.matmul(ps[:, GATES, 0:3 * NS], ohlo[:, k, :], gtw[:, k].rearrange("p f c -> p (f c)"),
                                    start=(k == 0), stop=(k == NT - 1))
                ins.then_inc(gates_done, 1)

            def turn(e, k, loads):
                pe.wait_ge(gathered[k], 16 * CT * loads)
                at_least(pe, xeT_ready, e - 1)
                for t in range(CT):
                    ins = pe.transpose(ps[:, k % 2, t * P:(t + 1) * P], xs[:, k, t, 0:DM], ident[:])
                ins.then_inc(xeT_done, 1)

            def up(e, k, loads):
                pe.wait_ge(ld_we[k], 32 * loads)
                pe.wait_ge(xeT_ready, e + 1)
                q = k % 2
                for c in range(FC):
                    if c == 0:
                        at_least(pe, relu_a, e - 1)
                    if c == 2:
                        at_least(pe, relu_b, e - 1)
                    ins = pe.matmul(ps[:, 2 + 2 * q + c // 2, (c % 2) * CAP:(c % 2 + 1) * CAP],
                                    w1s[:, k, c * P:(c + 1) * P], xTs[:, q, :], start=True, stop=True)
                    if c % 2:
                        ins.then_inc(up_done, 1)

            def down(e, k):
                q = k % 2
                pe.wait_ge(relu_a, e + 1)
                pe.wait_ge(relu_b, e + 1)
                at_least(pe, fin_made, e - 1)
                for t in range(CT):
                    for c in range(FC):
                        ins = pe.matmul(ps[:, 6 + q, t * P:(t + 1) * P], hTs[:, q, c, t * P:(t + 1) * P],
                                        w2s[:, k, c, :], start=(c == 0), stop=(c == FC - 1))
                ins.then_inc(down_done, 1)

            pe.wait_ge(pre_read, 1)
            for _ in range(10):
                pe.matmul(ps[:, PRE, 0:P], ident[:], ident[:], start=True, stop=True)
            turn(0, 0, 1)
            up(0, 0, 1)
            turn(1, 1, 1)
            gates()
            pe.wait_ge(idx_ready, 2)
            down(0, 0)
            up(1, 1, 1)
            turn(2, 2, 1)
            pe.wait_ge(gs_ready, 1)
            turn(3, 3, 1)
            up(2, 2, 1)
            down(1, 1)
            with pe.Fori(0, E // WR - 1) as g:
                for k in range(3, WR + 3):
                    turn(WR * g + k + 1, (k + 1) % WR, g + 1 + (k + 1) // WR)
                    up(WR * g + k, k % WR, g + 1 + k // WR)
                    down(WR * g + k - 1, (k - 1) % WR)
            up(E - 1, WR - 1, E // WR)
            down(E - 2, WR - 2)
            down(E - 1, WR - 1)

        block = ctx.enter_context(nc.Block())

        @block.sync
        def _(sp):
            sp.dma_start(win_n, W_in.rearrange("(k p) c -> p k c", p=P)).then_inc(ld_w, 16)
            sp.dma_start(conv_c[:], conv_w.rearrange("(k p) o t -> p k (o t)", p=P)).then_inc(ld_w, 16)
            xq = x.rearrange("(i q) t m -> q t i m", q=2)

            def load_x_direct(t0, n, j0):
                for q in range(2):
                    sp.dma_start(xt[q * GRID + j0:q * GRID + j0 + n, :, :], xq[q, t0:t0 + n]).then_inc(ld_x, 16)

            sp.wait_ge(const_dve, 1)
            load_x_direct(0, GRID - 3, 3)
            sp.dma_start(z[:, 10 * P:14 * P].rearrange("p (j c) -> p j c", j=H),
                         W_dt.rearrange("(j p) c -> p j c", p=P)).then_inc(ld_w, 16)
            sp.dma_start(z[:, 16 * P:18 * P], W_out).then_inc(ld_w, 16)
            sp.dma_start(cbh[:], conv_b.rearrange("(k p) -> p k", p=P), allow_slow_non_contiguous=True).then_inc(ld_w, 16)
            sp.dma_start(bdt[:], b_dt.rearrange("(k p) -> p k", p=P), allow_slow_non_contiguous=True).then_inc(ld_w, 16)
            sp.dma_start(dpar[:], D_param.rearrange("(k p) -> p k", p=P), allow_slow_non_contiguous=True).then_inc(ld_w, 16)
            sp.dma_start(asc[:], A_log.rearrange("(k p) n -> p k n", p=P)).then_inc(ld_w, 16)
            sp.dma_start(nw[:], norm_w.rearrange("(p o) -> p o", o=1)).then_inc(ld_w, 16)
            sp.dma_start(rs[:], residual_scale.unsqueeze(0).to_broadcast([P, 1])).then_inc(ld_w, 16)
            sp.dma_start(wg_s[:], Wg).then_inc(ld_w, 16)
            sp.wait_ge(const_dve, 5)
            sp.dma_start(z[0:NST, 14 * P:16 * P], W_C).then_inc(ld_bc, 16)
            sp.dma_start(z[32:32 + NST, 14 * P:16 * P], W_B).then_inc(ld_bc, 16)
            sp.dma_start(z[64:64 + NST, 14 * P:16 * P], W_C).then_inc(ld_bc, 16)
            sp.dma_start(z[96:96 + NST, 14 * P:16 * P], W_C).then_inc(ld_bc, 16)
            sp.dma_start(xpad[0:TOK, :].rearrange("(r k) m -> r (k m)", r=P),
                         x.rearrange("b (r k) m -> (b r) (k m)", r=P // B)).then_inc(st_pad, 16)
            sp.wait_ge(const_dve, 6)
            sp.dma_start(xpad[TOK:TOK + GRID, :], yg[0:GRID, 0, 0:DM // GRID, :].rearrange("p b t -> p (b t)")).then_inc(st_pad, 16)

            def store_xx(v):
                sp.wait_ge(xn_ready, v + 1)
                sp.dma_start(xx_d[bass.ds(v, 1)].rearrange("o p c -> p (o c)"),
                             xx[:].rearrange("p i m -> p (i m)")).then_inc(st_xx, 16)

            def store_b(v):
                sp.wait_ge(bsb_ready, v + 1)
                sp.dma_start(b_d[bass.ds(v, 1)].rearrange("o s n c -> (o n) s c"),
                             bsb[32:32 + NST].rearrange("p s b t -> p s (b t)")).then_inc(st_b, 16)
                sp.wait_ge(st_b, 16 * (v + 1))

            def spread_b(w, s, first=False):
                S = SPW * w + s
                at_least(sp, bm_done, 2 * (S - RING + 1))
                sp.dma_start(bb[:, s % RING, :],
                             b_d[bass.ds(w, 1), s].rearrange("o n c -> o (n c)")
                             .to_broadcast([P, NST * BS])).then_inc(ld_bb[s % RING], 16)

            def load_x(v):
                sp.wait_ge(xT_done, v)
                for q in range(2):
                    src = xpad[bass.ds(WIN * v - 3 + q * T, (TILES - 1) * 2 * T + GRID), :]
                    src = bass.AP(tensor=src.tensor, offset=src.offset,
                                  ap=[[DM, GRID], [2 * T * DM, TILES], [1, DM]])
                    sp.dma_start(xt[q * GRID:(q + 1) * GRID, :, :], src).then_inc(ld_x, 16)

            def load_xx(o):
                at_least(sp, st_x1, 96 * o)
                if isinstance(o, int):
                    sp.wait_ge(st_xx, 16 * (o + 1))
                sp.dma_start(xxr[:].rearrange("p i m -> p (i m)"),
                             xx_d[bass.ds(o, 1)].rearrange("o p c -> p (o c)")).then_inc(ld_xx, 16)

            def store_out(o, n):
                sp.wait_ge(h2_ready, o + 1)
                for buf, dst, width, c0 in ((h2b, rows_d, 2 * DM, 0), (xxr, rows_d, 2 * DM, DM), (xxr, outr, DM, 0)):
                    for q in range(2):
                        d = dst[bass.ds(WIN * o + q * T, (TILES - 1) * 2 * T + n), c0:c0 + DM]
                        d = bass.AP(tensor=d.tensor, offset=d.offset,
                                    ap=[[width, n], [2 * T * width, TILES], [1, DM]])
                        sp.dma_start(d, buf[q * GRID + 3:q * GRID + 3 + n, :, :]).then_inc(st_x1, 16)

            def store_lg(o, n):
                sp.wait_ge(lg_ready, o + 1)
                for q in range(2):
                    d = lg_d[bass.ds(WIN * o + q * T, (TILES - 1) * 2 * T + n), :]
                    d = bass.AP(tensor=d.tensor, offset=d.offset,
                                ap=[[E, n], [2 * T * E, TILES], [1, E]])
                    sp.dma_start(d, lgb[q * GRID + 3:q * GRID + 3 + n, :, :]).then_inc(st_lg, 16)

            store_xx(0)
            sp.wait_ge(xT_done, 1)
            load_x_direct(WIN - 3, GRID, 0)
            sp.wait_ge(b0_ready, 1)
            sp.dma_start(b0_d, b0s[32:32 + NST, :]).then_inc(st_b0, 16)
            sp.wait_ge(st_b0, 16)
            sp.dma_start(b0b[:].rearrange("p n b -> p (n b)"),
                         b0_d.rearrange("(o n) b -> o (n b)", o=1).to_broadcast([P, NST * B])).then_inc(ld_b0, 16)
            store_b(0)
            for s in range(RING):
                spread_b(0, s)
            store_xx(1)
            sp.wait_ge(st_pad, 32)
            load_x(2)

            def iteration(w, prep, ln, out_, nseg):
                for s in range(nseg):
                    if s == 0 and out_:
                        load_xx(w - 1)
                    if s == 1 and out_ == 2:
                        store_lg(w - 2, WIN)
                    if s == 3 and prep:
                        store_b(w + 1)
                    if s == 4 and ln:
                        store_xx(w + 2)
                    if s == 4 and ln == 2:
                        load_x(w + 3)
                    if s + RING < nseg:
                        spread_b(w, s + RING)
                    elif prep:
                        spread_b(w + 1, s + RING - SPW)
                    if s == nseg - 1 and out_:
                        store_out(w - 1, WIN)

            iteration(0, True, 2, 0, SPW)
            iteration(1, True, 2, 1, SPW)
            with sp.Fori(2, NWIN - 3) as w:
                iteration(w, True, 2, 2, SPW)
            iteration(NWIN - 3, True, 1, 2, SPW)
            iteration(NWIN - 2, True, 0, 2, SPW)
            iteration(NWIN - 1, False, 0, 2, LAST_SEGS)
            load_xx(NWIN - 1)
            store_lg(NWIN - 2, WIN)
            store_out(NWIN - 1, T - WIN * (NWIN - 1))
            store_lg(NWIN - 1, T - WIN * (NWIN - 1))
            sp.wait_ge(st_x1, 96 * NWIN)
            sp.wait_ge(st_lg, 32 * NWIN)
            sp_tail(sp)

        @block.gpsimd
        def _(pool):
            pool.memset(ident[:], 0.0).then_inc(const_pool, 1)
            pool.memset(sel[:], 0.0).then_inc(const_pool, 1)
            pool.wait_ge(const_pool, 2)
            pool.affine_select(out=ident[:], in_=ident[:], compare_op=ALU.not_equal, fill=1.0, base=0,
                               pattern=[[-1, P]], channel_multiplier=1).then_inc(const_pool, 1)

            def ln_pool(v):
                pool.wait_ge(ln_stat, v + 1)
                n = [0]

                def step(ins):
                    n[0] += 1
                    ins.then_inc(ln_small, 1)
                    pool.wait_ge(ln_small, LNK * v + n[0])

                rstd, q, q2, q3, r2, r12, a1, nmean, nm12 = (lnp[:, k, :] for k in range(9))
                step(pool.tensor_tensor(rstd, ve[:], neghalf_e[:], ALU.pow))
                step(pool.tensor_tensor(q, rstd, rstd, ALU.mult))
                step(pool.tensor_tensor(q2, q, mv[:, :, 1], ALU.mult))
                step(pool.tensor_tensor(q3, q2, eps_rms[:], ALU.add))
                step(pool.tensor_tensor(r2, q3, neghalf_e[:], ALU.pow))
                step(pool.tensor_tensor(r12, rstd, r2, ALU.mult))
                step(pool.tensor_tensor(a1, rstd, ones4[:], ALU.add))
                step(pool.tensor_tensor(nmean, mv[:, :, 0], minus4[:], ALU.mult))
                step(pool.tensor_tensor(q, nmean, rstd, ALU.mult))
                step(pool.tensor_tensor(nm12, nmean, r12, ALU.mult))

            def make_u(v):
                pool.wait_ge(dt_step, 2 * (v + 1))
                pool.wait_ge(xc_ready, v + 1)
                at_least(pool, bm_done, 2 * SPW * v)
                pool.tensor_tensor(u[:], dtb[:], xc[:], ALU.mult).then_inc(u_done, 1)

            def products(w, s, hf, k0=0, k1=4):
                S = SPW * w + s
                pool.wait_ge(u_done, w + 1)
                pool.wait_ge(ld_bb[s % RING], 16 * (SPW // RING * w + s // RING + 1))
                at_least(pool, y_done, S - RING + 1)
                at_least(pool, h0_ready, S - RING + 2)
                us = cols(u, hf)[:, :, SEG * s + 1:SEG * s + 1 + SEG]
                hr = rows(h, s % RING)
                for k in range(k0, k1):
                    n0, nn = k * NST // 4, NST // 4
                    o = hr[:, hf * RH + n0 * B:hf * RH + (n0 + nn) * B, 1:SLOT]
                    ins = pool.tensor_tensor(
                        o.rearrange("p (n b) t -> p n b t", b=B),
                        us.unsqueeze(1).to_broadcast([P, nn, B, SEG]),
                        bb[:, s % RING, n0 * BS:(n0 + nn) * BS].rearrange("p (n b t) -> p n b t", b=B, t=SEG),
                        ALU.mult)
                if k1 == 4:
                    ins.then_inc(bm_done, 1)

            def root(k):
                pool.wait_ge(s8_ready, k + 1)
                pool.tensor_tensor(nrm8[:], s8[:], half_e[:], ALU.pow).then_inc(pow_done, 1)
                pool.wait_ge(pow_done, k + 1)
                pool.tensor_tensor(nrt8[:], nrm8[:], guard8[:], ALU.add).then_inc(nrt_done, 1)

            def out_pool(o):
                pool.wait_ge(st2_done, o + 1)
                pool.tensor_tensor(nmean2[:], mv2[:, :, 0], minus4[:], ALU.mult).then_inc(rstd2_done, 1)
                pool.tensor_tensor(rstd2[:], ve2[:], neghalf_e[:], ALU.pow).then_inc(rstd2_done, 1)
                pool.wait_ge(rstd2_done, 3 * o + 2)
                pool.tensor_tensor(nbias2[:], nmean2[:], rstd2[:], ALU.mult).then_inc(rstd2_done, 1)

            pool.wait_ge(const_dve, 6)
            ln_pool(0)
            for k, off in enumerate((0, 64, 96)):
                pool.affine_select(out=sel[:], in_=sel[:], compare_op=ALU.not_equal, fill=1.0, base=-off,
                                   pattern=[[-1, NST], [0, P]], channel_multiplier=1).then_inc(const_pool, 1)
                pool.wait_ge(const_pool, 4 + k)
            pool.memset(tri[:], 1.0).then_inc(const_pool, 1)
            pool.wait_ge(const_pool, 7)
            pool.affine_select(out=tri[:], in_=tri[:], compare_op=ALU.is_gt, fill=0.0, base=0,
                               pattern=[[1, P]], channel_multiplier=-1).then_inc(const_pool, 1)
            pool.iota(iota_i[:], [[1, P]], base=0, channel_multiplier=0).then_inc(const_pool, 1)
            pool.iota(sidx[:], [[0, NT]], base=NT, channel_multiplier=NT).then_inc(const_pool, 1)
            ln_pool(1)
            make_u(0)
            pool.wait_ge(u_done, 1)
            pool.wait_ge(ld_b0, 16)
            for hf in range(H):
                pool.tensor_tensor(sqb[:, hf * RH:(hf + 1) * RH].rearrange("p (n b) -> p n b", b=B),
                                   cols(u, hf)[:, :, 0].unsqueeze(1).to_broadcast([P, NST, B]),
                                   b0b[:], ALU.mult).then_inc(pre_done, 1)
            root(0)
            products(0, 0, 0)
            products(0, 0, 1)
            products(0, 1, 0)

            def iteration(w, prep, ln, out_, nseg):
                for s in range(nseg):
                    S = SPW * w + s
                    if s == 3 and prep:
                        root(S + 1)
                    if s + 1 < nseg:
                        products(w, s + 1, 1)
                    elif prep:
                        products(w + 1, 0, 1)
                    ahead = AHEAD[s] if s + 2 < nseg else 0
                    if ahead:
                        products(w, s + 2, 0, 0, ahead)
                    if s == 2 and ln:
                        ln_pool(w + 2)
                    if s != 3 and (prep or s + 1 < nseg):
                        root(S + 1)
                    if s == 2 and out_:
                        out_pool(w - 1)
                    if s == 4 and prep:
                        make_u(w + 1)
                    if s + 2 >= nseg:
                        if prep:
                            products(w + 1, s + 2 - SPW, 0)
                    elif ahead < 4:
                        products(w, s + 2, 0, ahead, 4)

            AHEAD = (1, 3, 0, 0, 0, 0)
            iteration(0, True, 1, 0, SPW)
            with pool.Fori(1, NWIN - 2) as w:
                iteration(w, True, 1, 1, SPW)
            iteration(NWIN - 2, True, 0, 1, SPW)
            iteration(NWIN - 1, False, 0, 1, LAST_SEGS)
            out_pool(NWIN - 1)
            pool_tail(pool)

        @block.scalar
        def _(act):
            act.wait_ge(ld_w, 16 * N_WLOAD)
            act.activation(asc[:], asc[:], ACT.Tanh, scale=0.1).then_inc(asc_s, 1)
            act.wait_ge(asc_s, 1)
            act.activation(asc[:], asc[:], ACT.Exp, scale=10.0).then_inc(asc_s, 1)
            act.wait_ge(asc_s, 2)
            act.mul(asc[:], asc[:], -1.0 / 16.0).then_inc(asc_s, 1)
            act.activation(rs[:], rs[:], ACT.Tanh, scale=0.5).then_inc(rs_s, 1)
            act.mul(cbh[:], cbh[:], 0.5).then_inc(asc_s, 1)
            act.wait_ge(asc_s, 4)

            def evac_xT(v):
                act.wait_ge(xT_done, v + 1)
                at_least(act, g_done, 2 * v)
                act.copy(xnT[:].rearrange("p b t -> p (b t)"), bank(B_XT)).then_inc(xnT_ready, 1)

            def decay(w, s, first=False):
                S = SPW * w + s
                act.wait_ge(tanh_done, 1 if first else w + 2)
                at_least(act, scan_done, S - RING + 1)
                act.activation(rows(dA, s % RING)[:, :, 1:SLOT], zall[:, :, SEG * s:SEG * (s + 1)],
                               ACT.Exp, scale=16.0).then_inc(exp_done, 1)

            def take_over(w):
                act.wait_ge(sg_made, 2 * (w + 1))
                at_least(act, yg_done, SPW * w)
                act.copy(sgc[:], sgn[:]).then_inc(sg_ready, 1)

            def scale_x(w):
                act.wait_ge(xc_ready, w + 1)
                at_least(act, y_done, SPW * w)
                for hf in range(H):
                    act.activation(dxc[:, hf, :], xc[:, hf, :], ACT.Copy, scale=dpar[:, hf:hf + 1]).then_inc(dxc_ready, 1)

            def silu_x(v):
                at_least(act, u_done, v)
                at_least(act, bc_done, v)
                at_least(act, dxc_ready, 2 * v)
                at_least(act, xc_ready, v)
                for hf in range(H):
                    act.wait_ge(xh_done, 2 * v + hf + 1)
                    act.activation(thx[:, hf, :], bankc(B_XH[hf]), ACT.Tanh, bias=cbh[:, hf:hf + 1])
                    act.activation(xc[:, hf, :], bankc(B_XH[hf]), ACT.Identity, bias=cbh[:, hf:hf + 1]).then_inc(x_read, 1)

            def tanh_gate(v, hf):
                act.wait_ge(g_done, 2 * v + hf + 1)
                if hf == 0:
                    at_least(act, sg_ready, v)
                act.activation(sgn[:, hf, :], bankc(B_G[hf]), ACT.Tanh).then_inc(tg_done, 1)

            def exp_dt(v, hf):
                if hf == 0:
                    at_least(act, u_done, v)
                act.wait_ge(dt_done, 2 * v + hf + 1)
                act.activation(dtb[:, hf, :], bankc(B_DT[hf]), ACT.Exp, bias=bdt[:, hf:hf + 1]).then_inc(dt_read, 1)

            def evac_bc(v):
                act.wait_ge(bc_done, v + 1)
                at_least(act, st_b, 16 * v)
                act.copy(bsb[32:32 + NST].rearrange("p s b t -> p b s t"),
                         ps[32:32 + NST, B_BC, 0:B * COLS].rearrange("p (b c) -> p b c", b=B)[:, :, 1:COLS]
                         .rearrange("p b (s t) -> p b s t", t=SEG)).then_inc(bsb_ready, 1)
                at_least(act, cs_step, 4 * v)
                act.copy(cs_next[:], bankc(B_BC)).then_inc(bc_read, 1)
                act.copy(bcraw[:], bankc(B_BC)).then_inc(bc_read, 1)
                if isinstance(v, int) and v == 0:
                    act.copy(b0s[32:32 + NST, :],
                             ps[32:32 + NST, B_BC, 0:B * COLS].rearrange("p (b c) -> p b c", b=B)[:, :, 0]).then_inc(b0_ready, 1)

            def clamp_dt(v):
                act.wait_ge(e_capped, v + 1)
                act.activation(dtb[:], dtb[:], ACT.Ln, bias=1.0).then_inc(ln_step, 1)
                act.wait_ge(ln_step, v + 1)
                act.activation(dtb[:], dtb[:], ACT.Tanh, scale=0.5 / 0.0495, bias=spb[:, 0:1]).then_inc(dt_step, 1)
                act.wait_ge(dt_step, 2 * v + 1)
                act.activation(dtb[:], dtb[:], ACT.Copy, scale=0.0495 / 0.5, bias=0.0505).then_inc(dt_step, 1)
                act.wait_ge(dt_step, 2 * (v + 1))

            def norm_x(v):
                act.wait_ge(ln_small, LNK * (v + 1))
                at_least(act, st_xx, 16 * v)
                for i in range(TILES):
                    ins = act.activation(xx[:, i, :], xt[:, i, :], ACT.Identity, scale=lnp[:, 6, i:i + 1],
                                         bias=lnp[:, 1, i:i + 1])
                ins.then_inc(xx_made, 1)
                act.wait_ge(xx_made, v + 1)
                for i in range(TILES):
                    ins = act.activation(xt[:, i, :], xt[:, i, :], ACT.Identity, scale=lnp[:, 5, i:i + 1],
                                         bias=lnp[:, 8, i:i + 1])
                ins.then_inc(xn_ready, 1)

            def make_h2(o):
                act.wait_ge(rstd2_done, 3 * (o + 1))
                at_least(act, st_x1, 96 * o)
                at_least(act, h2T_done, o)
                for i in range(TILES):
                    ins = act.activation(h2b[:, i, :], xxr[:, i, :], ACT.Identity, scale=rstd2[:, i:i + 1],
                                         bias=nbias2[:, i:i + 1])
                ins.then_inc(h2_ready, 1)

            def evac_h2T(o):
                act.wait_ge(h2T_done, o + 1)
                at_least(act, lg_done, o)
                act.copy(h2T[:].rearrange("p i m -> p (i m)"), bank(B_H2)).then_inc(h2T_ready, 1)

            def decay_tanh(v, between, t0=0, t1=WIN):
                at_least(act, exp_done, SPW * v)
                for hf in range(H):
                    for n in range(NST):
                        if hf * NST + n in between:
                            between[hf * NST + n]()
                        ins = act.activation(zrow[:, hf * NST + n, :, t0:t1], cols(dtb, hf)[:, :, 1 + t0:1 + t1],
                                             ACT.Tanh, scale=asc[:, hf, n:n + 1])
                ins.then_inc(tanh_done, 1)

            act.wait_ge(wtr_done, 5)
            act.copy(wT[:, 12:16, :].rearrange("p k c -> p (k c)"), ps[:, 3, :])
            act.copy(wT[:, 16:18, :].rearrange("p k c -> p (k c)"), ps[:, 4, 0:2 * P]).then_inc(w_ready, 1)
            evac_xT(0)
            silu_x(0)
            for hf in range(H):
                exp_dt(0, hf)
            evac_bc(0)
            clamp_dt(0)
            decay_tanh(0, {0: lambda: tanh_gate(0, 0), 1: lambda: tanh_gate(0, 1), 16: lambda: evac_xT(1)}, 0, 3 * SEG)
            for s in range(3):
                decay(0, s, first=True)
            scale_x(0)
            silu_x(1)
            take_over(0)
            decay_tanh(0, {}, 3 * SEG, WIN)

            def iteration(w, prep, ln, out_, nseg, started=False):
                if not started:
                    for s in range(3):
                        decay(w, s)
                    scale_x(w)
                    if prep:
                        silu_x(w + 1)
                    take_over(w)
                decay(w, 3)
                if not prep:
                    make_h2(w - 1)
                    evac_h2T(w - 1)
                    return
                for hf in range(H):
                    exp_dt(w + 1, hf)
                decay(w, 4)
                clamp_dt(w + 1)
                decay(w, 5)
                between = {BC_ROW: lambda: evac_bc(w + 1), G_ROWS[0]: lambda: tanh_gate(w + 1, 0),
                           G_ROWS[1]: lambda: tanh_gate(w + 1, 1)}
                if ln:
                    if not started:
                        between[XX_ROW] = lambda: norm_x(w + 2)
                    between[XT_ROW] = lambda: evac_xT(w + 2)
                if out_:
                    between[H2M_ROW] = lambda: make_h2(w - 1)
                    between[H2_ROW] = lambda: evac_h2T(w - 1)
                decay_tanh(w + 1, between)

            BC_ROW, XX_ROW, G_ROWS, XT_ROW, H2M_ROW, H2_ROW = 0, 3, (2, 11), 14, 12, 28
            iteration(0, True, True, False, SPW, started=True)
            iteration(1, True, True, True, SPW)
            with act.Fori(2, NWIN - 2) as w:
                iteration(w, True, True, True, SPW)
            iteration(NWIN - 2, True, False, True, SPW)
            iteration(NWIN - 1, False, False, True, LAST_SEGS)
            make_h2(NWIN - 1)
            evac_h2T(NWIN - 1)
            act_tail(act)

        @block.vector
        def _(dve):
            dve.memset(xt[:], 0.0).then_inc(const_dve, 1)
            dve.memset(bound_w[:], 1.0 / MAX_NORM ** 2).then_inc(const_dve, 1)
            dve.memset(ones_r[:], 1.0)
            dve.memset(half_e[:], 0.5).then_inc(const_dve, 1)
            dve.memset(neghalf_e[:], -0.5).then_inc(const_dve, 1)
            dve.memset(eps_rms[:], 1e-6)
            dve.memset(ones4[:], 1.0)
            dve.memset(minus4[:], -1.0)
            dve.memset(guard8[:], 1e-8 / MAX_NORM)
            dve.memset(spb[:], -0.0505 * 0.5 / 0.0495)
            dve.memset(z[:, 14 * P:16 * P], 0.0).then_inc(const_dve, 1)
            dve.memset(yg[:], 0.0)
            for r in range(RING):
                ins = dve.memset(rows(dA, r)[:, :, 0], 0.0)
            ins.then_inc(const_dve, 1)

            def ln_stats(v, src, b6, m2, e1, ready, count, step, done):
                dve.wait_ge(ready, count)
                for i in range(TILES):
                    ins = dve.bn_stats(b6[:, i, :], src[:, i, :])
                ins.then_inc(step, 1)
                dve.wait_ge(step, 2 * v + 1)
                dve.memset(pad[:], 0.0)
                for i in range(TILES):
                    ins = dve.bn_aggr(m2[:, i, :], b6[:, i, :])
                ins.then_inc(step, 1)
                dve.wait_ge(step, 2 * (v + 1))
                dve.tensor_scalar(e1[:], m2[:, :, 1], 1e-5, None, ALU.add).then_inc(done, 1)

            def ln_in(v):
                ln_stats(v, xt, bst, mv, ve, ld_x, 32 * (v + 1), stat_step, ln_stat)

            def norm_x(v):
                dve.wait_ge(ln_small, LNK * (v + 1))
                at_least(dve, st_xx, 16 * v)
                for i in range(TILES):
                    ins = dve.tensor_scalar(xx[:, i, :], xt[:, i, :], lnp[:, 6, i:i + 1], lnp[:, 1, i:i + 1],
                                            ALU.mult, ALU.add)
                ins.then_inc(xx_made, 1)
                for i in range(TILES):
                    ins = dve.tensor_scalar(xt[:, i, :], xt[:, i, :], lnp[:, 5, i:i + 1], lnp[:, 8, i:i + 1],
                                            ALU.mult, ALU.add)
                ins.then_inc(xn_ready, 1)

            def make_xc(v):
                for hf in range(H):
                    dve.wait_ge(x_read, 2 * v + hf + 1)
                    ins = dve.scalar_tensor_tensor(out=xc[:, hf, :], in0=thx[:, hf, :], scalar=1.0,
                                                   in1=xc[:, hf, :], op0=ALU.add, op1=ALU.mult)
                ins.then_inc(xc_ready, 1)

            def cap_e(v):
                dve.wait_ge(dt_read, 2 * (v + 1))
                dve.tensor_scalar(dtb[:], dtb[:], E_MAX, None, ALU.min).then_inc(e_capped, 1)

            def make_gate(v, hf):
                dve.wait_ge(tg_done, 2 * v + hf + 1)
                dve.scalar_tensor_tensor(out=sgn[:, hf, :], in0=sgn[:, hf, :], scalar=1.0,
                                         in1=bankc(B_G[hf]), op0=ALU.add, op1=ALU.mult).then_inc(sg_made, 1)

            def split_c(v):
                dve.wait_ge(bc_read, 2 * (v + 1))
                n = [0]

                def step(ins):
                    n[0] += 1
                    ins.then_inc(cs_step, 1)
                    dve.wait_ge(cs_step, 4 * v + n[0])

                step(dve.tensor_tensor(bcraw[64:P], bcraw[64:P], cs_next[64:P], ALU.subtract))
                step(dve.tensor_copy(cs_next[64:P], bcraw[64:P]))
                step(dve.tensor_tensor(cs_next[96:P], bcraw[96:P], cs_next[96:P], ALU.subtract))

            def take_c(v):
                at_least(dve, cb_done, 3 * SPW * v)
                dve.tensor_copy(cs[:], cs_next[:]).then_inc(cs_step, 1)

            def sum_squares(k):
                dve.wait_ge(sq_done, k + 1)
                dve.tensor_reduce(s_p[:], sqb[:].rearrange("p (r b) -> p b r", b=B), AX_X,
                                  ALU.add).then_inc(red_done, 1)

            def take_norm(k):
                dve.wait_ge(nrm_done, k + 1)
                dve.tensor_copy(s8[:], ps[0:B, NB, 0:1]).then_inc(s8_ready, 1)

            def factor(k):
                dve.wait_ge(nrt_done, k + 1)
                dve.reciprocal(fac8[:], nrt8[:]).then_inc(rec_done, 1)
                dve.wait_ge(rec_done, k + 1)
                dve.tensor_scalar(fac_d[:], ident[0:B, 0:B], fac8[:, 0:1], None, ALU.mult).then_inc(fac_made, 1)

            def restart(k, last, S_next, s_next):
                dve.wait_ge(fac_done, k + 1)
                at_least(dve, y_done, S_next - RING + 1)
                dve.scalar_tensor_tensor(
                    out=rows(h, s_next % RING)[:, :, 0].rearrange("p (r b) -> p r b", b=B),
                    in0=ps[:, NB, 0:B].unsqueeze(1).to_broadcast([P, H * NST, B]), scalar=1.0,
                    in1=last.rearrange("p (r b) -> p r b", b=B), op0=ALU.min, op1=ALU.mult).then_inc(h0_ready, 1)

            def gate_y(w, s):
                S = SPW * w + s
                dve.wait_ge(y_done, S + 1)
                dve.wait_ge(sg_ready, w + 1)
                if s == 0:
                    at_least(dve, op_done, w)
                dve.tensor_tensor(
                    yg[:].rearrange("p h b t -> p (h b) t")[:, :, 3 + SEG * s:3 + SEG * (s + 1)],
                    ps[:, YB, 0:H * BS].rearrange("p (r t) -> p r t", t=SEG),
                    sgc[:].rearrange("p h (b c) -> p (h b) c", c=COLS)[:, :, SEG * s:SEG * (s + 1)],
                    ALU.mult).then_inc(yg_done, 1)

            def segment(w, s, last, early, extra):
                S = SPW * w + s
                dve.wait_ge(exp_done, S + 1)
                dve.wait_ge(bm_done, 2 * (S + 1))
                dve.wait_ge(h0_ready, S + 1)
                hs = h[:, s % RING, :]
                dve.tensor_tensor_scan(hs, dA[:, s % RING, :], hs, 0.0, ALU.mult, ALU.add).then_inc(scan_done, 1)
                dve.wait_ge(scan_done, S + 1)
                hr = rows(h, s % RING)
                hl = hr[:, :, SEG]
                if not last:
                    dve.tensor_tensor(sqb[:], hl, hl, ALU.mult).then_inc(sq_done, 1)
                if s > 0:
                    gate_y(w, s - 1)
                elif not (isinstance(w, int) and w == 0):
                    gate_y(w - 1, SPW - 1)
                if not last:
                    sum_squares(S + 1)
                early()
                h4 = hr.rearrange("p (f r) t -> p f r t", f=H)
                for j, (n0, n1) in enumerate(NCH):
                    dve.wait_ge(cb_done, 3 * S + j + 1)
                    m = h4[:, :, n0 * B:n1 * B, 0:SEG]
                    dve.tensor_tensor(m, m, ps[:, j, 0:(n1 - n0) * BS].rearrange("p (r t) -> p r t", t=SEG)
                                      .unsqueeze(1).to_broadcast([P, H, (n1 - n0) * B, SEG]),
                                      ALU.mult).then_inc(cm_done, 1)
                    if j == 0 and not last:
                        take_norm(S + 1)
                    if j == 1 and not last:
                        factor(S + 1)
                extra()
                if not last:
                    restart(S + 1, hl, S + 1, s + 1)

            def add_out(o):
                dve.wait_ge(op_done, o + 1)
                dve.wait_ge(ld_xx, 16 * (o + 1))
                dve.scalar_tensor_tensor(out=xxr[:].rearrange("p i m -> p (i m)"), in0=bank(out_bank(o)), scalar=rs[:, 0:1],
                                         in1=xxr[:].rearrange("p i m -> p (i m)"), op0=ALU.mult,
                                         op1=ALU.add).then_inc(x1_done, 1)

            def out_stats(o):
                ln_stats(o, xxr, bst2, mv2, ve2, x1_done, o + 1, stat2_step, st2_done)

            def evac_lg(o):
                dve.wait_ge(lg_done, o + 1)
                at_least(dve, st_lg, 32 * o)
                dve.tensor_copy(lgb[:].rearrange("p i e -> p (i e)"), ps[:, B_LG, 0:TILES * E]).then_inc(lg_ready, 1)

            ln_in(0)
            dve.wait_ge(ld_w, 16 * N_WLOAD)
            for hf in range(H):
                for k in range(TAPS):
                    dve.tensor_scalar(nat[:, hf * TAPS + k, :], win_n[:, hf, :], conv_c[:, hf, k:k + 1], 0.5,
                                      ALU.mult, ALU.mult)
            dve.tensor_scalar(nat[:, 8:10, :], win_n[:, 2:4, :], 0.5, None, ALU.mult).then_inc(taps_ready, 1)
            norm_x(0)
            dve.wait_ge(wtr_done, 3)
            dve.tensor_scalar(wT[:, 0:8, :].rearrange("p (k c) m -> p k (c m)", k=2), ps[:, 0:2, :], nw[:, 0:1], None, ALU.mult)
            dve.tensor_scalar(wT[:, 8:10, :], ps[:, 2, 0:2 * P].rearrange("p (k c) -> p k c", c=P), nw[:, 0:1], None, ALU.mult)
            dve.tensor_copy(wT[:, 10:12, :], ps[:, 2, 2 * P:4 * P].rearrange("p (k c) -> p k c", c=P)).then_inc(w_ready, 1)
            dve.wait_ge(rs_s, 1)
            dve.tensor_scalar(rs[:], rs[:], 0.25, 0.25, ALU.mult, ALU.add).then_inc(rs_s, 1)
            ln_in(1)
            make_xc(0)
            cap_e(0)
            split_c(0)
            take_c(0)
            norm_x(1)
            for hf in range(H):
                make_gate(0, hf)
            dve.wait_ge(st_pad, 32)
            dve.wait_ge(pre_done, 2)
            dve.tensor_copy(rows(h, 2)[:, :, 1], sqb[:]).then_inc(pre_done, 1)
            dve.wait_ge(pre_done, 3)
            h_first = rows(h, 2)[:, :, 1]
            dve.tensor_tensor(sqb[:], h_first, h_first, ALU.mult).then_inc(sq_done, 1)
            sum_squares(0)
            take_norm(0)
            factor(0)
            restart(0, h_first, 0, 0)

            def iteration(w, prep, ln, out_, nseg, cap_at=1):
                def early(s):
                    if s == 3 and isinstance(w, int) and w == 0:
                        norm_x(2)
                    if s == 1 and ln:
                        ln_in(w + 2)
                    if s == 4 and prep:
                        make_gate(w + 1, 1)
                    if s == 5:
                        take_c(w + 1)

                def late(s):
                    if s == 0:
                        if out_ == 2:
                            evac_lg(w - 2)
                        if prep:
                            make_xc(w + 1)
                    if s == cap_at and prep:
                        cap_e(w + 1)
                    if s == 1 and out_:
                        add_out(w - 1)
                    if s == 2 and out_:
                        out_stats(w - 1)
                    if s == 3 and prep:
                        make_gate(w + 1, 0)
                    if s == 4 and prep:
                        split_c(w + 1)

                for s in range(nseg):
                    segment(w, s, (not prep) and s == nseg - 1, lambda s=s: early(s), lambda s=s: late(s))

            iteration(0, True, 1, 0, SPW, cap_at=2)
            iteration(1, True, 1, 1, SPW)
            iteration(2, True, 1, 2, SPW)
            with dve.Fori(3, NWIN - 2) as w:
                iteration(w, True, 1, 2, SPW)
            iteration(NWIN - 2, True, 0, 2, SPW)
            iteration(NWIN - 1, False, 0, 2, LAST_SEGS)
            gate_y(NWIN - 1, LAST_SEGS - 1)
            evac_lg(NWIN - 2)
            add_out(NWIN - 1)
            out_stats(NWIN - 1)
            evac_lg(NWIN - 1)
            dve_tail(dve)

        @block.tensor
        def _(pe):
            pe.wait_ge(const_pool, 3)
            pe.wait_ge(taps_ready, 1)
            pe.wait_ge(ld_w, 16 * N_WLOAD)
            pe.wait_ge(ld_bc, 64)
            for g in range(5):
                for k in range(4 * g, min(4 * g + 4, 18)):
                    ins = pe.transpose(ps[:, g, (k % 4) * P:(k % 4 + 1) * P], nat[:, k, :], ident[:])
                ins.then_inc(wtr_done, 1)

            def turn_x(v):
                pe.wait_ge(xn_ready, v + 1)
                at_least(pe, bc_read, 2 * v)
                at_least(pe, bsb_ready, v)
                if isinstance(v, int) and v == 1:
                    pe.wait_ge(b0_ready, 1)
                for i in range(TILES):
                    ins = pe.transpose(ps[:, B_XT, i * P:(i + 1) * P], xt[:, i, :], ident[:])
                ins.then_inc(xT_done, 1)

            def project_x(v, hf, k0=0, k1=TAPS):
                if k0 == 0:
                    if hf == 0:
                        pe.wait_ge(xnT_ready, v + 1)
                    at_least(pe, sg_made, 2 * (v - 1) + hf + 1)
                for k in range(k0, k1):
                    ins = pe.matmul(bankc(B_XH[hf]), wT[:, hf * TAPS + k, :], xnT[:, :, k:k + COLS],
                                    start=(k == 0), stop=(k == TAPS - 1))
                if k1 == TAPS:
                    ins.then_inc(xh_done, 1)

            def project_gate(v, hf):
                pe.wait_ge(dt_read, 2 * v + hf + 1)
                pe.matmul(bankc(B_G[hf]), wT[:, 8 + hf, :], xnT[:, :, 3:GRID],
                          start=True, stop=True).then_inc(g_done, 1)

            def project_dt(v, hf):
                pe.wait_ge(xc_ready, v + 1)
                for ih in range(H):
                    ins = pe.matmul(bankc(B_DT[hf]), wT[:, 10 + hf * H + ih, :], xc[:, ih, :],
                                    start=(ih == 0), stop=(ih == H - 1))
                ins.then_inc(dt_done, 1)

            def project_bc(v):
                at_least(pe, x1_done, v - 1)
                for ih in range(H):
                    ins = pe.matmul(bankc(B_BC), wT[:, 14 + ih, :], xc[:, ih, :], start=(ih == 0), stop=(ih == H - 1))
                ins.then_inc(bc_done, 1)

            def project_out(o):
                pe.wait_ge(yg_done, NSEG if last_window(o) else SPW * (o + 1))
                if not last_window(o):
                    at_least(pe, lg_ready, o)
                if isinstance(o, int) and o == 0:
                    pe.wait_ge(xnT_ready, 3)
                for i in range(TILES):
                    for hf in range(H):
                        ins = pe.matmul(ps[:, out_bank(o), i * P:(i + 1) * P],
                                        yg[:, hf].rearrange("p b t -> p (b t)")[:, i * P:(i + 1) * P],
                                        wT[:, 16 + hf, :], start=(hf == 0), stop=(hf == H - 1))
                ins.then_inc(op_done, 1)

            def last_window(o):
                return isinstance(o, int) and o == NWIN - 1

            def turn_h2(o, used):
                pe.wait_ge(h2_ready, o + 1)
                if used is not None:
                    pe.wait_ge(*used)
                for i in range(TILES):
                    ins = pe.transpose(ps[:, B_H2, i * P:(i + 1) * P], h2b[:, i, :], ident[:])
                ins.then_inc(h2T_done, 1)

            def route(o):
                pe.wait_ge(h2T_ready, o + 1)
                for i in range(TILES):
                    ins = pe.matmul(ps[:, B_LG, i * E:(i + 1) * E], h2T[:, i, :], wg_s[:], start=True, stop=True)
                ins.then_inc(lg_done, 1)

            def norm_sum(k):
                pe.wait_ge(red_done, k + 1)
                at_least(pe, h0_ready, k)
                pe.matmul(ps[0:B, NB, 0:1], s_p[:], bound_w[:], start=True, stop=True).then_inc(nrm_done, 1)

            def norm_spread(k):
                pe.wait_ge(fac_made, k + 1)
                pe.matmul(ps[:, NB, 0:B], ones_r[:], fac_d[:], start=True, stop=True).then_inc(fac_done, 1)

            def spread_c(w, s, j):
                S = SPW * w + s
                at_least(pe, cm_done, 3 * (S - 1) + j + 1)
                pe.wait_ge(cs_step, 4 * (w + 1))
                n0, n1 = NCH[j]
                for n in range(n0, n1):
                    ins = pe.matmul(ps[:, j, (n - n0) * BS:(n - n0 + 1) * BS], sel[:, n, :],
                                    cs[:].rearrange("p (b c) -> p b c", b=B)[:, :, SEG * s:SEG * (s + 1)],
                                    start=True, stop=True)
                ins.then_inc(cb_done, 1)

            def sum_states(w, s, j):
                S = SPW * w + s
                pe.wait_ge(cm_done, 3 * S + j + 1)
                if j == 0:
                    at_least(pe, yg_done, S)
                hr = rows(h, s % RING).rearrange("p (f r) t -> p f r t", f=H)
                n0, n1 = NCH[j]
                for n in range(n0, n1):
                    pe.matmul(ps[:, YB, 0:H * BS], ident[:], hr[:, :, n * B:(n + 1) * B, 0:SEG],
                              start=(n == 0), stop=False)

            def add_dx(w, s):
                pe.wait_ge(dxc_ready, 2 * (w + 1))
                pe.matmul(ps[:, YB, 0:H * BS], ident[:],
                          dxc[:].rearrange("p h (b c) -> p (h b) c", c=COLS)[:, :, SEG * s:SEG * (s + 1)],
                          start=False, stop=True).then_inc(y_done, 1)

            turn_x(0)
            pe.wait_ge(w_ready, 2)
            pe.wait_ge(const_dve, 6)
            pe.wait_ge(asc_s, 4)
            for hf in range(H):
                project_x(0, hf)
            for hf in range(H):
                project_dt(0, hf)
            project_bc(0)
            for hf in range(H):
                project_gate(0, hf)
            pe.wait_ge(const_pool, 6)
            for j in range(3):
                spread_c(0, 0, j)
            turn_x(1)
            norm_sum(0)
            norm_spread(0)
            for hf in range(H):
                project_x(1, hf)

            def iteration(w, prep, ln, out_, nseg):
                def before(s):
                    if s == 1 and prep:
                        project_dt(w + 1, 1)
                    if s == 2 and prep:
                        project_gate(w + 1, 0)
                    if s == 3 and prep:
                        project_gate(w + 1, 1)
                    if s == 3 and not prep:
                        turn_h2(w - 1, (x1_done, w))
                    if s == 4:
                        if ln:
                            project_x(w + 2, 0, 2, 3)
                        if out_:
                            turn_h2(w - 1, (xnT_ready, w + 3) if ln else (bc_read, 2 * (w + 2)))
                    if s == 5 and out_:
                        route(w - 1)

                def after(s):
                    if s == 0:
                        if out_:
                            project_out(w - 1)
                        if prep:
                            project_dt(w + 1, 0)
                    if s == 1 and prep:
                        project_bc(w + 1)
                    if ln:
                        if s == 3:
                            project_x(w + 2, 0, 0, 2)
                        if s == 4:
                            project_x(w + 2, 0, 3, 4)
                            project_x(w + 2, 1, 0, 2)
                        if s == 5:
                            project_x(w + 2, 1, 2, 4)
                    if s == 3 and not prep:
                        route(w - 1)

                for s in range(nseg):
                    S = SPW * w + s
                    last = (not prep) and s == nseg - 1
                    if not last:
                        norm_sum(S + 1)
                    before(s)
                    for j in range(3):
                        if s + 1 < nseg:
                            spread_c(w, s + 1, j)
                        elif prep:
                            spread_c(w + 1, 0, j)
                        sum_states(w, s, j)
                        if j == 0 and not last:
                            norm_spread(S + 1)
                        if j == 0 and s == 3 and ln:
                            turn_x(w + 2)
                    add_dx(w, s)
                    after(s)

            iteration(0, True, 1, 0, SPW)
            iteration(1, True, 1, 1, SPW)
            with pe.Fori(2, NWIN - 2) as w:
                iteration(w, True, 1, 1, SPW)
            iteration(NWIN - 2, True, 0, 1, SPW)
            iteration(NWIN - 1, False, 0, 1, LAST_SEGS)
            project_out(NWIN - 1)
            turn_h2(NWIN - 1, (lg_ready, NWIN - 1))
            route(NWIN - 1)
            pe_tail(pe)


_INS = ['L0_attn_x', 'L0_attn_norm_w', 'L0_attn_W_in', 'L0_attn_conv_w', 'L0_attn_conv_b', 'L0_attn_W_dt',
        'L0_attn_b_dt', 'L0_attn_W_B', 'L0_attn_W_C', 'L0_attn_A_log', 'L0_attn_D_param', 'L0_attn_W_out',
        'L0_attn_residual_scale', 'L0_ffn_Wg', 'L0_ffn_w1', 'L0_ffn_w2']


def kernel(**inputs):
    import numpy as _np
    import concourse.bacc as _bacc
    from concourse import mybir as _mybir
    from concourse.bass_utils import run_bass_kernel_spmd as _run

    nc = _bacc.Bacc("TRN2", target_bir_lowering=False, num_devices=1)
    arrays, args = {}, []
    for name in _INS:
        a = _np.ascontiguousarray(inputs[name])
        if a.ndim == 0:
            a = a.reshape(1)
        arrays[f"in_{name}_dram"] = a
        args.append(nc.dram_tensor(f"in_{name}_dram", a.shape, _mybir.dt.from_np(a.dtype), kind="ExternalInput").ap())
    shape = inputs['L0_attn_x'].shape
    args.append(nc.dram_tensor("out_0_dram", shape, _mybir.dt.float32, kind="ExternalOutput").ap())
    mamba_moe(nc, *args)
    r = _run(nc, [arrays], core_ids=[0])
    return r.results[0]["out_0_dram"]
```
